# Optimizing a Trainium2 kernel written in Bass

```python
import numpy as np
import jax
import jax.numpy as jnp

def _softmax(x, axis=-1):
    return jax.nn.softmax(x, axis=axis)

def _gelu(x):
    return jax.nn.gelu(x, approximate=True)

def _silu(x):
    return jax.nn.silu(x)

def _sigmoid(x):
    return jax.nn.sigmoid(x)

def _layernorm(x, axis=-1, eps=1e-05):
    m = jnp.mean(x, axis=axis, keepdims=True)
    v = jnp.var(x, axis=axis, keepdims=True)
    return (x - m) / jnp.sqrt(v + eps)

def _scatter_add(tgt, idx, src, axis=0):
    return tgt.at[idx].add(src)

def _segment_sum(src, seg, n):
    return jax.ops.segment_sum(src, seg, n)
kernel_name = 'mk_adaln_d2_jaxref_r4_bd8e20'

def setup_inputs(seed: int=0):
    np.random.seed(seed)
    _w = jnp.asarray

    def _L0_attn_setup():
        import jax, jax.numpy as jnp
        import numpy as np
        B, L, D, H = (8, 512, 256, 16)
        HD = D // H
        K = 4
        EPS = 1e-06

        def _short_conv(x, w, b):
            xp = jnp.pad(x, ((0, 0), (K - 1, 0), (0, 0)))
            y = b
            for i in range(K):
                y = y + w[:, i] * xp[:, i:i + x.shape[1], :]
            return y

        def _delta_rule(q, k, v, beta):
            qT = jnp.moveaxis(q, 1, 0)
            kT = jnp.moveaxis(k, 1, 0)
            vT = jnp.moveaxis(v, 1, 0)
            bT = jnp.moveaxis(beta, 1, 0)

            def step(S, inp):
                q_t, k_t, v_t, b_t = inp
                pred = jnp.einsum('bhk,bhkv->bhv', k_t, S)
                S = S + b_t[..., None, None] * (k_t[..., None] * (v_t - pred)[..., None, :])
                o_t = jnp.einsum('bhk,bhkv->bhv', q_t, S)
                return (S, o_t)
            S0 = jnp.zeros((q.shape[0], H, HD, HD), q.dtype)
            _, o = jax.lax.scan(step, S0, (qT, kT, vT, bT))
            return jnp.moveaxis(o, 0, 1)

        def _rmsnorm(x, w):
            return x * jax.lax.rsqrt(jnp.mean(x * x, axis=-1, keepdims=True) + EPS) * w
        key = jax.random.key(seed)
        ks = jax.random.split(key, 12)
        s = 0.02
        inp = {'x': jax.random.normal(ks[0], (B, L, D), jnp.float32), 'Wq': jax.random.normal(ks[1], (D, D), jnp.float32) * s, 'bq': jnp.zeros((D,), jnp.float32), 'Wk': jax.random.normal(ks[2], (D, D), jnp.float32) * s, 'bk': jnp.zeros((D,), jnp.float32), 'Wv': jax.random.normal(ks[3], (D, D), jnp.float32) * s, 'bv': jnp.zeros((D,), jnp.float32), 'Wbeta': jax.random.normal(ks[4], (H, D), jnp.float32) * s, 'bbeta': jnp.zeros((H,), jnp.float32), 'Wo': jax.random.normal(ks[5], (D, D), jnp.float32) * s, 'bo': jnp.zeros((D,), jnp.float32), 'wq_conv': jax.random.normal(ks[6], (D, K), jnp.float32) * 0.2, 'bq_conv': jnp.zeros((D,), jnp.float32), 'wk_conv': jax.random.normal(ks[7], (D, K), jnp.float32) * 0.2, 'bk_conv': jnp.zeros((D,), jnp.float32), 'wv_conv': jax.random.normal(ks[8], (D, K), jnp.float32) * 0.2, 'bv_conv': jnp.zeros((D,), jnp.float32), 'norm_w': jnp.ones((HD,), jnp.float32)}
        return inp
    _L0_attn_in = _L0_attn_setup()

    def _L0_ffn_setup():
        import jax, jax.numpy as jnp
        import numpy as np
        HIDDEN = 256
        N_ROUTED = 16
        N_SHARED = 2
        TOP_K = 2
        MID_R = HIDDEN // 4
        MID_S = HIDDEN // 2
        key = jax.random.key(seed)
        ks = jax.random.split(key, 8)
        s = 0.02
        return {'x': jax.random.normal(ks[0], (2, 256, HIDDEN), dtype=jnp.float32), 'router_w': jax.random.normal(ks[1], (HIDDEN, N_ROUTED), dtype=jnp.float32) * s, 'wg_r': jax.random.normal(ks[2], (N_ROUTED, HIDDEN, MID_R), dtype=jnp.float32) * s, 'wu_r': jax.random.normal(ks[3], (N_ROUTED, HIDDEN, MID_R), dtype=jnp.float32) * s, 'wd_r': jax.random.normal(ks[4], (N_ROUTED, MID_R, HIDDEN), dtype=jnp.float32) * s, 'wg_s': jax.random.normal(ks[5], (N_SHARED, HIDDEN, MID_S), dtype=jnp.float32) * s, 'wu_s': jax.random.normal(ks[6], (N_SHARED, HIDDEN, MID_S), dtype=jnp.float32) * s, 'wd_s': jax.random.normal(ks[7], (N_SHARED, MID_S, HIDDEN), dtype=jnp.float32) * s}
    _L0_ffn_in = _L0_ffn_setup()
    _L0_c = _w((lambda *s: np.random.randn(*s).astype(np.float32) * 0.05)(4, 256))
    _L0_wmod = _w((lambda *s: np.random.randn(*s).astype(np.float32) * 0.05)(256, 6 * 256) * 256 ** (-0.5))

    def _L1_attn_setup():
        import jax, jax.numpy as jnp
        import numpy as np
        B, L, DIM, H, D = (4, 256, 256, 8, 32)
        key = jax.random.key(seed)
        ks = jax.random.split(key, 8)
        s = 0.02
        return dict(x=jax.random.normal(ks[0], (B, L, DIM), jnp.float32), W_in=jax.random.normal(ks[1], (DIM, DIM), jnp.float32) * s, b_in=jnp.zeros((DIM,), jnp.float32), W_qkva=jax.random.normal(ks[2], (H * D * 8, DIM), jnp.float32) * s, b_qkva=jnp.zeros((H * D * 8,), jnp.float32), W_y=jax.random.normal(ks[3], (DIM, H * D * 2), jnp.float32) * s, b_y=jnp.zeros((DIM,), jnp.float32), W_out=jax.random.normal(ks[4], (DIM, DIM), jnp.float32) * s, b_out=jnp.zeros((DIM,), jnp.float32), h0_re=jax.random.normal(ks[5], (H, D, D), jnp.float32), h0_im=jax.random.normal(ks[6], (H, D, D), jnp.float32))
    _L1_attn_in = _L1_attn_setup()

    def _L1_ffn_setup():
        import jax, jax.numpy as jnp
        import numpy as np
        from jax import lax
        LOKAL_GRUP = 7
        TOP_K = 2
        EPS = 1e-08
        CACHE_BONUS = 0.1

        def _route(tokens, uzman_embeddings, onbellek_durumu):
            sim = tokens @ uzman_embeddings.T
            _, local_idx = lax.top_k(sim, LOKAL_GRUP)
            t_norm = tokens / (jnp.linalg.norm(tokens, axis=-1, keepdims=True) + EPS)
            e_norm = uzman_embeddings / (jnp.linalg.norm(uzman_embeddings, axis=-1, keepdims=True) + EPS)
            local_embs = e_norm[local_idx]
            scores = jnp.einsum('nld,nd->nl', local_embs, t_norm)
            scores = scores + CACHE_BONUS * onbellek_durumu[local_idx]
            top_scores, top_local = lax.top_k(scores, TOP_K)
            global_idx = jnp.take_along_axis(local_idx, top_local, axis=1)
            weights = jax.nn.softmax(top_scores, axis=-1)
            return (global_idx, lax.stop_gradient(weights))
        key = jax.random.key(seed)
        ks = jax.random.split(key, 6)
        B, S, D, E, H = (2, 512, 256, 8, 1024)
        return {'x': jax.random.normal(ks[0], (B, S, D), jnp.float32), 'uzman_embeddings': jax.random.normal(ks[1], (E, D), jnp.float32) * 0.01, 'W1': jax.random.normal(ks[2], (E, D, H), jnp.float32) * 0.02, 'b1': jax.random.normal(ks[3], (E, H), jnp.float32) * 0.02, 'W2': jax.random.normal(ks[4], (E, H, D), jnp.float32) * 0.02, 'b2': jax.random.normal(ks[5], (E, D), jnp.float32) * 0.02, 'onbellek_durumu': jnp.ones((E,), jnp.float32)}
    _L1_ffn_in = _L1_ffn_setup()
    _L1_c = _w((lambda *s: np.random.randn(*s).astype(np.float32) * 0.05)(4, 256))
    _L1_wmod = _w((lambda *s: np.random.randn(*s).astype(np.float32) * 0.05)(256, 6 * 256) * 256 ** (-0.5))
    _d = {'L0_attn_x': _L0_attn_in['x'], 'L0_attn_Wq': _L0_attn_in['Wq'], 'L0_attn_bq': _L0_attn_in['bq'], 'L0_attn_Wk': _L0_attn_in['Wk'], 'L0_attn_bk': _L0_attn_in['bk'], 'L0_attn_Wv': _L0_attn_in['Wv'], 'L0_attn_bv': _L0_attn_in['bv'], 'L0_attn_Wbeta': _L0_attn_in['Wbeta'], 'L0_attn_bbeta': _L0_attn_in['bbeta'], 'L0_attn_Wo': _L0_attn_in['Wo'], 'L0_attn_bo': _L0_attn_in['bo'], 'L0_attn_wq_conv': _L0_attn_in['wq_conv'], 'L0_attn_bq_conv': _L0_attn_in['bq_conv'], 'L0_attn_wk_conv': _L0_attn_in['wk_conv'], 'L0_attn_bk_conv': _L0_attn_in['bk_conv'], 'L0_attn_wv_conv': _L0_attn_in['wv_conv'], 'L0_attn_bv_conv': _L0_attn_in['bv_conv'], 'L0_attn_norm_w': _L0_attn_in['norm_w'], 'L0_ffn_router_w': _L0_ffn_in['router_w'], 'L0_ffn_wg_r': _L0_ffn_in['wg_r'], 'L0_ffn_wu_r': _L0_ffn_in['wu_r'], 'L0_ffn_wd_r': _L0_ffn_in['wd_r'], 'L0_ffn_wg_s': _L0_ffn_in['wg_s'], 'L0_ffn_wu_s': _L0_ffn_in['wu_s'], 'L0_ffn_wd_s': _L0_ffn_in['wd_s'], 'L0_c': _L0_c, 'L0_wmod': _L0_wmod, 'L1_attn_W_in': _L1_attn_in['W_in'], 'L1_attn_b_in': _L1_attn_in['b_in'], 'L1_attn_W_qkva': _L1_attn_in['W_qkva'], 'L1_attn_b_qkva': _L1_attn_in['b_qkva'], 'L1_attn_W_y': _L1_attn_in['W_y'], 'L1_attn_b_y': _L1_attn_in['b_y'], 'L1_attn_W_out': _L1_attn_in['W_out'], 'L1_attn_b_out': _L1_attn_in['b_out'], 'L1_attn_h0_re': _L1_attn_in['h0_re'], 'L1_attn_h0_im': _L1_attn_in['h0_im'], 'L1_ffn_uzman_embeddings': _L1_ffn_in['uzman_embeddings'], 'L1_ffn_W1': _L1_ffn_in['W1'], 'L1_ffn_b1': _L1_ffn_in['b1'], 'L1_ffn_W2': _L1_ffn_in['W2'], 'L1_ffn_b2': _L1_ffn_in['b2'], 'L1_ffn_onbellek_durumu': _L1_ffn_in['onbellek_durumu'], 'L1_c': _L1_c, 'L1_wmod': _L1_wmod}
    _x0 = _d['L0_attn_x']
    _d['L0_attn_x'] = jax.random.normal(jax.random.fold_in(jax.random.key(seed), 1), (4, 1024, 256), dtype=_x0.dtype)
    del _x0
    return _d

def reference(L0_attn_x, L0_attn_Wq, L0_attn_bq, L0_attn_Wk, L0_attn_bk, L0_attn_Wv, L0_attn_bv, L0_attn_Wbeta, L0_attn_bbeta, L0_attn_Wo, L0_attn_bo, L0_attn_wq_conv, L0_attn_bq_conv, L0_attn_wk_conv, L0_attn_bk_conv, L0_attn_wv_conv, L0_attn_bv_conv, L0_attn_norm_w, L0_ffn_router_w, L0_ffn_wg_r, L0_ffn_wu_r, L0_ffn_wd_r, L0_ffn_wg_s, L0_ffn_wu_s, L0_ffn_wd_s, L0_c, L0_wmod, L1_attn_W_in, L1_attn_b_in, L1_attn_W_qkva, L1_attn_b_qkva, L1_attn_W_y, L1_attn_b_y, L1_attn_W_out, L1_attn_b_out, L1_attn_h0_re, L1_attn_h0_im, L1_ffn_uzman_embeddings, L1_ffn_W1, L1_ffn_b1, L1_ffn_W2, L1_ffn_b2, L1_ffn_onbellek_durumu, L1_c, L1_wmod):

    def _L0_attn_ref(x, Wq, bq, Wk, bk, Wv, bv, Wbeta, bbeta, Wo, bo, wq_conv, bq_conv, wk_conv, bk_conv, wv_conv, bv_conv, norm_w):
        import jax, jax.numpy as jnp
        import numpy as np
        B, L, D, H = (8, 512, 256, 16)
        HD = D // H
        K = 4
        EPS = 1e-06

        def _short_conv(x, w, b):
            xp = jnp.pad(x, ((0, 0), (K - 1, 0), (0, 0)))
            y = b
            for i in range(K):
                y = y + w[:, i] * xp[:, i:i + x.shape[1], :]
            return y

        def _delta_rule(q, k, v, beta):
            qT = jnp.moveaxis(q, 1, 0)
            kT = jnp.moveaxis(k, 1, 0)
            vT = jnp.moveaxis(v, 1, 0)
            bT = jnp.moveaxis(beta, 1, 0)

            def step(S, inp):
                q_t, k_t, v_t, b_t = inp
                pred = jnp.einsum('bhk,bhkv->bhv', k_t, S)
                S = S + b_t[..., None, None] * (k_t[..., None] * (v_t - pred)[..., None, :])
                o_t = jnp.einsum('bhk,bhkv->bhv', q_t, S)
                return (S, o_t)
            S0 = jnp.zeros((q.shape[0], H, HD, HD), q.dtype)
            _, o = jax.lax.scan(step, S0, (qT, kT, vT, bT))
            return jnp.moveaxis(o, 0, 1)

        def _rmsnorm(x, w):
            return x * jax.lax.rsqrt(jnp.mean(x * x, axis=-1, keepdims=True) + EPS) * w
        Bx, Lx, Dx = x.shape
        k = _short_conv(x @ Wk.T + bk, wk_conv, bk_conv)
        q = _short_conv(x @ Wq.T + bq, wq_conv, bq_conv)
        v = _short_conv(x @ Wv.T + bv, wv_conv, bv_conv)
        beta = jax.nn.sigmoid(x @ Wbeta.T + bbeta)
        k = k.reshape(Bx, Lx, H, HD)
        q = q.reshape(Bx, Lx, H, HD)
        v = v.reshape(Bx, Lx, H, HD)
        v = jax.nn.silu(v)
        knorm = jnp.linalg.norm(k, axis=-1, keepdims=True)
        qnorm = jnp.linalg.norm(q, axis=-1, keepdims=True)
        k = k / (knorm + EPS)
        v = v / (knorm + EPS)
        q = q / (qnorm + EPS)
        o = _delta_rule(q, k, v, beta)
        o = _rmsnorm(o, norm_w)
        o = o.reshape(Bx, Lx, Dx)
        return o @ Wo.T + bo

    def _L0_ffn_ref(x, router_w, wg_r, wu_r, wd_r, wg_s, wu_s, wd_s):
        import jax, jax.numpy as jnp
        import numpy as np
        HIDDEN = 256
        N_ROUTED = 16
        N_SHARED = 2
        TOP_K = 2
        MID_R = HIDDEN // 4
        MID_S = HIDDEN // 2
        orig_shape = x.shape
        flat = x.reshape(-1, orig_shape[-1])
        gs = jnp.einsum('td,ndm->tnm', flat, wg_s)
        us = jnp.einsum('td,ndm->tnm', flat, wu_s)
        out = jnp.einsum('tnm,nmd->td', jax.nn.silu(gs) * us, wd_s)
        logits = (flat @ router_w).astype(jnp.float32)
        probs = jax.nn.softmax(logits, axis=-1)
        weights, indices = jax.lax.top_k(probs, TOP_K)
        weights = weights / (weights.sum(axis=-1, keepdims=True) + 1e-09)
        weights = weights.astype(x.dtype)
        comb = jnp.sum(jax.nn.one_hot(indices, N_ROUTED, dtype=x.dtype) * weights[..., None], axis=1)
        g = jnp.einsum('td,edm->tem', flat, wg_r)
        u = jnp.einsum('td,edm->tem', flat, wu_r)
        h = jax.nn.silu(g) * u
        h = h * comb[:, :, None]
        out = out + jnp.einsum('tem,emd->td', h, wd_r)
        return out.reshape(orig_shape)

    def _L1_attn_ref(x, W_in, b_in, W_qkva, b_qkva, W_y, b_y, W_out, b_out, h0_re, h0_im):
        import jax, jax.numpy as jnp
        import numpy as np
        B, L, DIM, H, D = (4, 256, 256, 8, 32)
        b, Ls, dim = x.shape
        Hh, Dd = (h0_re.shape[0], h0_re.shape[1])
        u = jax.nn.silu(x @ W_in.T + b_in)
        qkva = (u @ W_qkva.T + b_qkva).reshape(b, Ls, Hh, Dd, 4, 2)
        c = jax.lax.complex(qkva[..., 0], qkva[..., 1])
        q, k, v, a = (c[..., 0], c[..., 1], c[..., 2], c[..., 3])
        mag2 = a.real * a.real + a.imag * a.imag
        a = a * (jax.lax.rsqrt(mag2) * jax.nn.sigmoid(jnp.log(mag2)))
        kv = jnp.einsum('blhd,blhe->blhde', k, v)
        h0 = jax.lax.complex(h0_re, h0_im)[None]
        kv = kv.at[:, 0].add(a[:, 0, ..., None] * h0)
        a_e = a[..., None]

        def comb(c1, c2):
            a1, x1 = c1
            a2, x2 = c2
            return (a1 * a2, a2 * x1 + x2)
        _, h = jax.lax.associative_scan(comb, (a_e, kv), axis=1)
        y = jnp.einsum('blhd,blhde->blhe', q, h)
        y2 = jnp.stack([y.real, y.imag], axis=-1).reshape(b, Ls, Hh * Dd * 2)
        y2 = jax.nn.silu(y2 @ W_y.T + b_y)
        return y2 @ W_out.T + b_out

    def _L1_ffn_ref(x, uzman_embeddings, W1, b1, W2, b2, onbellek_durumu):
        import jax, jax.numpy as jnp
        import numpy as np
        from jax import lax
        LOKAL_GRUP = 7
        TOP_K = 2
        EPS = 1e-08
        CACHE_BONUS = 0.1

        def _route(tokens, uzman_embeddings, onbellek_durumu):
            sim = tokens @ uzman_embeddings.T
            _, local_idx = lax.top_k(sim, LOKAL_GRUP)
            t_norm = tokens / (jnp.linalg.norm(tokens, axis=-1, keepdims=True) + EPS)
            e_norm = uzman_embeddings / (jnp.linalg.norm(uzman_embeddings, axis=-1, keepdims=True) + EPS)
            local_embs = e_norm[local_idx]
            scores = jnp.einsum('nld,nd->nl', local_embs, t_norm)
            scores = scores + CACHE_BONUS * onbellek_durumu[local_idx]
            top_scores, top_local = lax.top_k(scores, TOP_K)
            global_idx = jnp.take_along_axis(local_idx, top_local, axis=1)
            weights = jax.nn.softmax(top_scores, axis=-1)
            return (global_idx, lax.stop_gradient(weights))
        B, S, D = x.shape
        tokens = x.reshape(-1, D)
        global_idx, weights = _route(tokens, uzman_embeddings, onbellek_durumu)
        h = jnp.einsum('nd,edh->enh', tokens, W1) + b1[:, None, :]
        h = jax.nn.gelu(h, approximate=False)
        out_all = jnp.einsum('enh,ehd->end', h, W2) + b2[:, None, :]
        N = tokens.shape[0]
        out_sel = out_all[global_idx, jnp.arange(N)[:, None]]
        out = jnp.sum(weights[..., None] * out_sel, axis=1)
        return out.reshape(B, S, D)
    x = L0_attn_x
    mod = (_silu(L0_c) @ L0_wmod).reshape(L0_c.shape[0], 6, 1, -1)
    sa, ca, ga, sb, cb, gb = (mod[:, 0], mod[:, 1], mod[:, 2], mod[:, 3], mod[:, 4], mod[:, 5])
    ga = (2 * (ga >= 0) - 1) * jnp.maximum(jnp.abs(ga), 0.25)
    gb = (2 * (gb >= 0) - 1) * jnp.maximum(jnp.abs(gb), 0.25)
    h = _layernorm(x, axis=-1) * (1 + ca) + sa
    x = x + ga * _L0_attn_ref(h, L0_attn_Wq, L0_attn_bq, L0_attn_Wk, L0_attn_bk, L0_attn_Wv, L0_attn_bv, L0_attn_Wbeta, L0_attn_bbeta, L0_attn_Wo, L0_attn_bo, L0_attn_wq_conv, L0_attn_bq_conv, L0_attn_wk_conv, L0_attn_bk_conv, L0_attn_wv_conv, L0_attn_bv_conv, L0_attn_norm_w)
    h = _layernorm(x, axis=-1) * (1 + cb) + sb
    x = x + gb * _L0_ffn_ref(h, L0_ffn_router_w, L0_ffn_wg_r, L0_ffn_wu_r, L0_ffn_wd_r, L0_ffn_wg_s, L0_ffn_wu_s, L0_ffn_wd_s)
    mod = (_silu(L1_c) @ L1_wmod).reshape(L1_c.shape[0], 6, 1, -1)
    sa, ca, ga, sb, cb, gb = (mod[:, 0], mod[:, 1], mod[:, 2], mod[:, 3], mod[:, 4], mod[:, 5])
    ga = (2 * (ga >= 0) - 1) * jnp.maximum(jnp.abs(ga), 0.25)
    gb = (2 * (gb >= 0) - 1) * jnp.maximum(jnp.abs(gb), 0.25)
    h = _layernorm(x, axis=-1) * (1 + ca) + sa
    x = x + ga * _L1_attn_ref(h, L1_attn_W_in, L1_attn_b_in, L1_attn_W_qkva, L1_attn_b_qkva, L1_attn_W_y, L1_attn_b_y, L1_attn_W_out, L1_attn_b_out, L1_attn_h0_re, L1_attn_h0_im)
    h = _layernorm(x, axis=-1) * (1 + cb) + sb
    x = x + gb * _L1_ffn_ref(h, L1_ffn_uzman_embeddings, L1_ffn_W1, L1_ffn_b1, L1_ffn_W2, L1_ffn_b2, L1_ffn_onbellek_durumu)
    return x

_drawn_inputs = setup_inputs


def setup_inputs(seed=0):
    import zlib

    import numpy as np

    out = dict(_drawn_inputs(seed))
    spreads = {'L0_attn_bq': (0.0, 0.1),
     'L0_attn_bk': (0.0, 0.1),
     'L0_attn_bv': (0.0, 0.1),
     'L0_attn_bbeta': (0.0, 0.1),
     'L0_attn_bo': (0.0, 0.1),
     'L0_attn_bq_conv': (0.0, 0.1),
     'L0_attn_bk_conv': (0.0, 0.1),
     'L0_attn_bv_conv': (0.0, 0.1),
     'L0_attn_norm_w': (1.0, 0.2),
     'L1_attn_b_in': (0.0, 0.1),
     'L1_attn_b_qkva': (0.0, 0.1),
     'L1_attn_b_y': (0.0, 0.1),
     'L1_attn_b_out': (0.0, 0.1),
     'L1_ffn_onbellek_durumu': (1.0, 0.2)}
    factors = {}
    for name, (base, spread) in spreads.items():
        noise = np.random.default_rng([zlib.crc32(name.encode()), seed]).standard_normal(out[name].shape)
        drawn = base * np.exp(spread * noise) if base else spread * noise
        out[name] = jnp.asarray(drawn.astype(out[name].dtype))
    for name, factor in factors.items():
        out[name] = (out[name] * factor).astype(out[name].dtype)
    return out
```

```python
from contextlib import ExitStack

import numpy as np

import concourse.bass as bass
from concourse import mybir

F32 = mybir.dt.float32
I32 = mybir.dt.int32
ALU = mybir.AluOpType
ACT = mybir.ActivationFunctionType
AX = mybir.AxisListType

P = 128
B, L, D = 4, 1024, 256
KC = D // P
SEG = 128
NSEG = L // SEG
NT = B * SEG
H0, HD0, TAPS = 16, 16, 4
PAST = TAPS - 1
EV = HD0 // 2
E0, MID0, SHARED0 = 16, 64, 256
TILES0 = (E0 * MID0 + SHARED0) // P
ROUTED0 = E0 * MID0 // P
GROUPS0 = [(0, 3), (3, 6), (6, 8), (8, 10)]
H1, HD1 = 8, 32
HG = 2
HP = 4
LEVELS = 7
E1, MID1 = 8, 1024
HT1 = MID1 // P

SLOT = 2304
SLOTS = 4
LOADS = len(GROUPS0) + 2 * E1
STRIDE = 4096

COLS = {}


def column_layout():
    at = 0
    for name, n in (("bqkv", 6), ("bqkv_conv", 6), ("w_conv", 24), ("norm_w", 1), ("bbeta", 1),
                    ("b_in", 2), ("b_qka", 12), ("b_y", 2), ("b1", E1 * HT1)):
        COLS[name] = (at, n)
        at += n
    return at


NCOLS = column_layout()
CONSTS = {}


def const_layout():
    at = 0
    for name, n in (("ident", P), ("ones16", P), ("ones", P), ("head_of", HP), ("rev16", 16), ("rev8", 8),
                    ("up8", 8), ("masks", LEVELS * 64), ("sel", ROUTED0 * P)):
        CONSTS[name] = (at, n)
        at += n
    return at


NCONST = const_layout()
ROWS = {"bo": (0, D), "b_out": (D, D), "b_v": (2 * D, 512), "cache": (2 * D + 512, E1)}
NROWS = 2 * D + 512 + E1


class Signal:

    def __init__(self, handle, stride):
        self.handle, self.stride, self.count = handle, stride, 0


def build(nc, ins, out):
    with ExitStack() as ctx:
        def sb(name, shape, dt=F32):
            return ctx.enter_context(nc.sbuf_tensor(name, shape, dt))

        w_qkv = sb("w_qkv", [P, KC, 3 * D])
        w_beta = sb("w_beta", [P, KC, H0])
        w_o = sb("w_o", [P, KC, D])
        w_router = sb("w_router", [P, KC, E0])
        w_in = sb("w_in", [P, KC, D])
        w_qka = sb("w_qka", [P, KC, 12, P])
        w_v = sb("w_v", [P, KC, 512])
        w_y = sb("w_y", [P, 4, D])
        w_out = sb("w_out", [P, KC, D])
        w_emb = sb("w_emb", [P, KC, E1])
        b2 = sb("b2", [E1, D])
        cols = sb("cols", [P, NCOLS])
        consts = sb("consts", [P, NCONST])
        rows = sb("rows", [P, NROWS])
        ring = sb("ring", [P, SLOTS, SLOT])
        c_cols = sb("c_cols", [P, 2, KC, B])
        silu_c = sb("silu_c", [P, 2, KC, B])
        shift_scale = sb("shift_scale", [P, 2, 4, KC, B])
        gates = sb("gates", [P, 2, 2, B, D])
        emb_rnorm = sb("emb_rnorm", [P, E1])

        def col(name, i=0):
            return cols[:, COLS[name][0] + i:COLS[name][0] + i + 1]

        def const(name):
            a, n = CONSTS[name]
            return consts[:, a:a + n]

        def row(name):
            a, n = ROWS[name]
            return rows[:, a:a + n]

        ident = const("ident")
        masks = const("masks").bitcast(I32).rearrange("p (l j) -> p l j", l=LEVELS)
        sel = const("sel")[0:E0].rearrange("p (c j) -> p c j", c=ROUTED0)

        X = sb("X", [P, B, D])
        xn = sb("xn", [P, B, D])
        hT = sb("hT", [P, KC, B, SEG])
        ln_stats = sb("ln_stats", [P, B, 6])
        ln_mv = sb("ln_mv", [P, B, 2])
        ln_var = sb("ln_var", [P, B])
        ln_std = sb("ln_std", [P, B])
        ln_rstd = sb("ln_rstd", [P, B])
        past = sb("past", [P, 6, B, PAST])
        S0 = sb("S0", [P, EV, HD0])
        H3 = sb("H3", [P, HG, B, 3, HD1])
        arena = sb("arena", [P, 24096])

        def carve(offset, shape):
            n = int(np.prod(shape[1:]))
            flat = arena[0:shape[0], offset:offset + n]
            assert offset + n <= 24096, (offset, n)
            names = "abcdef"[:len(shape) - 1]
            view = flat if len(shape) == 2 else flat.rearrange(
                f"p ({' '.join(names)}) -> p {' '.join(names)}",
                **{k: v for k, v in zip(names, shape[1:])})
            return view, offset + n

        o = 0
        PX, o = carve(o, [P, KC, B, PAST + SEG])
        kqv, o = carve(o, [P, 3, KC, B, SEG])
        sq, o = carve(o, [P, KC, B, SEG])
        rn, o = carve(o, [P, KC, B, SEG])
        KQ, o = carve(o, [P, 2, HD0, SEG])
        V0, o = carve(o, [P, EV, SEG])
        beta_scan, o = carve(o, [P, SEG])
        nbeta, o = carve(o, [P, SEG])
        KQ_S, o = carve(o, [P, SEG, 2, EV])
        delta, o = carve(o, [P, SEG, EV])
        tmp_dot, o = carve(o, [P, HD0, SEG])
        prod, o = carve(o, [P, 2, EV, HD0])
        outer, o = carve(o, [P, EV, HD0])
        qk_dot, o = carve(o, [P, SEG])
        O0, o = carve(o, [P, EV, SEG])
        betaT, o = carve(o, [H0, B, SEG])
        oT = kqv[:, 0]
        o = 0
        hid0, o = carve(o, [P, TILES0, B, SEG])
        sg0, o = carve(o, [P, 2, B, SEG])
        combT, o = carve(o, [E0, B, SEG])
        lg, o = carve(o, [P, 12, B, E0])
        sm, o = carve(o, [P, 16, B])
        o = 0
        V3, o = carve(o, [P, B, H1, 3, HD1])
        y2T, o = carve(o, [P, 4, B, SEG])
        uT, o = carve(o, [P, KC, B, SEG])
        Q3, o = carve(o, [P, 3, B, SEG])
        K2, o = carve(o, [P, 2, B, SEG])
        TT, o = carve(o, [P, 2, 1024])
        t1, o = carve(o, [P, 2, NT])
        t2, o = carve(o, [P, 2, NT])
        u1, o = carve(o, [P, 2, NT // 2])
        u2, o = carve(o, [P, 2, NT // 2])
        Kx, o = carve(o, [P, 2, HP, B, SEG])
        score, o = carve(o, [P, B, HP, 2, SEG])
        Hx, o = carve(o, [P, B, 2, HP, 2 * HD1])
        diag, o = carve(o, [P, B, HP, 2])
        KT = t2.rearrange("p r (b c) -> p (r b) c", c=2 * P).rearrange("p b (r c) -> p b r c", r=2)
        o = 0
        hid1, o = carve(o, [P, 2, HT1, B, SEG])
        acc, o = carve(o, [P, B, D])
        combT1, o = carve(o, [E1, B, SEG])
        sqh, o = carve(o, [P, KC, B, SEG])
        rt, o = carve(o, [P, 16, B, E1])
        rs, o = carve(o, [P, 24, B])

        bank = [ctx.enter_context(nc.psum_tensor(f"bank{i}", [P, 512], F32)) for i in range(8)]

        signals = []

        def signal(name, stride=STRIDE):
            s = Signal(ctx.enter_context(nc.semaphore(name)), stride)
            signals.append(s)
            return s

        tables_in = signal("tables_in")
        silu_done = signal("silu_done")
        mod_cols = signal("mod_cols")
        mod_rows = signal("mod_rows")
        mod_rows_taken = signal("mod_rows_taken")
        emb_sq = signal("emb_sq")
        emb_sum = signal("emb_sum")
        emb_root = signal("emb_root")
        started = signal("started")
        seg_open = signal("seg_open")
        passed = signal("passed")
        x_in = signal("x_in", 16)
        x_out = signal("x_out", 16)
        ring_in = [signal(f"ring_in{i}", 16 * (LOADS // SLOTS)) for i in range(SLOTS)]
        kq_out = signal("kq_out", 16 * 4)
        k_scan = signal("k_scan", 16 * 8)
        q_scan = signal("q_scan", 16 * 8)
        v_scan = signal("v_scan", 16 * 8)
        beta_in = signal("beta_in", 16 * 8)
        o_out = signal("o_out", 16 * 8)
        o_in = signal("o_in", 16)
        dve_step = signal("dve_step")
        ln_var_ok = signal("ln_var_ok")
        xn_ok = signal("xn_ok")
        px_free = signal("px_free")
        k_sq = signal("k_sq")
        conv_v = signal("conv_v")
        k_unit = signal("k_unit")
        q_unit = signal("q_unit")
        v_unit = signal("v_unit")
        o0_ok = signal("o0_ok")
        o_sq = signal("o_sq")
        o_norm_ok = signal("o_norm_ok")
        logit_sub = signal("logit_sub")
        comb_ok = signal("comb_ok")
        comb_copied = signal("comb_copied")
        hid0_ok = signal("hid0_ok")
        res_taken = signal("res_taken")
        x_done = signal("x_done")
        mag_ok = signal("mag_ok")
        k_neg = signal("k_neg")
        v3_ok = signal("v3_ok")
        a_ok = signal("a_ok")
        pairs_ok = signal("pairs_ok")
        diag_ok = signal("diag_ok")
        q_ready = signal("q_ready")
        masked = signal("masked")
        state_ok = signal("state_ok")
        hsq_ok = signal("hsq_ok")
        rt_var = signal("rt_var")
        rt_gap = signal("rt_gap")
        comb1_ok = signal("comb1_ok")
        comb1_copied = signal("comb1_copied")
        acc_ok = signal("acc_ok")
        x_final = signal("x_final")
        ln_tr = signal("ln_tr")
        proj = signal("proj")
        nrm = signal("nrm")
        res = signal("res")
        router = signal("router")
        comb_tr = signal("comb_tr")
        gate_mm = signal("gate_mm")
        up_mm = signal("up_mm")
        slot_used = signal("slot_used")
        u_mm = signal("u_mm")
        plane_mm = signal("plane_mm")
        v_mm = signal("v_mm")
        diag_mm = signal("diag_mm")
        scored = signal("scored")
        y_mm = signal("y_mm")
        kt_mm = signal("kt_mm")
        r_mm = signal("r_mm")
        y3_mm = signal("y3_mm")
        h1_mm = signal("h1_mm")
        down_mm = signal("down_mm")
        down_bias = signal("down_bias")
        act_step = signal("act_step")
        ln_root = signal("ln_root")
        hT_ok = signal("hT_ok")
        px_ok = signal("px_ok")
        beta_ok = signal("beta_ok")
        root = signal("root")
        v_silu = signal("v_silu")
        exp_ok = signal("exp_ok")
        sg_ok = signal("sg_ok")
        u_ok = signal("u_ok")
        plane_ok = signal("plane_ok")
        mag_root = signal("mag_root")
        hx_ok = signal("hx_ok")
        kx_ready = signal("kx_ready")
        y2_ok = signal("y2_ok")
        kt_ok = signal("kt_ok")
        y3_ok = signal("y3_ok")
        rt_root = signal("rt_root")
        rt_exp = signal("rt_exp")
        hid1_ok = signal("hid1_ok")
        pool_step = signal("pool_step")
        zeroed = signal("zeroed")
        score_init = signal("score_init")
        k_ready = signal("k_ready")

        last = {}

        def up(s, who=None):
            s.count += 1
            if who is not None:
                last[who] = s
            return s.handle, 1

        def up16(s):
            s.count += 16
            return s.handle, 16

        def top_up(eng, mine):
            for s in mine:
                if s.count:
                    assert s.count <= s.stride
                    if s.count < s.stride:
                        eng.sem_inc(s.handle, s.stride - s.count)

        kqv_d = nc.dram_tensor("kqv_d", (3, D, B, SEG), F32, kind="Internal").ap()
        beta_d = nc.dram_tensor("beta_d", (H0, B, SEG), F32, kind="Internal").ap()
        o_d = nc.dram_tensor("o_d", (KC, H0 // KC, 2, EV, B, SEG), F32, kind="Internal").ap()

        x_seg = ins["x"].rearrange("b (s p) d -> s p b d", p=SEG)
        out_seg = out.rearrange("b (s p) d -> s p b d", p=SEG)
        block = ctx.enter_context(nc.Block())

        TABLES = [(w_qkv, "w_qkv"), (w_beta, "w_beta"), (w_o, "w_o"), (w_router, "w_router"), (w_in, "w_in"),
                  (w_qka, "w_qka"), (w_v, "w_v"), (w_y, "w_y"), (w_out, "w_out"), (w_emb, "w_emb"), (b2, "b2"),
                  (cols, "cols"), (consts, "consts"), (c_cols, "c_cols")]
        wmod = [ring[:, 2 * i:2 * i + 2, :].rearrange("p a s -> p (a s)")[:, 0:KC * 1536].rearrange(
            "p (k n) -> p k n", k=KC) for i in range(2)]

        @block.sync
        def _(sp):
            for t, name in TABLES:
                sp.dma_start(t[:], ins[name]).then_inc(tables_in.handle, 16)
            sp.dma_start(rows[:, :], ins["rows"].partition_broadcast(P)).then_inc(tables_in.handle, 16)
            for i in range(2):
                sp.dma_start(wmod[i], ins["wmod"][i]).then_inc(tables_in.handle, 16)
            for g in range(HG):
                for b in range(B):
                    sp.dma_start(H3[:, g, b, 1:3], ins["h0"][:, g]).then_inc(tables_in.handle, 16)
            with sp.Fori(0, NSEG) as seg:
                def at(s, k):
                    return s.handle, seg * s.stride + k

                sp.wait_ge(started.handle, seg * 4 + 4)
                sp.sem_inc(seg_open.handle, 1)
                sp.dma_start(X[:, :, :], x_seg[bass.ds(seg, 1)].rearrange("a p b d -> (a p) b d"))\
                    .then_inc(*up16(x_in))

                def load(n):
                    s = n % SLOTS
                    if n >= SLOTS:
                        was = n - SLOTS
                        if was < len(GROUPS0) - 1:
                            sp.wait_ge(*at(slot_used, was + 1))
                        elif was < len(GROUPS0):
                            sp.wait_ge(*at(res, 4))
                        else:
                            e, second = divmod(was - len(GROUPS0), 2)
                            sp.wait_ge(*(at(down_mm, 2 * (e + 1)) if second else at(h1_mm, HT1 * (e + 1))))
                    if n < len(GROUPS0):
                        a, b = GROUPS0[n]
                        w = 768 * (b - a)
                        src = ins["w_ffn0"][:, 768 * a:768 * b]
                    else:
                        w, src = 2048, ins["w_ffn1"][n - len(GROUPS0)]
                    sp.dma_start(ring[:, s, 0:w], src).then_inc(*up16(ring_in[s]))

                for n in range(SLOTS):
                    load(n)
                sp.wait_ge(*at(beta_ok, 1))
                sp.dma_start(beta_d, betaT[:, :, :]).then_inc(*up16(kq_out))
                sp.wait_ge(*at(kq_out, 16))
                for half in range(2):
                    for b in range(B):
                        p0 = half * 64 + b * H0
                        sp.dma_start(beta_scan[p0:p0 + H0, :], beta_d.rearrange("h b t -> b h t")[b])\
                            .then_inc(*up16(beta_in))
                for z, (ready, sem) in enumerate(((k_unit, k_scan), (q_unit, q_scan), (v_unit, v_scan))):
                    sp.wait_ge(*at(ready, KC))
                    sp.dma_start(kqv_d[z].rearrange("(k p) b t -> p k b t", p=P), kqv[:, z]).then_inc(*up16(kq_out))
                    sp.wait_ge(*at(kq_out, kq_out.count))
                    for half in range(2):
                        for b in range(B):
                            p0 = half * 64 + b * H0
                            if z < 2:
                                src = kqv_d[z].rearrange("(h d) b t -> b h d t", h=H0)[b]
                                sp.dma_start(KQ[p0:p0 + H0, z], src).then_inc(*up16(sem))
                            else:
                                src = kqv_d[z].rearrange("(h g e) b t -> g b h e t", h=H0, g=2)[half, b]
                                sp.dma_start(V0[p0:p0 + H0], src).then_inc(*up16(sem))
                sp.wait_ge(*at(o0_ok, 1))
                for half in range(2):
                    for b in range(B):
                        p0 = half * 64 + b * H0
                        dst = o_d.rearrange("k h g e b t -> g b (k h) e t")[half, b]
                        sp.dma_start(dst, O0[p0:p0 + H0]).then_inc(*up16(o_out))
                sp.wait_ge(*at(o_out, o_out.stride))
                sp.dma_start(oT, o_d.rearrange("k h g e b t -> (h g e) k b t")).then_inc(*up16(o_in))
                for n in range(SLOTS, LOADS):
                    load(n)
                sp.wait_ge(*at(x_final, 1))
                sp.dma_start(out_seg[bass.ds(seg, 1)].rearrange("a p b d -> (a p) b d"), X[:, :, :])\
                    .then_inc(*up16(x_out))
                sp.wait_ge(*at(x_out, 16))
                sp.sem_inc(passed.handle, 1)
            for s in (x_in, x_out, kq_out, k_scan, q_scan, v_scan, o_out, o_in, *ring_in):
                assert s.count <= s.stride, (s.count, s.stride)

        @block.scalar
        def _(act):
            me = "act"

            def settle():
                s = last[me]
                act.wait_ge(s.handle, seg * s.stride + s.count)

            NTAB = 16 * (len(TABLES) + 3 + HG * B)
            act.wait_ge(tables_in.handle, NTAB)
            act.activation(silu_c[:, :, :, :].rearrange("p a k b -> p (a k b)"),
                           c_cols[:, :, :, :].rearrange("p a k b -> p (a k b)"), ACT.Silu).then_inc(silu_done.handle, 1)
            act.wait_ge(emb_sum.handle, 1)
            act.activation(emb_rnorm[:, :], bank[1][:, 0:E1], ACT.Sqrt).then_inc(emb_root.handle, 1)
            act.wait_ge(emb_root.handle, 1)
            act.sem_inc(started.handle, 1)
            with act.Fori(0, NSEG) as seg:
                def at(s, k):
                    return s.handle, seg * s.stride + k

                act.wait_ge(seg_open.handle, seg + 1)

                def layer_norm(n, blk, which):
                    act.wait_ge(*at(ln_var_ok, n + 1))
                    act.activation(ln_std[:, :], ln_var[:, :], ACT.Sqrt).then_inc(*up(ln_root, me))
                    act.wait_ge(*at(ln_tr, n + 1))
                    for k in range(KC):
                        for b in range(B):
                            ins_ = act.activation(hT[:, k, b, :], bank[k][:, b * SEG:(b + 1) * SEG], ACT.Identity,
                                                  bias=shift_scale[:, blk, which, k, b:b + 1],
                                                  scale=shift_scale[:, blk, which + 1, k, b:b + 1])
                    ins_.then_inc(*up(hT_ok, me))

                layer_norm(0, 0, 0)
                for z in range(3):
                    for k in range(KC):
                        n = z * KC + k
                        act.wait_ge(*at(proj, n + 1))
                        if z:
                            act.wait_ge(*at(px_free, (z - 1) * KC + k + 1))
                        act.activation(PX[:, k, :, PAST:], bank[2 + n % 2][:, :].rearrange("p (b t) -> p b t", b=B),
                                       ACT.Identity, bias=col("bqkv", n)).then_inc(*up(px_ok, me))
                act.wait_ge(*at(proj, 7))
                act.activation(betaT[:, :, :].rearrange("p b t -> p (b t)"), bank[4][0:H0, :], ACT.Sigmoid,
                               bias=col("bbeta")[0:H0]).then_inc(*up(beta_ok, me))
                for n in range(4):
                    act.wait_ge(*at(nrm, n + 1))
                    if n >= 2:
                        act.wait_ge(*at(v_unit, n - 1))
                    act.activation(rn[:, n % 2].rearrange("p b t -> p (b t)"), bank[5 + n % 2][:, :], ACT.Sqrt)\
                        .then_inc(*up(root, me))
                    if n < 2:
                        act.wait_ge(*at(conv_v, n + 1))
                        act.activation(kqv[:, 2, n], kqv[:, 2, n], ACT.Silu).then_inc(*up(v_silu, me))
                for k in range(KC):
                    act.wait_ge(*at(o_sq, KC + k + 1))
                    act.activation(rn[:, k], sq[:, k], ACT.Sqrt).then_inc(*up(root, me))

                layer_norm(1, 0, 2)
                act.wait_ge(*at(logit_sub, 1))
                act.activation(lg[:, 1], lg[:, 0], ACT.Exp).then_inc(*up(exp_ok, me))
                for i in range(TILES0):
                    act.wait_ge(*at(gate_mm, i + 1))
                    if i >= 2:
                        act.wait_ge(*at(hid0_ok, i - 1))
                    act.activation(sg0[:, i % 2].rearrange("p b t -> p (b t)"), bank[3 * (i % 2)][:, :], ACT.Silu)\
                        .then_inc(*up(sg_ok, me))

                layer_norm(2, 1, 0)
                for k in range(KC):
                    act.wait_ge(*at(u_mm, k + 1))
                    act.activation(uT[:, k].rearrange("p b t -> p (b t)"), bank[2 + k][:, :], ACT.Silu,
                                   bias=col("b_in", k)).then_inc(*up(u_ok, me))
                for hg in range(HG):
                    for c in range(6):
                        n = hg * 6 + c
                        act.wait_ge(*at(plane_mm, n + 1))
                        dst = (Q3[:, 1], Q3[:, 2], K2[:, 0], K2[:, 1])[c].rearrange("p b t -> p (b t)") if c < 4 \
                            else TT[:, c - 4, 0:NT]
                        if hg and c == 0:
                            act.wait_ge(*at(y_mm, 2 * hg))
                        if hg and c == 2:
                            act.wait_ge(*at(kt_mm, B * hg))
                        if hg and c == 4:
                            act.wait_ge(*at(state_ok, hg))
                        act.activation(dst, bank[n % 4][:, :], ACT.Identity, bias=col("b_qka", n))\
                            .then_inc(*up(plane_ok, me))
                    act.wait_ge(*at(mag_ok, hg + 1))
                    act.activation(t2[:, 0], t1[:, 0], ACT.Sqrt).then_inc(*up(mag_root, me))
                    act.wait_ge(*at(zeroed, 2))
                    for h in range(HP):
                        for r in range(2):
                            act.activation(Hx[32 * h:32 * h + 32, :, r, h],
                                           H3[32 * h:32 * h + 32, hg, :, 1 - r:3 - r].rearrange("p b r e -> p b (r e)"),
                                           ACT.Copy).then_inc(*up(hx_ok, me))
                    for lev in range(LEVELS):
                        m = 1 << lev
                        for bp in range(2):
                            u = (hg * LEVELS + lev) * 2 + bp
                            if lev:
                                act.wait_ge(*at(k_ready, u - 1))
                            if u >= 2:
                                act.wait_ge(*at(scored, 2 * (u - 1)))
                            for r in range(2):
                                for h in range(HP):
                                    src = K2[32 * h:32 * h + 32, r, 2 * bp:2 * bp + 2]
                                    dst = Kx[32 * h:32 * h + 32, r, h, 2 * bp:2 * bp + 2]
                                    if lev:
                                        half = "p b (n two m) -> p (b n) two m"
                                        src = src.rearrange(half, two=2, m=m // 2)[:, :, 0]
                                        dst = dst.rearrange(half, two=2, m=m // 2)[:, :, 0]
                                    ins_ = act.activation(dst, src, ACT.Copy)
                            ins_.then_inc(*up(kx_ready, me))
                    for j in range(2):
                        act.wait_ge(*at(y_mm, 2 * hg + j + 1))
                        act.activation(y2T[:, 2 * hg + j].rearrange("p b t -> p (b t)"), bank[4 + j][:, :], ACT.Copy)\
                            .then_inc(*up(y2_ok, me))
                    for b in range(B):
                        act.wait_ge(*at(kt_mm, hg * B + b + 1))
                        act.activation(KT[:, b].rearrange("p r c -> p (r c)"), bank[b][:, 0:2 * P], ACT.Copy)\
                            .then_inc(*up(kt_ok, me))
                for k in range(KC):
                    act.wait_ge(*at(y3_mm, k + 1))
                    act.activation(uT[:, k].rearrange("p b t -> p (b t)"), bank[k][:, :], ACT.Silu,
                                   bias=col("b_y", k)).then_inc(*up(y3_ok, me))

                layer_norm(3, 1, 2)
                act.wait_ge(*at(rt_var, 1))
                act.activation(rs[:, 1], rs[:, 0], ACT.Sqrt).then_inc(*up(rt_root, me))
                act.wait_ge(*at(rt_gap, 1))
                act.activation(rs[:, 11], rs[:, 10], ACT.Exp).then_inc(*up(rt_exp, me))
                for e in range(E1):
                    for t in range(HT1):
                        n = e * HT1 + t
                        act.wait_ge(*at(h1_mm, n + 1))
                        if e >= 2:
                            act.wait_ge(*at(down_mm, 2 * (e - 1)))
                        act.activation(hid1[:, e % 2, t].rearrange("p b t -> p (b t)"), bank[n % 4][:, :], ACT.Gelu,
                                       bias=col("b1", n)).then_inc(*up(hid1_ok, me))
                settle()
                top_up(act, [ln_root, hT_ok, px_ok, beta_ok, root, v_silu, exp_ok, sg_ok, u_ok, plane_ok, mag_root,
                             hx_ok, kx_ready, y2_ok, kt_ok, y3_ok, rt_root, rt_exp, hid1_ok])
                act.sem_inc(started.handle, 1)

        @block.vector
        def _(dve):
            me = "dve"

            NTAB = 16 * (len(TABLES) + 3 + HG * B)
            steps = [0]

            def once(ins_):
                steps[0] += 1
                ins_.then_inc(mod_rows_taken.handle, 1)
                dve.wait_ge(mod_rows_taken.handle, steps[0])

            once(dve.memset(past[:, :, :, :], 0.0))
            once(dve.memset(S0[:, :, :], 0.0))
            dve.wait_ge(tables_in.handle, NTAB)
            once(dve.tensor_scalar(H3[:, :, :, 0].rearrange("p g b e -> p (g b) e"),
                                   H3[:, :, :, 2].rearrange("p g b e -> p (g b) e"), -1.0, None, ALU.mult))
            esq = arena[:, 4096:4096 + KC * E1].rearrange("p (k e) -> p k e", k=KC)
            dve.tensor_tensor(esq, w_emb[:, :, :], w_emb[:, :, :], ALU.mult).then_inc(emb_sq.handle, 1)
            dve.wait_ge(silu_done.handle, 1)
            c_wide = arena[:, 0:2 * KC * B * P].rearrange("p (a j) -> p a j", j=P)
            once(dve.memset(c_wide, 1.0))
            dve.tensor_tensor(c_wide, c_wide, silu_c[:, :, :, :].rearrange("p a k b -> p (a k b)").unsqueeze(2)
                              .to_broadcast([P, 2 * KC * B, P]), ALU.mult).then_inc(emb_sq.handle, 1)
            dve.wait_ge(mod_cols.handle, 1)
            once(dve.tensor_copy(shift_scale[:, :, :, :, :].rearrange("p a w k b -> p (a w k b)"), bank[0][:, 0:64]))
            for blk in range(2):
                for w in (1, 3):
                    v = shift_scale[:, blk, w].rearrange("p k b -> p (k b)")
                    once(dve.tensor_scalar(v, v, 1.0, None, ALU.add))
            dve.wait_ge(emb_root.handle, 1)
            once(dve.tensor_scalar(emb_rnorm[:, :], emb_rnorm[:, :], 1e-8, None, ALU.add))
            once(dve.reciprocal(emb_rnorm[:, :], emb_rnorm[:, :]))
            dve.sem_inc(mod_cols.handle, 1)
            half_t = arena[:, 8192:8192 + 512]
            for i in range(8):
                g = gates[:, i // 4, (i // 2) % 2, 2 * (i % 2):2 * (i % 2) + 2].rearrange("p b d -> p (b d)")
                dve.wait_ge(mod_rows.handle, i + 1)
                once(dve.tensor_scalar(half_t, bank[i][:, :], 0.0, 2.0, ALU.is_ge, ALU.mult))
                once(dve.tensor_scalar(g, bank[i][:, :], -1.0, 0.25, ALU.mult, ALU.max))
                once(dve.tensor_tensor(g, g, bank[i][:, :], ALU.max))
                once(dve.scalar_tensor_tensor(g, half_t, -1.0, g, ALU.add, ALU.mult))
            dve.sem_inc(started.handle, 1)

            with dve.Fori(0, NSEG) as seg:
                def at(s, k):
                    return s.handle, seg * s.stride + k

                def settle():
                    s = last[me]
                    dve.wait_ge(s.handle, seg * s.stride + s.count)

                def step(ins_):
                    ins_.then_inc(*up(dve_step, me))
                    settle()

                def layer_norm(n):
                    if n == 0:
                        dve.wait_ge(*at(x_in, 16))
                    else:
                        settle()
                    for b in range(B):
                        ins_ = dve.bn_stats(ln_stats[:, b, :], X[:, b, :])
                    step(ins_)
                    dve.sem_inc(passed.handle, 1)
                    for b in range(B):
                        ins_ = dve.bn_aggr(ln_mv[:, b, :], ln_stats[:, b, :])
                    step(ins_)
                    dve.tensor_scalar(ln_var[:, :], ln_mv[:, :, 1], 1e-5, None, ALU.add).then_inc(*up(ln_var_ok, me))
                    dve.wait_ge(*at(ln_root, n + 1))
                    step(dve.reciprocal(ln_rstd[:, :], ln_std[:, :]))
                    for b in range(B):
                        ins_ = dve.tensor_scalar(xn[:, b, :], X[:, b, :], ln_mv[:, b, 0:1], ln_rstd[:, b:b + 1],
                                                 ALU.subtract, ALU.mult)
                    ins_.then_inc(*up(xn_ok, me))

                def residual(n, banks, blk, which, bias):
                    for j in range(2):
                        two = slice(2 * j, 2 * j + 2)
                        dve.wait_ge(*at(res, 2 * n + j + 1))
                        y = bank[banks[j]][:, :].rearrange("p (b d) -> p b d", b=2)
                        g = gates[:, blk, which, two]
                        if bias is None:
                            step(dve.tensor_tensor(xn[:, two], y, g, ALU.mult))
                        else:
                            step(dve.tensor_tensor(xn[:, two], y, row(bias).unsqueeze(1).to_broadcast([P, 2, D]),
                                                   ALU.add))
                            step(dve.tensor_tensor(xn[:, two], xn[:, two], g, ALU.mult))
                        dve.tensor_tensor(X[:, two], X[:, two], xn[:, two], ALU.add).then_inc(*up(x_done, me))

                dve.wait_ge(seg_open.handle, seg + 1)

                layer_norm(0)
                for z in range(3):
                    for k in range(KC):
                        n = z * KC + k
                        y = kqv[:, z, k]
                        step(dve.tensor_copy(PX[:, k, :, 0:PAST], past[:, n]))
                        dve.wait_ge(*at(px_ok, n + 1))
                        step(dve.tensor_scalar(y, PX[:, k, :, 0:SEG], col("w_conv", 4 * n), col("bqkv_conv", n),
                                               ALU.mult, ALU.add))
                        for i in range(1, TAPS):
                            step(dve.scalar_tensor_tensor(y, PX[:, k, :, i:i + SEG], col("w_conv", 4 * n + i), y,
                                                          ALU.mult, ALU.add))
                        dve.tensor_copy(past[:, n], PX[:, k, :, SEG:]).then_inc(*up(px_free, me))
                        if z < 2:
                            if z:
                                dve.wait_ge(*at(nrm, k + 1))
                            dve.tensor_tensor(sq[:, k], y, y, ALU.mult).then_inc(*up(k_sq, me))
                        else:
                            settle()
                            dve.sem_inc(*up(conv_v))
                for z in range(2):
                    for k in range(KC):
                        n = z * KC + k
                        dve.wait_ge(*at(root, n + 1))
                        step(dve.tensor_scalar(rn[:, k], rn[:, k], 1e-6, None, ALU.add))
                        step(dve.reciprocal(rn[:, k], rn[:, k]))
                        dve.tensor_tensor(kqv[:, z, k], kqv[:, z, k], rn[:, k], ALU.mult)\
                           .then_inc(*up((k_unit, q_unit)[z], me))
                        if z == 0:
                            dve.wait_ge(*at(v_silu, k + 1))
                            dve.tensor_tensor(kqv[:, 2, k], kqv[:, 2, k], rn[:, k], ALU.mult)\
                               .then_inc(*up(v_unit, me))
                dve.wait_ge(*at(beta_in, beta_in.stride))
                dve.wait_ge(*at(v_scan, v_scan.stride))
                step(dve.tensor_tensor(V0[:, :, :], V0[:, :, :], beta_scan[:, :].unsqueeze(1)
                                       .to_broadcast([P, EV, SEG]), ALU.mult))
                step(dve.tensor_scalar(nbeta[:, :], beta_scan[:, :], -1.0, None, ALU.mult))
                dve.wait_ge(*at(k_scan, k_scan.stride))
                dve.wait_ge(*at(q_scan, q_scan.stride))
                S_twice = S0[:, :, :].unsqueeze(1).to_broadcast([P, 2, EV, HD0])
                for t in range(SEG):
                    step(dve.tensor_tensor(prod[:, :, :, :], S_twice, KQ[:, :, :, t].unsqueeze(2)
                                           .to_broadcast([P, 2, EV, HD0]), ALU.mult))
                    step(dve.tensor_reduce(KQ_S[:, t], prod[:, :, :, :], AX.X, ALU.add))
                    step(dve.scalar_tensor_tensor(delta[:, t], KQ_S[:, t, 0], nbeta[:, t:t + 1], V0[:, :, t],
                                                  ALU.mult, ALU.add))
                    step(dve.tensor_tensor(outer[:, :, :], delta[:, t].unsqueeze(2).to_broadcast([P, EV, HD0]),
                                           KQ[:, 0, :, t].unsqueeze(1).to_broadcast([P, EV, HD0]), ALU.mult))
                    step(dve.tensor_tensor(S0[:, :, :], S0[:, :, :], outer[:, :, :], ALU.add))
                step(dve.tensor_tensor(tmp_dot[:, :, :], KQ[:, 0], KQ[:, 1], ALU.mult))
                step(dve.tensor_reduce(qk_dot[:, :], tmp_dot[:, :, :].rearrange("p d t -> p t d"), AX.X, ALU.add))
                step(dve.tensor_tensor(delta[:, :, :], delta[:, :, :], qk_dot[:, :].unsqueeze(2)
                                       .to_broadcast([P, SEG, EV]), ALU.mult))
                dve.tensor_tensor(O0[:, :, :].rearrange("p e t -> p t e"), KQ_S[:, :, 1], delta[:, :, :], ALU.add)\
                   .then_inc(*up(o0_ok, me))
                dve.wait_ge(*at(o_in, 16))
                for k in range(KC):
                    dve.tensor_tensor(sq[:, k], oT[:, k], oT[:, k], ALU.mult).then_inc(*up(o_sq, me))
                for k in range(KC):
                    dve.wait_ge(*at(nrm, 5 + k))
                    dve.tensor_scalar(sq[:, k].rearrange("p b t -> p (b t)"), bank[5 + k][:, :], 1.0 / HD0, 1e-6,
                                      ALU.mult, ALU.add).then_inc(*up(o_sq, me))
                for k in range(KC):
                    dve.wait_ge(*at(root, 5 + k))
                    step(dve.reciprocal(rn[:, k], rn[:, k]))
                    dve.scalar_tensor_tensor(oT[:, k], oT[:, k], col("norm_w"), rn[:, k], ALU.mult, ALU.mult)\
                       .then_inc(*up(o_norm_ok, me))
                residual(0, (2, 3), 0, 0, "bo")

                layer_norm(1)

                def wide(v, n):
                    return v.unsqueeze(2).to_broadcast([P, B, n])

                def pick(best, hot, scores, tie, rev, s1, s2, m):
                    n = rev.shape[-1]
                    step(dve.tensor_reduce(best, scores, AX.X, ALU.max))
                    step(dve.tensor_tensor(s1, scores, wide(best, n), ALU.is_equal))
                    if tie is not None:
                        step(dve.tensor_scalar(s1, s1, 1e30, -1e30, ALU.mult, ALU.add))
                        step(dve.tensor_tensor(s1, s1, tie, ALU.add))
                        step(dve.tensor_reduce(m, s1, AX.X, ALU.max))
                        step(dve.tensor_tensor(s1, s1, wide(m, n), ALU.is_equal))
                    step(dve.tensor_tensor(s2, s1, rev.unsqueeze(1).to_broadcast([P, B, n]), ALU.mult))
                    step(dve.tensor_reduce(m, s2, AX.X, ALU.max))
                    step(dve.tensor_tensor(hot, s2, wide(m, n), ALU.is_equal))

                dve.wait_ge(*at(router, 1))
                logits = bank[7][:, 0:B * E0].rearrange("p (b e) -> p b e", b=B)
                step(dve.tensor_reduce(sm[:, 0], logits, AX.X, ALU.max))
                dve.tensor_tensor(lg[:, 0], logits, wide(sm[:, 0], E0), ALU.subtract).then_inc(*up(logit_sub, me))
                dve.wait_ge(*at(exp_ok, 1))
                step(dve.tensor_reduce(sm[:, 1], lg[:, 1], AX.X, ALU.add))
                step(dve.reciprocal(sm[:, 2], sm[:, 1]))
                step(dve.tensor_tensor(lg[:, 2], lg[:, 1], wide(sm[:, 2], E0), ALU.mult))
                pick(sm[:, 3], lg[:, 3], lg[:, 2], None, const("rev16"), lg[:, 4], lg[:, 5], sm[:, 4])
                step(dve.scalar_tensor_tensor(lg[:, 6].rearrange("p b e -> p (b e)"),
                                              lg[:, 3].rearrange("p b e -> p (b e)"), -4.0,
                                              lg[:, 2].rearrange("p b e -> p (b e)"), ALU.mult, ALU.add))
                pick(sm[:, 5], lg[:, 7], lg[:, 6], None, const("rev16"), lg[:, 4], lg[:, 5], sm[:, 4])
                step(dve.tensor_tensor(sm[:, 6], sm[:, 3], sm[:, 5], ALU.add))
                step(dve.tensor_scalar(sm[:, 6], sm[:, 6], 1e-9, None, ALU.add))
                step(dve.reciprocal(sm[:, 7], sm[:, 6]))
                step(dve.tensor_tensor(lg[:, 8], lg[:, 3], lg[:, 7], ALU.add))
                step(dve.tensor_tensor(lg[:, 8], lg[:, 8], lg[:, 2], ALU.mult))
                dve.tensor_tensor(lg[:, 9], lg[:, 8], wide(sm[:, 7], E0), ALU.mult).then_inc(*up(comb_ok, me))
                dve.wait_ge(*at(comb_tr, 1))
                dve.tensor_copy(combT[:, :, :].rearrange("p b t -> p (b t)"), bank[6][0:E0, :])\
                   .then_inc(*up(comb_copied, me))
                for i in range(TILES0):
                    h = hid0[:, i].rearrange("p b t -> p (b t)")
                    dve.wait_ge(*at(sg_ok, i + 1))
                    dve.wait_ge(*at(up_mm, i + 1))
                    ins_ = dve.tensor_tensor(h, sg0[:, i % 2].rearrange("p b t -> p (b t)"),
                                             bank[3 * (i % 2) + 1][:, :], ALU.mult)
                    if i < ROUTED0:
                        step(ins_)
                        ins_ = dve.tensor_tensor(h, h, bank[3 * (i % 2) + 2][:, :], ALU.mult)
                    ins_.then_inc(*up(hid0_ok, me))
                residual(1, (6, 7), 0, 1, None)

                layer_norm(2)
                for b in range(B):
                    dve.wait_ge(*at(v_mm, b + 1))
                    step(dve.tensor_tensor(V3[:, b, :, 1:3, :].rearrange("p h r e -> p h (r e)"),
                                           bank[4 + b][:, :].rearrange("p (h j) -> p h j", h=H1),
                                           row("b_v").rearrange("p (h j) -> p h j", h=H1), ALU.add))
                    dve.tensor_scalar(V3[:, b, :, 0, :], V3[:, b, :, 2, :], -1.0, None, ALU.mult)\
                       .then_inc(*up(v3_ok, me))
                flat = "p r b t -> p r (b t)"
                for hg in range(HG):
                    q2 = Q3[:, 1:3].rearrange(flat)
                    k2 = K2[:, :].rearrange(flat)
                    a2 = TT[:, :, 0:NT]

                    def twice(v):
                        return v.unsqueeze(1).to_broadcast([P, 2, v.shape[-1]])

                    dve.wait_ge(*at(plane_ok, 6 * hg + 6))
                    step(dve.tensor_tensor(t1[:, :, :], a2, a2, ALU.mult))
                    dve.tensor_tensor(t1[:, 0], t1[:, 0], t1[:, 1], ALU.add).then_inc(*up(mag_ok, me))
                    settle()
                    step(dve.tensor_scalar(t1[:, 1], t1[:, 0], 1.0, None, ALU.add))
                    step(dve.reciprocal(t1[:, 1], t1[:, 1]))
                    dve.wait_ge(*at(mag_root, hg + 1))
                    step(dve.tensor_tensor(t1[:, 0], t2[:, 0], t1[:, 1], ALU.mult))
                    step(dve.tensor_tensor(a2, a2, twice(t1[:, 0]), ALU.mult))
                    step(dve.tensor_tensor(t1[:, :, :], q2, twice(k2[:, 0]), ALU.mult))
                    step(dve.tensor_tensor(t2[:, :, :], q2, twice(k2[:, 1]), ALU.mult))
                    step(dve.tensor_tensor(t1[:, 0], t1[:, 0], t2[:, 1], ALU.subtract))
                    dve.tensor_tensor(t1[:, 1], t1[:, 1], t2[:, 0], ALU.add).then_inc(*up(pairs_ok, me))
                    step(dve.tensor_scalar(Q3[:, 0], Q3[:, 2], -1.0, None, ALU.mult))
                    off = 0
                    for lev in range(LEVELS):
                        n = NT >> lev
                        w = TT[:, :, off:off + n].rearrange("p r (j two) -> p r j two", two=2)
                        nxt = TT[:, :, off + n:off + n + n // 2]
                        ta, tb = t2[:, :, 0:n // 2], t2[:, :, 256:256 + n // 2]
                        step(dve.tensor_tensor(ta, w[:, :, :, 0], twice(w[:, 0, :, 1]), ALU.mult))
                        step(dve.tensor_tensor(tb, w[:, :, :, 0], twice(w[:, 1, :, 1]), ALU.mult))
                        step(dve.tensor_tensor(nxt[:, 0], ta[:, 0], tb[:, 1], ALU.subtract))
                        step(dve.tensor_tensor(nxt[:, 1], ta[:, 1], tb[:, 0], ALU.add))
                        off += n
                    dve.sem_inc(*up(a_ok))
                    dve.wait_ge(*at(diag_mm, hg + 1))
                    dve.tensor_copy(diag[:, :, :, :].rearrange("p b h r -> p (b h r)"), bank[6][:, 0:B * HP * 2])\
                       .then_inc(*up(diag_ok, me))
                    step(dve.tensor_tensor(t1[:, :, :], q2, twice(TT[:, 0, 0:NT]), ALU.mult))
                    step(dve.tensor_tensor(t2[:, :, :], Q3[:, 0:2].rearrange(flat), twice(TT[:, 1, 0:NT]), ALU.mult))
                    step(dve.tensor_tensor(q2, t1[:, :, :], t2[:, :, :], ALU.add))
                    for bp in range(2):
                        two = slice(2 * bp, 2 * bp + 2)
                        dve.tensor_scalar(Q3[:, 0, two], Q3[:, 2, two], -1.0, None, ALU.mult).then_inc(*up(q_ready, me))
                    off = 0
                    for lev in range(LEVELS):
                        m = 1 << lev
                        nb = SEG // (2 * m)
                        for bp in range(2):
                            u = (hg * LEVELS + lev) * 2 + bp
                            for i in range(2):
                                b = 2 * bp + i
                                dve.wait_ge(*at(scored, 2 * u + i + 1))
                                if lev == 0:
                                    dve.wait_ge(*at(score_init, B * hg + b + 1))
                                dve.sem_inc(passed.handle, 1)
                                dst = score[:, b].rearrange("p h r (n two m) -> p (h r) n two m", two=2, m=m)[:, :, :, 1]
                                dve.copy_predicated(
                                    dst,
                                    masks[:, lev].rearrange("p (n m) -> p n m", m=m).unsqueeze(1)
                                    .to_broadcast([P, 2 * HP, nb, m]),
                                    bank[b][:, :].rearrange("p (g n m) -> p g n m", g=2 * HP, m=m))\
                                   .then_inc(*up(masked, me))
                            n = 2 * nb
                            half = "p r b (n two m) -> p r (b n) two m"
                            two = slice(2 * bp, 2 * bp + 2)
                            Tb = TT[:, :, off + bp * 2 * n:off + (bp + 1) * 2 * n]\
                                .rearrange("p r (n two) -> p r n two", two=2)[:, :, :, 0]

                            def over(v):
                                return v.unsqueeze(1).unsqueeze(3).to_broadcast([P, 2, n, m])

                            def tmp(t):
                                return t[:, :, 0:P].rearrange("p r (n m) -> p r n m", m=m)

                            q_hi = Q3[:, 1:3, two].rearrange(half, two=2, m=m)[:, :, :, 1]
                            q_lo = Q3[:, 0:2, two].rearrange(half, two=2, m=m)[:, :, :, 1]
                            dve.tensor_tensor(tmp(t1), q_hi, over(Tb[:, 0]), ALU.mult).then_inc(*up(dve_step, me))
                            step(dve.tensor_tensor(tmp(t2), q_lo, over(Tb[:, 1]), ALU.mult))
                            step(dve.tensor_tensor(q_hi, tmp(t1), tmp(t2), ALU.add))
                            dve.tensor_scalar(q_lo[:, 0], q_hi[:, 1], -1.0, None, ALU.mult).then_inc(*up(q_ready, me))
                        off += NT >> lev
                    dve.wait_ge(*at(r_mm, hg + 1))
                    settle()
                    for b in range(B):
                        old = t1[:, 0, 64 * b:64 * b + 64]
                        step(dve.scalar_tensor_tensor(old, H3[:, hg, b, 1:3].rearrange("p r e -> p (r e)"),
                                                      TT[:, 0, off + b:off + b + 1],
                                                      bank[7][:, 64 * b:64 * b + 64], ALU.mult, ALU.add))
                        step(dve.scalar_tensor_tensor(t1[:, 1, 64 * b:64 * b + 64],
                                                      H3[:, hg, b, 0:2].rearrange("p r e -> p (r e)"),
                                                      TT[:, 1, off + b:off + b + 1], old, ALU.mult, ALU.add))
                    step(dve.tensor_copy(H3[:, hg, :, 1:3].rearrange("p b r e -> p b (r e)"),
                                         t1[:, 1, 0:256].rearrange("p (b j) -> p b j", b=B)))
                    dve.tensor_scalar(H3[:, hg, :, 0], H3[:, hg, :, 2], -1.0, None, ALU.mult)\
                       .then_inc(*up(state_ok, me))
                residual(2, (2, 3), 1, 0, "b_out")

                layer_norm(3)
                dve.wait_ge(*at(hT_ok, 4))
                dve.tensor_tensor(sqh[:, :, :, :], hT[:, :, :, :], hT[:, :, :, :], ALU.mult).then_inc(*up(hsq_ok, me))
                dve.wait_ge(*at(router, 2))
                dve.tensor_copy(rs[:, 0], bank[7][:, 32:36]).then_inc(*up(rt_var, me))
                sim = rt[:, 0]
                step(dve.tensor_copy(sim, bank[7][:, 0:B * E1].rearrange("p (b e) -> p b e", b=B)))
                step(dve.tensor_scalar(rt[:, 1], sim, -1.0, None, ALU.mult))
                pick(rs[:, 2], rt[:, 2], rt[:, 1], None, const("up8"), rt[:, 3], rt[:, 4], rs[:, 3])
                dve.wait_ge(*at(rt_root, 1))
                step(dve.tensor_scalar(rs[:, 4], rs[:, 1], 1e-8, None, ALU.add))
                step(dve.reciprocal(rs[:, 5], rs[:, 4]))
                step(dve.tensor_tensor(rt[:, 5], sim, emb_rnorm[:, :].unsqueeze(1).to_broadcast([P, B, E1]), ALU.mult))
                step(dve.tensor_tensor(rt[:, 5], rt[:, 5], wide(rs[:, 5], E1), ALU.mult))
                step(dve.tensor_scalar(rt[:, 6], row("cache").unsqueeze(1).to_broadcast([P, B, E1]), 0.1, None,
                                       ALU.mult))
                step(dve.tensor_tensor(rt[:, 5], rt[:, 5], rt[:, 6], ALU.add))

                def flat2(v):
                    return v.rearrange("p b e -> p (b e)")

                step(dve.scalar_tensor_tensor(flat2(rt[:, 5]), flat2(rt[:, 2]), -1e30, flat2(rt[:, 5]),
                                              ALU.mult, ALU.add))
                pick(rs[:, 6], rt[:, 7], rt[:, 5], sim, const("rev8"), rt[:, 3], rt[:, 4], rs[:, 3])
                step(dve.scalar_tensor_tensor(flat2(rt[:, 8]), flat2(rt[:, 7]), -1e30, flat2(rt[:, 5]),
                                              ALU.mult, ALU.add))
                pick(rs[:, 7], rt[:, 9], rt[:, 8], sim, const("rev8"), rt[:, 3], rt[:, 4], rs[:, 3])
                dve.tensor_tensor(rs[:, 10], rs[:, 7], rs[:, 6], ALU.subtract).then_inc(*up(rt_gap, me))
                dve.wait_ge(*at(rt_exp, 1))
                step(dve.tensor_scalar(rs[:, 12], rs[:, 11], 1.0, None, ALU.add))
                step(dve.reciprocal(rs[:, 13], rs[:, 12]))
                step(dve.tensor_tensor(rs[:, 14], rs[:, 11], rs[:, 13], ALU.mult))
                step(dve.tensor_tensor(rt[:, 7], rt[:, 7], wide(rs[:, 13], E1), ALU.mult))
                step(dve.tensor_tensor(rt[:, 9], rt[:, 9], wide(rs[:, 14], E1), ALU.mult))
                dve.tensor_tensor(rt[:, 10], rt[:, 7], rt[:, 9], ALU.add).then_inc(*up(comb1_ok, me))
                dve.wait_ge(*at(comb_tr, 2))
                dve.tensor_copy(combT1[:, :, :].rearrange("p b t -> p (b t)"), bank[6][0:E1, :])\
                   .then_inc(*up(comb1_copied, me))
                for j in range(2):
                    dve.wait_ge(*at(down_bias, j + 1))
                    dve.tensor_copy(acc[:, 2 * j:2 * j + 2].rearrange("p b d -> p (b d)"), bank[6 + j][:, :])\
                       .then_inc(*up(acc_ok, me))
                for e in range(E1):
                    settle()
                    for j in range(2):
                        dve.wait_ge(*at(down_mm, 2 * e + j + 1))
                        for i in range(2):
                            b = 2 * j + i
                            ins_ = dve.scalar_tensor_tensor(acc[:, b], bank[4 + 2 * (e % 2) + j][:, i * D:(i + 1) * D],
                                                            rt[:, 10, b, e:e + 1], acc[:, b], ALU.mult, ALU.add)
                        ins_.then_inc(*up(acc_ok, me))
                settle()
                step(dve.tensor_tensor(xn[:, :, :], acc[:, :, :], gates[:, 1, 1], ALU.mult))
                dve.tensor_tensor(X[:, :, :], X[:, :, :], xn[:, :, :], ALU.add).then_inc(*up(x_final, me))
                settle()
                top_up(dve, [dve_step, ln_var_ok, xn_ok, px_free, k_sq, conv_v, k_unit, q_unit, v_unit, o0_ok, o_sq,
                             o_norm_ok, logit_sub, comb_ok, comb_copied, hid0_ok, x_done, mag_ok, v3_ok, a_ok,
                             pairs_ok, diag_ok, q_ready, masked, state_ok, hsq_ok, rt_var, rt_gap, comb1_ok,
                             comb1_copied, acc_ok, x_final])
                dve.sem_inc(started.handle, 1)

        @block.gpsimd
        def _(pool):
            me = "pool"
            pool.sem_inc(started.handle, 1)
            with pool.Fori(0, NSEG) as seg:
                def at(s, k):
                    return s.handle, seg * s.stride + k

                def settle():
                    s = last[me]
                    pool.wait_ge(s.handle, seg * s.stride + s.count)

                def step(ins_):
                    ins_.then_inc(*up(pool_step, me))
                    settle()

                pool.wait_ge(*at(ln_var_ok, 3))
                pool.sem_inc(passed.handle, 1)
                pool.memset(Kx[:, :, :, :, :].rearrange("p r h b t -> p (r h b t)"), 0.0).then_inc(*up(zeroed, me))
                pool.memset(Hx[:, :, :, :, :].rearrange("p b r h j -> p (b r h j)"), 0.0).then_inc(*up(zeroed, me))
                for hg in range(HG):
                    pool.wait_ge(*at(diag_ok, hg + 1))
                    if hg:
                        pool.wait_ge(*at(y_mm, 2 * hg))
                    for b in range(B):
                        pool.tensor_tensor(score[:, b].rearrange("p h r t -> p (h r) t"),
                                           ident.unsqueeze(1).to_broadcast([P, 2 * HP, SEG]),
                                           diag[:, b].rearrange("p h r -> p (h r)").unsqueeze(2)
                                           .to_broadcast([P, 2 * HP, SEG]), ALU.mult).then_inc(*up(score_init, me))
                    off = 0
                    for lev in range(LEVELS):
                        m = 1 << lev
                        n = SEG // m
                        for bp in range(2):
                            u = (hg * LEVELS + lev) * 2 + bp
                            pool.wait_ge(*at(kx_ready, u + 1))
                            if lev == 0:
                                pool.wait_ge(*at(a_ok, hg + 1))
                            two = slice(2 * bp, 2 * bp + 2)
                            Tb = TT[:, :, off + bp * 2 * n:off + (bp + 1) * 2 * n]\
                                .rearrange("p r (n two) -> p r n two", two=2)[:, :, :, 1]

                            def over(v):
                                return v.unsqueeze(1).unsqueeze(3).to_broadcast([P, 2, n, m])

                            def tmp(t):
                                return t[:, :, 0:P].rearrange("p r (n m) -> p r n m", m=m)

                            kk = K2[:, :, two].rearrange("p r b (n two m) -> p r (b n) two m", two=2, m=m)[:, :, :, 0]
                            settle()
                            pool.tensor_tensor(tmp(u1), kk, over(Tb[:, 0]), ALU.mult).then_inc(*up(pool_step, me))
                            step(pool.tensor_tensor(tmp(u2), kk, over(Tb[:, 1]), ALU.mult))
                            pool.tensor_tensor(kk[:, 0], tmp(u1)[:, 0], tmp(u2)[:, 1], ALU.subtract)\
                                .then_inc(*up(pool_step, me))
                            pool.tensor_tensor(kk[:, 1], tmp(u1)[:, 1], tmp(u2)[:, 0], ALU.add)\
                                .then_inc(*up(k_ready, me))
                        off += NT >> lev
                settle()
                top_up(pool, [pool_step, zeroed, score_init, k_ready])
                pool.sem_inc(started.handle, 1)

        @block.tensor
        def _(pe):
            NTAB = 16 * (len(TABLES) + 3 + HG * B)
            mm = pe.matmul
            pe.wait_ge(tables_in.handle, NTAB)
            pe.wait_ge(emb_sq.handle, 2)
            esq = arena[:, 4096:4096 + KC * E1].rearrange("p (k e) -> p k e", k=KC)
            for k in range(KC):
                i_ = mm(bank[1][:, 0:E1], const("ones"), esq[:, k], start=(k == 0), stop=(k == KC - 1))
            i_.then_inc(emb_sum.handle, 1)
            for blk in range(2):
                for w, src in enumerate((0, 1, 3, 4)):
                    for kc in range(KC):
                        at_ = ((blk * 4 + w) * KC + kc) * B
                        for k in range(KC):
                            i_ = mm(bank[0][:, at_:at_ + B], wmod[blk][:, k, src * D + kc * P:src * D + kc * P + P],
                                    silu_c[:, blk, k, :], start=(k == 0), stop=(k == KC - 1))
            i_.then_inc(mod_cols.handle, 1)
            pe.wait_ge(mod_cols.handle, 2)
            c_wide = arena[:, 0:2 * KC * B * P].rearrange("p (a k b j) -> p a k b j", a=2, k=KC, b=B)
            for i in range(8):
                blk, g = i // 4, (i // 2) % 2
                for j in range(2):
                    b = 2 * (i % 2) + j
                    for k in range(KC):
                        src = (2 + 3 * g) * D
                        i_ = mm(bank[i][:, j * D:(j + 1) * D], c_wide[:, blk, k, b], wmod[blk][:, k, src:src + D],
                                start=(k == 0), stop=(k == KC - 1))
                i_.then_inc(mod_rows.handle, 1)
            pe.sem_inc(started.handle, 1)

            with pe.Fori(0, NSEG) as seg:
                def at(s, k):
                    return s.handle, seg * s.stride + k

                def rhs(t, k):
                    return t[:, k].rearrange("p b t -> p (b t)")

                def layer_norm(n):
                    pe.wait_ge(*at(xn_ok, n + 1))
                    for k in range(KC):
                        for b in range(B):
                            i_ = pe.transpose(bank[k][:, b * SEG:(b + 1) * SEG], xn[:, b, k * P:(k + 1) * P], ident)
                    i_.then_inc(*up(ln_tr))
                    pe.wait_ge(*at(hT_ok, n + 1))

                def channels(dst, w, cols_, src, n=KC):
                    for k in range(n):
                        i_ = mm(dst, w[:, k, cols_], rhs(src, k), start=(k == 0), stop=(k == n - 1))
                    return i_

                def tokens(banks, src, w):
                    for j in range(2):
                        for i in range(2):
                            for k in range(KC):
                                i_ = mm(bank[banks[j]][:, i * D:(i + 1) * D], src[:, k, 2 * j + i, :], w[:, k, :],
                                        start=(k == 0), stop=(k == KC - 1))
                        i_.then_inc(*up(res))

                pe.wait_ge(seg_open.handle, seg + 1)
                layer_norm(0)
                for n in range(6):
                    if n >= 2:
                        pe.wait_ge(*at(px_ok, n - 1))
                    channels(bank[2 + n % 2][:, :], w_qkv, slice(n * P, (n + 1) * P), hT).then_inc(*up(proj))
                channels(bank[4][0:H0, :], w_beta, slice(0, H0), hT).then_inc(*up(proj))
                for n in range(4):
                    pe.wait_ge(*at(k_sq, n + 1))
                    if n >= 2:
                        pe.wait_ge(*at(root, n - 1))
                    mm(bank[5 + n % 2][:, :], const("ones16"), rhs(sq, n % 2), start=True, stop=True)\
                        .then_inc(*up(nrm))
                for k in range(KC):
                    pe.wait_ge(*at(o_sq, k + 1))
                    pe.wait_ge(*at(root, 3 + k))
                    mm(bank[5 + k][:, :], const("ones16"), rhs(sq, k), start=True, stop=True).then_inc(*up(nrm))
                pe.wait_ge(*at(o_norm_ok, KC))
                tokens((2, 3), oT, w_o)

                layer_norm(1)
                for b in range(B):
                    for k in range(KC):
                        i_ = mm(bank[7][:, b * E0:(b + 1) * E0], hT[:, k, b, :], w_router[:, k, :],
                                start=(k == 0), stop=(k == KC - 1))
                i_.then_inc(*up(router))

                def ring0(g):
                    n = GROUPS0[g][1] - GROUPS0[g][0]
                    w = n * P
                    r = ring[:, g]
                    return (r[:, 0:2 * w].rearrange("p (k c) -> p k c", k=KC),
                            r[:, 2 * w:4 * w].rearrange("p (k c) -> p k c", k=KC),
                            r[:, 4 * w:4 * w + n * D].rearrange("p (t c) -> p t c", t=n))

                def spread(i):
                    mm(bank[3 * (i % 2) + 2][:, :], sel[:, i, :], combT[:, :, :].rearrange("e b t -> e (b t)"),
                       start=True, stop=True).then_inc(*up(up_mm))

                def turn_weights(n, src, width):
                    for b in range(B):
                        i_ = pe.transpose(bank[6][0:width, b * SEG:(b + 1) * SEG], src[:, b, :], ident)
                    i_.then_inc(*up(comb_tr))

                for g, (first, end) in enumerate(GROUPS0):
                    pe.wait_ge(*at(ring_in[g], 16))
                    wg, wu, _ = ring0(g)
                    for i in range(first, end):
                        if i == 2:
                            pe.wait_ge(*at(comb_ok, 1))
                            turn_weights(0, lg[:, 9], E0)
                            pe.wait_ge(*at(comb_copied, 1))
                            spread(0)
                            spread(1)
                        if i >= 2:
                            pe.wait_ge(*at(sg_ok, i - 1))
                            pe.wait_ge(*at(hid0_ok, i - 1))
                        c = slice((i - first) * P, (i - first + 1) * P)
                        channels(bank[3 * (i % 2)][:, :], wg, c, hT).then_inc(*up(gate_mm))
                        i_ = channels(bank[3 * (i % 2) + 1][:, :], wu, c, hT)
                        if i >= ROUTED0:
                            i_.then_inc(*up(up_mm))
                        elif i >= 2:
                            spread(i)
                pe.wait_ge(*at(hid0_ok, TILES0))
                for b in range(B):
                    for g, (first, end) in enumerate(GROUPS0):
                        wd = ring0(g)[2]
                        for i in range(first, end):
                            i_ = mm(bank[6 + b // 2][:, (b % 2) * D:(b % 2 + 1) * D], hid0[:, i, b, :],
                                    wd[:, i - first, :], start=(i == 0), stop=(i == TILES0 - 1))
                        if b == B - 1 and g < len(GROUPS0) - 1:
                            i_.then_inc(*up(slot_used))
                    if b % 2:
                        i_.then_inc(*up(res))

                layer_norm(2)
                for k in range(KC):
                    channels(bank[2 + k][:, :], w_in, slice(k * P, (k + 1) * P), hT).then_inc(*up(u_mm))
                pe.wait_ge(*at(u_ok, KC))
                for b in range(B):
                    for k in range(KC):
                        i_ = mm(bank[4 + b][:, :], uT[:, k, b, :], w_v[:, k, :], start=(k == 0), stop=(k == KC - 1))
                    i_.then_inc(*up(v_mm))
                for hg in range(HG):
                    if hg:
                        pe.wait_ge(*at(kt_ok, B * hg))
                    for c in range(6):
                        n = hg * 6 + c
                        if c >= 4:
                            pe.wait_ge(*at(plane_ok, n - 3))
                        channels(bank[n % 4][:, :], w_qka[:, :, n, :],
                                 slice(0, P), uT).then_inc(*up(plane_mm))
                    pe.wait_ge(*at(v3_ok, B))
                    pe.wait_ge(*at(pairs_ok, hg + 1))
                    d6 = bank[6][:, 0:B * HP * 2].rearrange("p (b h r) -> p b h r", b=B, r=2)
                    for b in range(B):
                        for r in range(2):
                            i_ = mm(d6[:, b, :, r], t1[:, r, b * SEG:(b + 1) * SEG], const("head_of"),
                                    start=True, stop=True)
                    i_.then_inc(*up(diag_mm))
                    for lev in range(LEVELS):
                        m = 1 << lev
                        for bp in range(2):
                            u = (hg * LEVELS + lev) * 2 + bp
                            pe.wait_ge(*at(kx_ready, u + 1))
                            pe.wait_ge(*at(q_ready, hg * 16 + lev * 2 + bp + 1))
                            if lev:
                                pe.wait_ge(*at(masked, 2 * (u - 1)))
                            for b in (2 * bp, 2 * bp + 1):
                                for h in range(HP):
                                    for r in range(2):
                                        qv = Q3[:, 1 - r:3 - r, b].rearrange("p r (n two m) -> p r n two m",
                                                                             two=2, m=m)[:, :, :, 1]
                                        i_ = mm(bank[b][:, h * P:(h + 1) * P], Kx[:, r, h, b, :], qv,
                                                start=(r == 0), stop=(r == 1))
                                i_.then_inc(*up(scored))
                    pe.wait_ge(*at(hx_ok, 2 * HP * (hg + 1)))
                    pe.wait_ge(*at(q_ready, hg * 16 + 16))
                    pe.wait_ge(*at(masked, 28 * (hg + 1)))
                    for j in range(2):
                        for b in range(B):
                            y = bank[4 + j][:, b * SEG:(b + 1) * SEG]
                            for r in range(2):
                                mm(y, Hx[:, b, r, 2 * j:2 * j + 2].rearrange("p h j -> p (h j)"),
                                   Q3[:, 1 + r, b, :], start=(r == 0), stop=False, skip_group_check=True)
                            for i in range(2):
                                h = 2 * j + i
                                for r in range(2):
                                    i_ = mm(y[64 * i:64 * i + 64],
                                            V3[:, b, hg * HP + h, 1 - r:3 - r, :].rearrange("p r e -> p (r e)"),
                                            score[:, b, h, r, :], start=False, stop=(r == 1), skip_group_check=True)
                        i_.then_inc(*up(y_mm))
                    pe.wait_ge(*at(k_ready, 14 * (hg + 1)))
                    for b in range(B):
                        for r in range(2):
                            i_ = pe.transpose(bank[b][:, r * P:(r + 1) * P], K2[:, r, b, :], ident)
                        i_.then_inc(*up(kt_mm))
                    if hg:
                        pe.wait_ge(*at(state_ok, hg))
                    for b in range(B):
                        pe.wait_ge(*at(kt_ok, hg * B + b + 1))
                        for h in range(HP):
                            for r in range(2):
                                i_ = mm(bank[7][32 * h:32 * h + 32, 64 * b:64 * b + 64], KT[:, b, r, 32 * h:32 * h + 32],
                                        V3[:, b, hg * HP + h, 1 - r:3 - r, :].rearrange("p r e -> p (r e)"),
                                        start=(r == 0), stop=(r == 1))
                    i_.then_inc(*up(r_mm))
                pe.wait_ge(*at(y2_ok, 4))
                for k in range(KC):
                    channels(bank[k][:, :], w_y, slice(k * P, (k + 1) * P), y2T, 4).then_inc(*up(y3_mm))
                pe.wait_ge(*at(y3_ok, KC))
                tokens((2, 3), uT, w_out)

                layer_norm(3)
                for b in range(B):
                    for k in range(KC):
                        mm(bank[7][:, b * E1:(b + 1) * E1], hT[:, k, b, :], w_emb[:, k, :],
                           start=(k == 0), stop=(k == KC - 1))
                pe.wait_ge(*at(hsq_ok, 1))
                for b in range(B):
                    for k in range(KC):
                        i_ = mm(bank[7][:, 32 + b:33 + b], sqh[:, k, b, :], const("ones")[:, 0:1],
                                start=(k == 0), stop=(k == KC - 1))
                i_.then_inc(*up(router))

                def hidden(e):
                    n = len(GROUPS0) + 2 * e
                    pe.wait_ge(*at(ring_in[n % SLOTS], 16 * (n // SLOTS + 1)))
                    w1 = ring[:, n % SLOTS, 0:2048].rearrange("p (k c) -> p k c", k=KC)
                    for t in range(HT1):
                        if e or t >= 4:
                            pe.wait_ge(*at(hid1_ok, e * HT1 + t - 3))
                        channels(bank[t % 4][:, :], w1, slice(t * P, (t + 1) * P), hT).then_inc(*up(h1_mm))

                hidden(0)
                pe.wait_ge(*at(comb1_ok, 1))
                turn_weights(1, rt[:, 10], E1)
                pe.wait_ge(*at(comb1_copied, 1))
                for j in range(2):
                    for i in range(2):
                        i_ = mm(bank[6 + j][:, i * D:(i + 1) * D], combT1[:, 2 * j + i, :], b2[:, :],
                                start=True, stop=True)
                    i_.then_inc(*up(down_bias))
                for e in range(E1):
                    if e + 1 < E1:
                        hidden(e + 1)
                    n = len(GROUPS0) + 2 * e + 1
                    pe.wait_ge(*at(ring_in[n % SLOTS], 16 * (n // SLOTS + 1)))
                    pe.wait_ge(*at(hid1_ok, HT1 * (e + 1)))
                    w2 = ring[:, n % SLOTS, 0:2048].rearrange("p (t c) -> p t c", t=HT1)
                    for j in range(2):
                        if e:
                            pe.wait_ge(*at(acc_ok, 2 * (e - 1) + j + 1))
                        for i in range(2):
                            for t in range(HT1):
                                i_ = mm(bank[4 + 2 * (e % 2) + j][:, i * D:(i + 1) * D], hid1[:, e % 2, t, 2 * j + i, :],
                                        w2[:, t, :], start=(t == 0), stop=(t == HT1 - 1))
                        i_.then_inc(*up(down_mm))
                pe.wait_ge(*at(down_mm, down_mm.count))
                top_up(pe, [ln_tr, proj, nrm, res, router, comb_tr, gate_mm, up_mm, slot_used, u_mm, plane_mm, v_mm,
                            diag_mm, scored, y_mm, kt_mm, r_mm, y3_mm, h1_mm, down_mm, down_bias])
                pe.sem_inc(started.handle, 1)


INPUTS = {"x": (B, L, D), "w_qkv": (P, KC, 3 * D), "w_beta": (P, KC, H0), "w_o": (P, KC, D),
          "w_router": (P, KC, E0), "w_in": (P, KC, D), "w_qka": (P, KC, 12, P), "w_v": (P, KC, 512),
          "w_y": (P, 4, D), "w_out": (P, KC, D), "w_emb": (P, KC, E1), "b2": (E1, D), "cols": (P, NCOLS),
          "consts": (P, NCONST), "rows": (NROWS,), "c_cols": (P, 2, KC, B), "wmod": (2, P, KC, 1536),
          "w_ffn0": (P, 768 * TILES0), "w_ffn1": (2 * E1, P, 2048)}


def constants():
    t = np.zeros((P, NCONST), np.float32)

    def put(name, v):
        a, n = CONSTS[name]
        t[:v.shape[0], a:a + n] = v

    p = np.arange(P)
    put("ident", np.eye(P))
    put("ones16", (p[:, None] // HD0 == p[None] // HD0) * 1.0)
    put("ones", np.ones((P, P)))
    put("head_of", (p[:, None] // HD1 == np.arange(HP)[None]) * 1.0)
    put("rev16", np.tile(16.0 - np.arange(16), (P, 1)))
    put("rev8", np.tile(8.0 - np.arange(8), (P, 1)))
    put("up8", np.tile(1.0 + np.arange(8), (P, 1)))
    masks = []
    for lev in range(LEVELS):
        m = 1 << lev
        j = np.arange(64)
        block = j // m
        masks.append((p[:, None] // (2 * m) == block[None]) & (p[:, None] % (2 * m) < m))
    put("masks", np.concatenate(masks, 1) * 1.0)
    sel = (np.arange(E0)[:, None, None] == 2 * np.arange(ROUTED0)[None, :, None] + p[None, None] // MID0) * 1.0
    put("sel", sel.reshape(E0, -1))
    return t


def kernel(**inputs):
    import concourse.bacc as bacc
    from concourse.bass_utils import run_bass_kernel_spmd

    a = {k: np.asarray(v) for k, v in inputs.items()}

    def chunks(w):
        return w.reshape(-1, P, w.shape[-1]).transpose(1, 0, 2)

    def column(v):
        return v.reshape(-1, P).T

    def planes(w):
        v = w.reshape(HG, P, 4, 2, *w.shape[1:])
        return np.stack([v[g, :, c, r] for g in range(HG) for c in (0, 1, 3) for r in range(2)])

    w_qkva, b_qkva = a["L1_attn_W_qkva"], a["L1_attn_b_qkva"]
    values = w_qkva.reshape(H1, HD1, 4, 2, D)[:, :, 2].transpose(0, 2, 1, 3).reshape(512, D)
    b_values = b_qkva.reshape(H1, HD1, 4, 2)[:, :, 2].transpose(0, 2, 1).reshape(512)
    w_y = a["L1_attn_W_y"].reshape(D, H1, HD1, 2).transpose(1, 3, 2, 0).reshape(512, D)
    conv = [a[f"L0_attn_w{z}_conv"].reshape(KC, P, TAPS).transpose(1, 0, 2).reshape(P, -1) for z in "kqv"]
    cols_ = [column(a[f"L0_attn_b{z}"]) for z in "kqv"] + [column(a[f"L0_attn_b{z}_conv"]) for z in "kqv"] + conv
    bbeta = np.zeros((P, 1), np.float32)
    bbeta[:H0, 0] = a["L0_attn_bbeta"]
    cols_ += [np.tile(a["L0_attn_norm_w"], P // HD0)[:, None], bbeta, column(a["L1_attn_b_in"]),
              planes(b_qkva).T, column(a["L1_attn_b_y"]), column(a["L1_ffn_b1"].reshape(-1))]
    h0 = np.stack([a["L1_attn_h0_re"], a["L1_attn_h0_im"]], 2).reshape(HG, P, 2, HD1).transpose(1, 0, 2, 3)

    def hidden_columns(shared, routed):
        both = [w.transpose(1, 0, 2).reshape(D, -1) for w in (routed, shared)]
        return np.concatenate(both, 1)

    gate = chunks(hidden_columns(a["L0_ffn_wg_s"], a["L0_ffn_wg_r"]))
    up_ = chunks(hidden_columns(a["L0_ffn_wu_s"], a["L0_ffn_wu_r"]))
    down = chunks(np.concatenate([a["L0_ffn_wd_r"].reshape(-1, D), a["L0_ffn_wd_s"].reshape(-1, D)]))
    ffn0 = []
    for s, e in GROUPS0:
        ffn0 += [gate[:, :, s * P:e * P].reshape(P, -1), up_[:, :, s * P:e * P].reshape(P, -1),
                 down[:, s:e].reshape(P, -1)]
    ffn1 = []
    for e in range(E1):
        ffn1 += [chunks(a["L1_ffn_W1"][e]).reshape(P, -1), chunks(a["L1_ffn_W2"][e]).reshape(P, -1)]
    arrays = {
        "x": a["L0_attn_x"],
        "w_qkv": chunks(np.concatenate([a[f"L0_attn_W{z}"].T for z in "kqv"], 1)),
        "w_beta": chunks(a["L0_attn_Wbeta"].T), "w_o": chunks(a["L0_attn_Wo"].T),
        "w_router": chunks(a["L0_ffn_router_w"]), "w_in": chunks(a["L1_attn_W_in"].T),
        "w_qka": chunks(planes(w_qkva).reshape(12 * P, D).T).reshape(P, KC, 12, P),
        "w_v": chunks(values.T), "w_y": chunks(w_y), "w_out": chunks(a["L1_attn_W_out"].T),
        "w_emb": chunks(a["L1_ffn_uzman_embeddings"].T), "b2": a["L1_ffn_b2"],
        "cols": np.concatenate(cols_, 1), "consts": constants(),
        "rows": np.concatenate([a["L0_attn_bo"], a["L1_attn_b_out"], b_values, a["L1_ffn_onbellek_durumu"]]),
        "c_cols": np.stack([a["L0_c"].T.reshape(KC, P, B), a["L1_c"].T.reshape(KC, P, B)]).transpose(2, 0, 1, 3),
        "wmod": np.stack([chunks(a["L0_wmod"]), chunks(a["L1_wmod"])]),
        "w_ffn0": np.concatenate(ffn0, 1), "w_ffn1": np.stack(ffn1), "h0": h0,
    }
    arrays = {k: np.ascontiguousarray(v) for k, v in arrays.items()}
    for k, shape in INPUTS.items():
        assert arrays[k].shape == shape, (k, arrays[k].shape, shape)
    nc = bacc.Bacc("TRN2", target_bir_lowering=False, num_devices=1)
    ins = {k: nc.dram_tensor(f"in_{k}", v.shape, mybir.dt.from_np(v.dtype), kind="ExternalInput").ap()
           for k, v in arrays.items()}
    out = nc.dram_tensor("out_x", (B, L, D), F32, kind="ExternalOutput").ap()
    nc.disable_value_cache = True
    build(nc, ins, out)
    r = run_bass_kernel_spmd(nc, [{f"in_{k}": v for k, v in arrays.items()}], core_ids=[0])
    return r.results[0]["out_x"]
```

```python
from contextlib import ExitStack

import numpy as np

import concourse.bass as bass
from concourse import mybir

F32 = mybir.dt.float32
I32 = mybir.dt.int32
ALU = mybir.AluOpType
ACT = mybir.ActivationFunctionType
AX = mybir.AxisListType

P = 128
B, L, D = 4, 1024, 256
KC = D // P
SEG = 128
NSEG = L // SEG
NT = B * SEG
H0, HD0, TAPS = 16, 16, 4
PAST = TAPS - 1
EV = HD0 // 2
E0, MID0, SHARED0 = 16, 64, 256
TILES0 = (E0 * MID0 + SHARED0) // P
ROUTED0 = E0 * MID0 // P
DOWN0 = [(0, 4), (4, 8), (8, 10)]
H1, HD1 = 8, 32
HG = 2
HP = 4
LEVELS = 7
E1, MID1 = 8, 1024
HT1 = MID1 // P

SLOT = 1024
SLOTS = 5
UP0_AT, DOWN0_AT = 0, TILES0 // 2
V_AT = DOWN0_AT + len(DOWN0)
QKA_AT = V_AT + 1
Y_AT = QKA_AT + 3
EXPERT_AT = Y_AT + 1


def expert_order():
    order = [(0, 0)]
    for e in range(E1):
        order += [(0, e + 1)] * (e + 1 < E1) + [(1, e)]
    return order


EXPERT_LOADS = [(w, e, half) for w, e in expert_order() for half in range(2)]
LOADS = EXPERT_AT + len(EXPERT_LOADS)
assert LOADS % SLOTS == 0
SCAN_TILE, SCAN_EXPERT = 2, 13
STRIDE = 4096

COLS = {}


def column_layout():
    at = 0
    for name, n in (("bqkv", 6), ("bqkv_conv", 6), ("w_conv", 24), ("norm_w", 1), ("bbeta", 1),
                    ("b_in", 2), ("b_qka", 12), ("b_y", 2), ("b1", E1 * HT1)):
        COLS[name] = (at, n)
        at += n
    return at


NCOLS = column_layout()
CONSTS = {}


def const_layout():
    at = 0
    for name, n in (("ident", P), ("ones16", P), ("ones", P), ("head_of", HP), ("rev16", 16), ("rev8", 8),
                    ("up8", 8), ("masks", LEVELS * 64), ("sel", ROUTED0 * P)):
        CONSTS[name] = (at, n)
        at += n
    return at


NCONST = const_layout()
ROWS = {"bo": (0, D), "b_out": (D, D), "b_v": (2 * D, 512), "cache": (2 * D + 512, E1)}
NROWS = 2 * D + 512 + E1


class Signal:

    def __init__(self, handle, stride):
        self.handle, self.stride, self.count = handle, stride, 0


def build(nc, ins, out):
    with ExitStack() as ctx:
        def sb(name, shape, dt=F32):
            return ctx.enter_context(nc.sbuf_tensor(name, shape, dt))

        w_qkv = sb("w_qkv", [P, KC, 3 * D])
        w_beta = sb("w_beta", [P, KC, H0])
        w_o = sb("w_o", [P, KC, D])
        w_router = sb("w_router", [P, KC, E0])
        w_in = sb("w_in", [P, KC, D])
        w_out = sb("w_out", [P, KC, D])
        w_emb = sb("w_emb", [P, KC, E1])
        b2 = sb("b2", [E1, D])
        cols = sb("cols", [P, NCOLS])
        consts = sb("consts", [P, NCONST])
        rows = sb("rows", [P, NROWS])
        ring = sb("ring", [P, SLOTS, SLOT])
        c_cols = sb("c_cols", [P, 2, KC, B])
        silu_c = sb("silu_c", [P, 2, KC, B])
        shift_scale = sb("shift_scale", [P, 2, 4, KC, B])
        gates = sb("gates", [P, 2, 2, B, D])
        emb_rnorm = sb("emb_rnorm", [P, E1])

        def col(name, i=0):
            return cols[:, COLS[name][0] + i:COLS[name][0] + i + 1]

        def const(name):
            a, n = CONSTS[name]
            return consts[:, a:a + n]

        def row(name):
            a, n = ROWS[name]
            return rows[:, a:a + n]

        ident = const("ident")
        masks = const("masks").bitcast(I32).rearrange("p (l j) -> p l j", l=LEVELS)
        sel = const("sel")[0:E0].rearrange("p (c j) -> p c j", c=ROUTED0)

        X = sb("X", [P, B, D])
        xn = sb("xn", [P, B, D])
        hT = sb("hT", [P, KC, B, SEG])
        ln_stats = sb("ln_stats", [P, B, 6])
        ln_mv = sb("ln_mv", [P, B, 2])
        ln_var = sb("ln_var", [P, B])
        ln_std = sb("ln_std", [P, B])
        ln_rstd = sb("ln_rstd", [P, B])
        past = sb("past", [P, 6, B, PAST])
        S0 = sb("S0", [P, EV, HD0])
        H3 = sb("H3", [P, HG, B, 3, HD1])
        KQ = sb("KQ", [P, 2, HD0, SEG])
        V0 = sb("V0", [P, EV, SEG])
        beta_scan = sb("beta_scan", [P, SEG])
        nbeta = sb("nbeta", [P, SEG])
        KQ_S = sb("KQ_S", [P, SEG, 2, EV])
        delta = sb("delta", [P, SEG, EV])
        prod = sb("prod", [P, 2, EV, HD0])
        outer = sb("outer", [P, EV, HD0])
        arena = sb("arena", [P, 24096])

        def carve(offset, shape):
            n = int(np.prod(shape[1:]))
            flat = arena[0:shape[0], offset:offset + n]
            assert offset + n <= 24096, (offset, n)
            names = "abcdef"[:len(shape) - 1]
            view = flat if len(shape) == 2 else flat.rearrange(
                f"p ({' '.join(names)}) -> p {' '.join(names)}",
                **{k: v for k, v in zip(names, shape[1:])})
            return view, offset + n

        o = 0
        PX, o = carve(o, [P, KC, B, PAST + SEG])
        kqv, o = carve(o, [P, 3, KC, B, SEG])
        sq, o = carve(o, [P, KC, B, SEG])
        rn, o = carve(o, [P, KC, B, SEG])
        tmp_dot, o = carve(o, [P, HD0, SEG])
        qk_dot, o = carve(o, [P, SEG])
        O0, o = carve(o, [P, EV, SEG])
        betaT, o = carve(o, [H0, B, SEG])
        oT, o = carve(o, [P, KC, B, SEG])
        osq, o = carve(o, [P, KC, B, SEG])
        orn, o = carve(o, [P, KC, B, SEG])
        X_next, o = carve(o, [P, B, D])
        o = 0
        hid0, o = carve(o, [P, TILES0, B, SEG])
        sg0, o = carve(o, [P, 2, B, SEG])
        combT, o = carve(o, [E0, B, SEG])
        lg, o = carve(o, [P, 12, B, E0])
        sm, o = carve(o, [P, 16, B])
        o = 0
        V3, o = carve(o, [P, B, H1, 3, HD1])
        y2T, o = carve(o, [P, 4, B, SEG])
        uT, o = carve(o, [P, KC, B, SEG])
        Q3, o = carve(o, [P, 3, B, SEG])
        K2, o = carve(o, [P, 2, B, SEG])
        TT, o = carve(o, [P, 2, 1024])
        t1, o = carve(o, [P, 2, NT])
        t2, o = carve(o, [P, 2, NT])
        u1, o = carve(o, [P, 2, NT // 2])
        u2, o = carve(o, [P, 2, NT // 2])
        Kx, o = carve(o, [P, 2, HP, B, SEG])
        score, o = carve(o, [P, B, HP, 2, SEG])
        Hx, o = carve(o, [P, B, 2, HP, 2 * HD1])
        diag, o = carve(o, [P, B, HP, 2])
        KT = t2.rearrange("p r (b c) -> p (r b) c", c=2 * P).rearrange("p b (r c) -> p b r c", r=2)
        o = 0
        hid1, o = carve(o, [P, 2, HT1, B, SEG])
        acc, o = carve(o, [P, B, D])
        combT1, o = carve(o, [E1, B, SEG])
        sqh, o = carve(o, [P, KC, B, SEG])
        rt, o = carve(o, [P, 16, B, E1])
        rs, o = carve(o, [P, 24, B])

        bank = [ctx.enter_context(nc.psum_tensor(f"bank{i}", [P, 512], F32)) for i in range(8)]

        signals = []

        def signal(name, stride=STRIDE):
            s = Signal(ctx.enter_context(nc.semaphore(name)), stride)
            signals.append(s)
            return s

        tables_in = signal("tables_in")
        silu_done = signal("silu_done")
        mod_cols = signal("mod_cols")
        mod_rows = signal("mod_rows")
        mod_rows_taken = signal("mod_rows_taken")
        emb_sq = signal("emb_sq")
        emb_sum = signal("emb_sum")
        emb_root = signal("emb_root")
        started = signal("started")
        seg_open = signal("seg_open")
        passed = signal("passed")
        x_in = signal("x_in", 16)
        x_next_in = signal("x_next_in", 16)
        x_out = signal("x_out", 16)
        ring_in = [signal(f"ring_in{i}", 16 * (LOADS // SLOTS)) for i in range(SLOTS)]
        kq_out = signal("kq_out", 16 * 4)
        k_scan = signal("k_scan", 16 * 8)
        q_scan = signal("q_scan", 16 * 8)
        v_scan = signal("v_scan", 16 * 8)
        beta_in = signal("beta_in", 16 * 8)
        o_out = signal("o_out", 16 * 8)
        o_in = signal("o_in", 16)
        dve_step = signal("dve_step")
        ln_var_ok = signal("ln_var_ok")
        xn_ok = signal("xn_ok")
        px_free = signal("px_free")
        k_sq = signal("k_sq")
        conv_v = signal("conv_v")
        k_unit = signal("k_unit")
        q_unit = signal("q_unit")
        v_unit = signal("v_unit")
        o0_ok = signal("o0_ok")
        o_sq = signal("o_sq")
        o_norm_ok = signal("o_norm_ok")
        logit_sub = signal("logit_sub")
        comb_ok = signal("comb_ok")
        comb_copied = signal("comb_copied")
        hid0_ok = signal("hid0_ok")
        res_taken = signal("res_taken")
        x_done = signal("x_done")
        mag_ok = signal("mag_ok")
        k_neg = signal("k_neg")
        v3_ok = signal("v3_ok")
        a_ok = signal("a_ok")
        pairs_ok = signal("pairs_ok")
        diag_ok = signal("diag_ok")
        q_ready = signal("q_ready")
        masked = signal("masked")
        state_ok = signal("state_ok")
        hsq_ok = signal("hsq_ok")
        rt_var = signal("rt_var")
        rt_gap = signal("rt_gap")
        comb1_ok = signal("comb1_ok")
        comb1_copied = signal("comb1_copied")
        acc_ok = signal("acc_ok")
        x_final = signal("x_final")
        ln_tr = signal("ln_tr")
        proj = signal("proj")
        nrm = signal("nrm")
        res = signal("res")
        router = signal("router")
        comb_tr = signal("comb_tr")
        gate_mm = signal("gate_mm")
        up_mm = signal("up_mm")
        down0_used = signal("down0_used")
        u_mm = signal("u_mm")
        plane_mm = signal("plane_mm")
        v_mm = signal("v_mm")
        diag_mm = signal("diag_mm")
        scored = signal("scored")
        y_mm = signal("y_mm")
        kt_mm = signal("kt_mm")
        r_mm = signal("r_mm")
        y3_mm = signal("y3_mm")
        h1_mm = signal("h1_mm")
        down_mm = signal("down_mm")
        down_bias = signal("down_bias")
        act_step = signal("act_step")
        ln_root = signal("ln_root")
        hT_ok = signal("hT_ok")
        px_ok = signal("px_ok")
        beta_ok = signal("beta_ok")
        root = signal("root")
        v_silu = signal("v_silu")
        exp_ok = signal("exp_ok")
        sg_ok = signal("sg_ok")
        u_ok = signal("u_ok")
        plane_ok = signal("plane_ok")
        mag_root = signal("mag_root")
        hx_ok = signal("hx_ok")
        kx_ready = signal("kx_ready")
        y2_ok = signal("y2_ok")
        kt_ok = signal("kt_ok")
        y3_ok = signal("y3_ok")
        rt_root = signal("rt_root")
        rt_exp = signal("rt_exp")
        hid1_ok = signal("hid1_ok")
        pool_step = signal("pool_step")
        zeroed = signal("zeroed")
        score_init = signal("score_init")
        k_ready = signal("k_ready")

        last = {}

        def up(s, who=None):
            s.count += 1
            if who is not None:
                last[who] = s
            return s.handle, 1

        def up16(s):
            s.count += 16
            return s.handle, 16

        def top_up(eng, mine):
            for s in mine:
                assert s.count <= s.stride
                if s.count < s.stride:
                    eng.sem_inc(s.handle, s.stride - s.count)
                s.count = 0

        def turns(eng, turn):
            turn(-1, False, True)
            with eng.Fori(0, NSEG - 1) as seg:
                turn(seg, True, True)
            turn(NSEG - 1, True, False)

        kqv_d = nc.dram_tensor("kqv_d", (3, D, B, SEG), F32, kind="Internal").ap()
        beta_d = nc.dram_tensor("beta_d", (H0, B, SEG), F32, kind="Internal").ap()
        o_d = nc.dram_tensor("o_d", (KC, H0 // KC, 2, EV, B, SEG), F32, kind="Internal").ap()

        x_seg = ins["x"].rearrange("b (s p) d -> s p b d", p=SEG)
        out_seg = out.rearrange("b (s p) d -> s p b d", p=SEG)
        block = ctx.enter_context(nc.Block())

        TABLES = [(w_qkv, "w_qkv"), (w_beta, "w_beta"), (w_o, "w_o"), (w_router, "w_router"), (w_in, "w_in"),
                  (w_out, "w_out"), (w_emb, "w_emb"), (b2, "b2"),
                  (cols, "cols"), (consts, "consts"), (c_cols, "c_cols")]
        wmod = [arena[:, 12288 + i * KC * 1536:12288 + (i + 1) * KC * 1536].rearrange("p (k n) -> p k n", k=KC)
                for i in range(2)]

        @block.sync
        def _(sp):
            for t, name in TABLES:
                sp.dma_start(t[:], ins[name]).then_inc(tables_in.handle, 16)
            sp.dma_start(rows[:, :], ins["rows"].partition_broadcast(P)).then_inc(tables_in.handle, 16)
            for i in range(2):
                sp.dma_start(wmod[i], ins["wmod"][i]).then_inc(tables_in.handle, 16)
            for g in range(HG):
                for b in range(B):
                    sp.dma_start(H3[:, g, b, 1:3], ins["h0"][:, g]).then_inc(tables_in.handle, 16)

            def turn(seg, rest, nxt):
                def at(s, k):
                    return s.handle, (seg + 1) * s.stride + k

                sp.wait_ge(started.handle, (seg + 1) * 4 + 4)
                sp.sem_inc(seg_open.handle, 1)
                if nxt:
                    src = x_seg[bass.ds(seg + 1, 1)] if rest else x_seg[0:1]
                    sp.dma_start(X_next, src.rearrange("a p b d -> (a p) b d")).then_inc(*up16(x_next_in))

                def load(n):
                    if n >= SLOTS:
                        was = n - SLOTS
                        if was < DOWN0_AT:
                            free = at(up_mm, 2 * was + 2)
                        elif was < V_AT:
                            d = was - DOWN0_AT
                            free = at(down0_used, d + 1) if d + 1 < len(DOWN0) else at(res, 4)
                        elif was < QKA_AT:
                            free = at(v_mm, B)
                        elif was < Y_AT:
                            free = at(plane_mm, 4 * (was - QKA_AT + 1))
                        elif was < EXPERT_AT:
                            free = at(y3_mm, KC)
                        else:
                            w, e, half = EXPERT_LOADS[was - EXPERT_AT]
                            free = at(down_mm, 2 * e + 2) if w else at(h1_mm, HT1 * e + 4 * half + 4)
                        sp.wait_ge(*free)
                    sp.dma_start(ring[:, n % SLOTS, :], ins["w_ring"][n]).then_inc(*up16(ring_in[n % SLOTS]))

                if rest:
                    here = x_seg[bass.ds(seg, 1)] if nxt else x_seg[NSEG - 1:NSEG]
                    sp.dma_start(X[:, :, :], here.rearrange("a p b d -> (a p) b d")).then_inc(*up16(x_in))
                    for n in range(SLOTS):
                        load(n)
                    sp.wait_ge(*at(o0_ok, 1))
                    for half in range(2):
                        for b in range(B):
                            p0 = half * 64 + b * H0
                            dst = o_d.rearrange("k h g e b t -> g b (k h) e t")[half, b]
                            sp.dma_start(dst, O0[p0:p0 + H0]).then_inc(*up16(o_out))
                    sp.wait_ge(*at(o_out, o_out.stride))
                    sp.dma_start(oT, o_d.rearrange("k h g e b t -> (h g e) k b t")).then_inc(*up16(o_in))
                if nxt:
                    sp.wait_ge(*at(beta_ok, 1))
                    sp.dma_start(beta_d, betaT[:, :, :]).then_inc(*up16(kq_out))
                    sp.wait_ge(*at(kq_out, 16))
                    for half in range(2):
                        for b in range(B):
                            p0 = half * 64 + b * H0
                            sp.dma_start(beta_scan[p0:p0 + H0, :], beta_d.rearrange("h b t -> b h t")[b])\
                                .then_inc(*up16(beta_in))
                    for z, (ready, sem) in enumerate(((k_unit, k_scan), (q_unit, q_scan), (v_unit, v_scan))):
                        sp.wait_ge(*at(ready, KC))
                        sp.dma_start(kqv_d[z].rearrange("(k p) b t -> p k b t", p=P), kqv[:, z]).then_inc(*up16(kq_out))
                        sp.wait_ge(*at(kq_out, kq_out.count))
                        for half in range(2):
                            for b in range(B):
                                p0 = half * 64 + b * H0
                                if z < 2:
                                    src = kqv_d[z].rearrange("(h d) b t -> b h d t", h=H0)[b]
                                    sp.dma_start(KQ[p0:p0 + H0, z], src).then_inc(*up16(sem))
                                else:
                                    src = kqv_d[z].rearrange("(h g e) b t -> g b h e t", h=H0, g=2)[half, b]
                                    sp.dma_start(V0[p0:p0 + H0], src).then_inc(*up16(sem))
                if rest:
                    for n in range(SLOTS, LOADS):
                        load(n)
                    sp.wait_ge(*at(x_final, 1))
                    there = out_seg[bass.ds(seg, 1)] if nxt else out_seg[NSEG - 1:NSEG]
                    sp.dma_start(there.rearrange("a p b d -> (a p) b d"), X[:, :, :]).then_inc(*up16(x_out))
                    sp.wait_ge(*at(x_out, 16))
                sp.sem_inc(passed.handle, 1)
                top_up(sp, [x_in, x_next_in, x_out, kq_out, k_scan, q_scan, v_scan, beta_in, o_out, o_in, *ring_in])

            turns(sp, turn)

        @block.scalar
        def _(act):
            me = "act"

            NTAB = 16 * (len(TABLES) + 3 + HG * B)
            act.wait_ge(tables_in.handle, NTAB)
            act.activation(silu_c[:, :, :, :].rearrange("p a k b -> p (a k b)"),
                           c_cols[:, :, :, :].rearrange("p a k b -> p (a k b)"), ACT.Silu).then_inc(silu_done.handle, 1)
            act.wait_ge(emb_sum.handle, 1)
            act.activation(emb_rnorm[:, :], bank[1][:, 0:E1], ACT.Sqrt).then_inc(emb_root.handle, 1)
            act.wait_ge(emb_root.handle, 1)
            act.sem_inc(started.handle, 1)

            def turn(seg, rest, nxt):
                def at(s, k):
                    return s.handle, (seg + 1) * s.stride + k

                def settle():
                    s = last[me]
                    act.wait_ge(s.handle, (seg + 1) * s.stride + s.count)

                act.wait_ge(seg_open.handle, seg + 2)

                def layer_norm(n, blk, which):
                    act.wait_ge(*at(ln_var_ok, n + 1))
                    act.activation(ln_std[:, :], ln_var[:, :], ACT.Sqrt).then_inc(*up(ln_root, me))
                    act.wait_ge(*at(ln_tr, n + 1))
                    for k in range(KC):
                        for b in range(B):
                            ins_ = act.activation(hT[:, k, b, :], bank[k][:, b * SEG:(b + 1) * SEG], ACT.Identity,
                                                  bias=shift_scale[:, blk, which, k, b:b + 1],
                                                  scale=shift_scale[:, blk, which + 1, k, b:b + 1])
                    ins_.then_inc(*up(hT_ok, me))

                done = KC if rest else 0
                if rest:
                    for k in range(KC):
                        act.wait_ge(*at(o_sq, KC + k + 1))
                        act.activation(orn[:, k], osq[:, k], ACT.Sqrt).then_inc(*up(root, me))

                if nxt:
                    layer_norm(0, 0, 0)
                    for z in range(3):
                        for k in range(KC):
                            n = z * KC + k
                            act.wait_ge(*at(proj, n + 1))
                            if z:
                                act.wait_ge(*at(px_free, (z - 1) * KC + k + 1))
                            act.activation(PX[:, k, :, PAST:], bank[2 + n % 2][:, :].rearrange("p (b t) -> p b t", b=B),
                                           ACT.Identity, bias=col("bqkv", n)).then_inc(*up(px_ok, me))
                    act.wait_ge(*at(proj, 7))
                    act.activation(betaT[:, :, :].rearrange("p b t -> p (b t)"), bank[4][0:H0, :], ACT.Sigmoid,
                                   bias=col("bbeta")[0:H0]).then_inc(*up(beta_ok, me))
                    for n in range(4):
                        act.wait_ge(*at(nrm, done + n + 1))
                        if n >= 2:
                            act.wait_ge(*at(v_unit, n - 1))
                        act.activation(rn[:, n % 2].rearrange("p b t -> p (b t)"), bank[5 + n % 2][:, :], ACT.Sqrt)\
                            .then_inc(*up(root, me))
                        if n < 2:
                            act.wait_ge(*at(conv_v, n + 1))
                            act.activation(kqv[:, 2, n], kqv[:, 2, n], ACT.Silu).then_inc(*up(v_silu, me))
                if rest:
                    layer_norm(nxt, 0, 2)
                    act.wait_ge(*at(logit_sub, 1))
                    act.activation(lg[:, 1], lg[:, 0], ACT.Exp).then_inc(*up(exp_ok, me))
                    for i in range(TILES0):
                        act.wait_ge(*at(gate_mm, i + 1))
                        if i >= 2:
                            act.wait_ge(*at(hid0_ok, i - 1))
                        act.activation(sg0[:, i % 2].rearrange("p b t -> p (b t)"), bank[3 * (i % 2)][:, :], ACT.Silu)\
                            .then_inc(*up(sg_ok, me))

                    layer_norm(nxt + 1, 1, 0)
                    for k in range(KC):
                        act.wait_ge(*at(u_mm, k + 1))
                        act.activation(uT[:, k].rearrange("p b t -> p (b t)"), bank[2 + k][:, :], ACT.Silu,
                                       bias=col("b_in", k)).then_inc(*up(u_ok, me))
                    for hg in range(HG):
                        for c in range(6):
                            n = hg * 6 + c
                            act.wait_ge(*at(plane_mm, n + 1))
                            dst = (Q3[:, 1], Q3[:, 2], K2[:, 0], K2[:, 1])[c].rearrange("p b t -> p (b t)") if c < 4 \
                                else TT[:, c - 4, 0:NT]
                            if hg and c == 0:
                                act.wait_ge(*at(y_mm, 2 * hg))
                            if hg and c == 2:
                                act.wait_ge(*at(kt_mm, B * hg))
                            if hg and c == 4:
                                act.wait_ge(*at(state_ok, hg))
                            act.activation(dst, bank[n % 4][:, :], ACT.Identity, bias=col("b_qka", n))\
                                .then_inc(*up(plane_ok, me))
                        act.wait_ge(*at(mag_ok, hg + 1))
                        act.activation(t2[:, 0], t1[:, 0], ACT.Sqrt).then_inc(*up(mag_root, me))
                        act.wait_ge(*at(zeroed, 2))
                        for h in range(HP):
                            for r in range(2):
                                act.activation(Hx[32 * h:32 * h + 32, :, r, h],
                                               H3[32 * h:32 * h + 32, hg, :, 1 - r:3 - r].rearrange("p b r e -> p b (r e)"),
                                               ACT.Copy).then_inc(*up(hx_ok, me))
                        for lev in range(LEVELS):
                            m = 1 << lev
                            for bp in range(2):
                                u = (hg * LEVELS + lev) * 2 + bp
                                if lev:
                                    act.wait_ge(*at(k_ready, u - 1))
                                if u >= 2:
                                    act.wait_ge(*at(scored, 2 * (u - 1)))
                                for r in range(2):
                                    for h in range(HP):
                                        src = K2[32 * h:32 * h + 32, r, 2 * bp:2 * bp + 2]
                                        dst = Kx[32 * h:32 * h + 32, r, h, 2 * bp:2 * bp + 2]
                                        if lev:
                                            half = "p b (n two m) -> p (b n) two m"
                                            src = src.rearrange(half, two=2, m=m // 2)[:, :, 0]
                                            dst = dst.rearrange(half, two=2, m=m // 2)[:, :, 0]
                                        ins_ = act.activation(dst, src, ACT.Copy)
                                ins_.then_inc(*up(kx_ready, me))
                        for j in range(2):
                            act.wait_ge(*at(y_mm, 2 * hg + j + 1))
                            act.activation(y2T[:, 2 * hg + j].rearrange("p b t -> p (b t)"), bank[4 + j][:, :], ACT.Copy)\
                                .then_inc(*up(y2_ok, me))
                        for b in range(B):
                            act.wait_ge(*at(kt_mm, hg * B + b + 1))
                            act.activation(KT[:, b].rearrange("p r c -> p (r c)"), bank[b][:, 0:2 * P], ACT.Copy)\
                                .then_inc(*up(kt_ok, me))
                    for k in range(KC):
                        act.wait_ge(*at(y3_mm, k + 1))
                        act.activation(uT[:, k].rearrange("p b t -> p (b t)"), bank[k][:, :], ACT.Silu,
                                       bias=col("b_y", k)).then_inc(*up(y3_ok, me))

                    layer_norm(nxt + 2, 1, 2)
                    act.wait_ge(*at(rt_var, 1))
                    act.activation(rs[:, 1], rs[:, 0], ACT.Sqrt).then_inc(*up(rt_root, me))
                    act.wait_ge(*at(rt_gap, 1))
                    act.activation(rs[:, 11], rs[:, 10], ACT.Exp).then_inc(*up(rt_exp, me))
                    for e in range(E1):
                        for t in range(HT1):
                            n = e * HT1 + t
                            act.wait_ge(*at(h1_mm, n + 1))
                            if e >= 2:
                                act.wait_ge(*at(down_mm, 2 * (e - 1)))
                            act.activation(hid1[:, e % 2, t].rearrange("p b t -> p (b t)"), bank[n % 4][:, :], ACT.Gelu,
                                           bias=col("b1", n)).then_inc(*up(hid1_ok, me))
                settle()
                top_up(act, [ln_root, hT_ok, px_ok, beta_ok, root, v_silu, exp_ok, sg_ok, u_ok, plane_ok, mag_root,
                             hx_ok, kx_ready, y2_ok, kt_ok, y3_ok, rt_root, rt_exp, hid1_ok])
                act.sem_inc(started.handle, 1)

            turns(act, turn)

        @block.vector
        def _(dve):
            me = "dve"

            NTAB = 16 * (len(TABLES) + 3 + HG * B)
            steps = [0]

            def once(ins_):
                steps[0] += 1
                ins_.then_inc(mod_rows_taken.handle, 1)
                dve.wait_ge(mod_rows_taken.handle, steps[0])

            once(dve.memset(past[:, :, :, :], 0.0))
            once(dve.memset(S0[:, :, :], 0.0))
            dve.wait_ge(tables_in.handle, NTAB)
            once(dve.tensor_scalar(H3[:, :, :, 0].rearrange("p g b e -> p (g b) e"),
                                   H3[:, :, :, 2].rearrange("p g b e -> p (g b) e"), -1.0, None, ALU.mult))
            esq = arena[:, 4096:4096 + KC * E1].rearrange("p (k e) -> p k e", k=KC)
            dve.tensor_tensor(esq, w_emb[:, :, :], w_emb[:, :, :], ALU.mult).then_inc(emb_sq.handle, 1)
            dve.wait_ge(silu_done.handle, 1)
            c_wide = arena[:, 0:2 * KC * B * P].rearrange("p (a j) -> p a j", j=P)
            once(dve.memset(c_wide, 1.0))
            dve.tensor_tensor(c_wide, c_wide, silu_c[:, :, :, :].rearrange("p a k b -> p (a k b)").unsqueeze(2)
                              .to_broadcast([P, 2 * KC * B, P]), ALU.mult).then_inc(emb_sq.handle, 1)
            dve.wait_ge(mod_cols.handle, 1)
            once(dve.tensor_copy(shift_scale[:, :, :, :, :].rearrange("p a w k b -> p (a w k b)"), bank[0][:, 0:64]))
            for blk in range(2):
                for w in (1, 3):
                    v = shift_scale[:, blk, w].rearrange("p k b -> p (k b)")
                    once(dve.tensor_scalar(v, v, 1.0, None, ALU.add))
            dve.wait_ge(emb_root.handle, 1)
            once(dve.tensor_scalar(emb_rnorm[:, :], emb_rnorm[:, :], 1e-8, None, ALU.add))
            once(dve.reciprocal(emb_rnorm[:, :], emb_rnorm[:, :]))
            dve.sem_inc(mod_cols.handle, 1)
            half_t = arena[:, 8192:8192 + 512]
            for i in range(8):
                g = gates[:, i // 4, (i // 2) % 2, 2 * (i % 2):2 * (i % 2) + 2].rearrange("p b d -> p (b d)")
                dve.wait_ge(mod_rows.handle, i + 1)
                once(dve.tensor_scalar(half_t, bank[i][:, :], 0.0, 2.0, ALU.is_ge, ALU.mult))
                once(dve.tensor_scalar(g, bank[i][:, :], -1.0, 0.25, ALU.mult, ALU.max))
                once(dve.tensor_tensor(g, g, bank[i][:, :], ALU.max))
                once(dve.scalar_tensor_tensor(g, half_t, -1.0, g, ALU.add, ALU.mult))
            dve.sem_inc(started.handle, 1)


            def turn(seg, rest, nxt):
                def at(s, k):
                    return s.handle, (seg + 1) * s.stride + k

                def settle():
                    s = last[me]
                    dve.wait_ge(s.handle, (seg + 1) * s.stride + s.count)

                def step(ins_):
                    ins_.then_inc(*up(dve_step, me))
                    settle()

                def layer_norm(n, rows_=X):
                    if rows_ is not X:
                        dve.wait_ge(*at(x_next_in, 16))
                    elif last:
                        settle()
                    for b in range(B):
                        ins_ = dve.bn_stats(ln_stats[:, b, :], rows_[:, b, :])
                    step(ins_)
                    dve.sem_inc(passed.handle, 1)
                    for b in range(B):
                        ins_ = dve.bn_aggr(ln_mv[:, b, :], ln_stats[:, b, :])
                    step(ins_)
                    dve.tensor_scalar(ln_var[:, :], ln_mv[:, :, 1], 1e-5, None, ALU.add).then_inc(*up(ln_var_ok, me))
                    dve.wait_ge(*at(ln_root, n + 1))
                    step(dve.reciprocal(ln_rstd[:, :], ln_std[:, :]))
                    for b in range(B):
                        ins_ = dve.tensor_scalar(xn[:, b, :], rows_[:, b, :], ln_mv[:, b, 0:1], ln_rstd[:, b:b + 1],
                                                 ALU.subtract, ALU.mult)
                    ins_.then_inc(*up(xn_ok, me))

                def residual(n, banks, blk, which, bias):
                    for j in range(2):
                        two = slice(2 * j, 2 * j + 2)
                        dve.wait_ge(*at(res, 2 * n + j + 1))
                        y = bank[banks[j]][:, :].rearrange("p (b d) -> p b d", b=2)
                        g = gates[:, blk, which, two]
                        if bias is None:
                            step(dve.tensor_tensor(xn[:, two], y, g, ALU.mult))
                        else:
                            step(dve.tensor_tensor(xn[:, two], y, row(bias).unsqueeze(1).to_broadcast([P, 2, D]),
                                                   ALU.add))
                            step(dve.tensor_tensor(xn[:, two], xn[:, two], g, ALU.mult))
                        dve.tensor_tensor(X[:, two], X[:, two], xn[:, two], ALU.add).then_inc(*up(x_done, me))

                dve.wait_ge(seg_open.handle, seg + 2)

                done = KC if rest else 0
                scanned = [0]

                def scan(n):
                    if not nxt:
                        return
                    settle()
                    if scanned[0] == 0:
                        dve.wait_ge(*at(beta_in, beta_in.stride))
                        dve.wait_ge(*at(v_scan, v_scan.stride))
                        step(dve.tensor_tensor(V0[:, :, :], V0[:, :, :], beta_scan[:, :].unsqueeze(1)
                                               .to_broadcast([P, EV, SEG]), ALU.mult))
                        step(dve.tensor_scalar(nbeta[:, :], beta_scan[:, :], -1.0, None, ALU.mult))
                        dve.wait_ge(*at(k_scan, k_scan.stride))
                        dve.wait_ge(*at(q_scan, q_scan.stride))
                    S_twice = S0[:, :, :].unsqueeze(1).to_broadcast([P, 2, EV, HD0])
                    for t in range(scanned[0], min(scanned[0] + n, SEG)):
                        step(dve.tensor_tensor(prod[:, :, :, :], S_twice, KQ[:, :, :, t].unsqueeze(2)
                                               .to_broadcast([P, 2, EV, HD0]), ALU.mult))
                        step(dve.tensor_reduce(KQ_S[:, t], prod[:, :, :, :], AX.X, ALU.add))
                        step(dve.scalar_tensor_tensor(delta[:, t], KQ_S[:, t, 0], nbeta[:, t:t + 1], V0[:, :, t],
                                                      ALU.mult, ALU.add))
                        step(dve.tensor_tensor(outer[:, :, :], delta[:, t].unsqueeze(2).to_broadcast([P, EV, HD0]),
                                               KQ[:, 0, :, t].unsqueeze(1).to_broadcast([P, EV, HD0]), ALU.mult))
                        step(dve.tensor_tensor(S0[:, :, :], S0[:, :, :], outer[:, :, :], ALU.add))
                        scanned[0] += 1

                if rest:
                    step(dve.tensor_tensor(tmp_dot[:, :, :], KQ[:, 0], KQ[:, 1], ALU.mult))
                    step(dve.tensor_reduce(qk_dot[:, :], tmp_dot[:, :, :].rearrange("p d t -> p t d"), AX.X, ALU.add))
                    step(dve.tensor_tensor(delta[:, :, :], delta[:, :, :], qk_dot[:, :].unsqueeze(2)
                                           .to_broadcast([P, SEG, EV]), ALU.mult))
                    dve.tensor_tensor(O0[:, :, :].rearrange("p e t -> p t e"), KQ_S[:, :, 1], delta[:, :, :], ALU.add)\
                       .then_inc(*up(o0_ok, me))
                    dve.wait_ge(*at(o_in, 16))
                    for k in range(KC):
                        dve.tensor_tensor(osq[:, k], oT[:, k], oT[:, k], ALU.mult).then_inc(*up(o_sq, me))
                    for k in range(KC):
                        dve.wait_ge(*at(nrm, 1 + k))
                        dve.tensor_scalar(osq[:, k].rearrange("p b t -> p (b t)"), bank[5 + k][:, :], 1.0 / HD0, 1e-6,
                                          ALU.mult, ALU.add).then_inc(*up(o_sq, me))
                    for k in range(KC):
                        dve.wait_ge(*at(root, 1 + k))
                        step(dve.reciprocal(orn[:, k], orn[:, k]))
                        dve.scalar_tensor_tensor(oT[:, k], oT[:, k], col("norm_w"), orn[:, k], ALU.mult, ALU.mult)\
                           .then_inc(*up(o_norm_ok, me))
                    dve.wait_ge(*at(x_in, 16))
                    residual(0, (2, 3), 0, 0, "bo")

                if nxt:
                    layer_norm(0, X_next)
                    for z in range(3):
                        for k in range(KC):
                            n = z * KC + k
                            y = kqv[:, z, k]
                            step(dve.tensor_copy(PX[:, k, :, 0:PAST], past[:, n]))
                            dve.wait_ge(*at(px_ok, n + 1))
                            step(dve.tensor_scalar(y, PX[:, k, :, 0:SEG], col("w_conv", 4 * n), col("bqkv_conv", n),
                                                   ALU.mult, ALU.add))
                            for i in range(1, TAPS):
                                step(dve.scalar_tensor_tensor(y, PX[:, k, :, i:i + SEG], col("w_conv", 4 * n + i), y,
                                                              ALU.mult, ALU.add))
                            dve.tensor_copy(past[:, n], PX[:, k, :, SEG:]).then_inc(*up(px_free, me))
                            if z < 2:
                                if z:
                                    dve.wait_ge(*at(nrm, done + k + 1))
                                dve.tensor_tensor(sq[:, k], y, y, ALU.mult).then_inc(*up(k_sq, me))
                            else:
                                settle()
                                dve.sem_inc(*up(conv_v))
                    for z in range(2):
                        for k in range(KC):
                            n = z * KC + k
                            dve.wait_ge(*at(root, done + n + 1))
                            step(dve.tensor_scalar(rn[:, k], rn[:, k], 1e-6, None, ALU.add))
                            step(dve.reciprocal(rn[:, k], rn[:, k]))
                            dve.tensor_tensor(kqv[:, z, k], kqv[:, z, k], rn[:, k], ALU.mult)\
                               .then_inc(*up((k_unit, q_unit)[z], me))
                            if z == 0:
                                dve.wait_ge(*at(v_silu, k + 1))
                                dve.tensor_tensor(kqv[:, 2, k], kqv[:, 2, k], rn[:, k], ALU.mult)\
                                   .then_inc(*up(v_unit, me))
                if rest:
                    layer_norm(nxt)

                    def wide(v, n):
                        return v.unsqueeze(2).to_broadcast([P, B, n])

                    def pick(best, hot, scores, tie, rev, s1, s2, m):
                        n = rev.shape[-1]
                        step(dve.tensor_reduce(best, scores, AX.X, ALU.max))
                        step(dve.tensor_tensor(s1, scores, wide(best, n), ALU.is_equal))
                        if tie is not None:
                            step(dve.tensor_scalar(s1, s1, 1e30, -1e30, ALU.mult, ALU.add))
                            step(dve.tensor_tensor(s1, s1, tie, ALU.add))
                            step(dve.tensor_reduce(m, s1, AX.X, ALU.max))
                            step(dve.tensor_tensor(s1, s1, wide(m, n), ALU.is_equal))
                        step(dve.tensor_tensor(s2, s1, rev.unsqueeze(1).to_broadcast([P, B, n]), ALU.mult))
                        step(dve.tensor_reduce(m, s2, AX.X, ALU.max))
                        step(dve.tensor_tensor(hot, s2, wide(m, n), ALU.is_equal))

                    dve.wait_ge(*at(router, 1))
                    logits = bank[7][:, 0:B * E0].rearrange("p (b e) -> p b e", b=B)
                    step(dve.tensor_reduce(sm[:, 0], logits, AX.X, ALU.max))
                    dve.tensor_tensor(lg[:, 0], logits, wide(sm[:, 0], E0), ALU.subtract).then_inc(*up(logit_sub, me))
                    dve.wait_ge(*at(exp_ok, 1))
                    step(dve.tensor_reduce(sm[:, 1], lg[:, 1], AX.X, ALU.add))
                    step(dve.reciprocal(sm[:, 2], sm[:, 1]))
                    step(dve.tensor_tensor(lg[:, 2], lg[:, 1], wide(sm[:, 2], E0), ALU.mult))
                    pick(sm[:, 3], lg[:, 3], lg[:, 2], None, const("rev16"), lg[:, 4], lg[:, 5], sm[:, 4])
                    step(dve.scalar_tensor_tensor(lg[:, 6].rearrange("p b e -> p (b e)"),
                                                  lg[:, 3].rearrange("p b e -> p (b e)"), -4.0,
                                                  lg[:, 2].rearrange("p b e -> p (b e)"), ALU.mult, ALU.add))
                    pick(sm[:, 5], lg[:, 7], lg[:, 6], None, const("rev16"), lg[:, 4], lg[:, 5], sm[:, 4])
                    step(dve.tensor_tensor(sm[:, 6], sm[:, 3], sm[:, 5], ALU.add))
                    step(dve.tensor_scalar(sm[:, 6], sm[:, 6], 1e-9, None, ALU.add))
                    step(dve.reciprocal(sm[:, 7], sm[:, 6]))
                    step(dve.tensor_tensor(lg[:, 8], lg[:, 3], lg[:, 7], ALU.add))
                    step(dve.tensor_tensor(lg[:, 8], lg[:, 8], lg[:, 2], ALU.mult))
                    dve.tensor_tensor(lg[:, 9], lg[:, 8], wide(sm[:, 7], E0), ALU.mult).then_inc(*up(comb_ok, me))
                    dve.wait_ge(*at(comb_tr, 1))
                    dve.tensor_copy(combT[:, :, :].rearrange("p b t -> p (b t)"), bank[6][0:E0, :])\
                       .then_inc(*up(comb_copied, me))
                    for i in range(TILES0):
                        h = hid0[:, i].rearrange("p b t -> p (b t)")
                        dve.wait_ge(*at(sg_ok, i + 1))
                        dve.wait_ge(*at(up_mm, i + 1))
                        ins_ = dve.tensor_tensor(h, sg0[:, i % 2].rearrange("p b t -> p (b t)"),
                                                 bank[3 * (i % 2) + 1][:, :], ALU.mult)
                        if i < ROUTED0:
                            step(ins_)
                            ins_ = dve.tensor_tensor(h, h, bank[3 * (i % 2) + 2][:, :], ALU.mult)
                        ins_.then_inc(*up(hid0_ok, me))
                        scan(SCAN_TILE)
                    residual(1, (6, 7), 0, 1, None)

                    layer_norm(nxt + 1)
                    for b in range(B):
                        dve.wait_ge(*at(v_mm, b + 1))
                        step(dve.tensor_tensor(V3[:, b, :, 1:3, :].rearrange("p h r e -> p h (r e)"),
                                               bank[4 + b][:, :].rearrange("p (h j) -> p h j", h=H1),
                                               row("b_v").rearrange("p (h j) -> p h j", h=H1), ALU.add))
                        dve.tensor_scalar(V3[:, b, :, 0, :], V3[:, b, :, 2, :], -1.0, None, ALU.mult)\
                           .then_inc(*up(v3_ok, me))
                    flat = "p r b t -> p r (b t)"
                    for hg in range(HG):
                        q2 = Q3[:, 1:3].rearrange(flat)
                        k2 = K2[:, :].rearrange(flat)
                        a2 = TT[:, :, 0:NT]

                        def twice(v):
                            return v.unsqueeze(1).to_broadcast([P, 2, v.shape[-1]])

                        dve.wait_ge(*at(plane_ok, 6 * hg + 6))
                        step(dve.tensor_tensor(t1[:, :, :], a2, a2, ALU.mult))
                        dve.tensor_tensor(t1[:, 0], t1[:, 0], t1[:, 1], ALU.add).then_inc(*up(mag_ok, me))
                        settle()
                        step(dve.tensor_scalar(t1[:, 1], t1[:, 0], 1.0, None, ALU.add))
                        step(dve.reciprocal(t1[:, 1], t1[:, 1]))
                        dve.wait_ge(*at(mag_root, hg + 1))
                        step(dve.tensor_tensor(t1[:, 0], t2[:, 0], t1[:, 1], ALU.mult))
                        step(dve.tensor_tensor(a2, a2, twice(t1[:, 0]), ALU.mult))
                        step(dve.tensor_tensor(t1[:, :, :], q2, twice(k2[:, 0]), ALU.mult))
                        step(dve.tensor_tensor(t2[:, :, :], q2, twice(k2[:, 1]), ALU.mult))
                        step(dve.tensor_tensor(t1[:, 0], t1[:, 0], t2[:, 1], ALU.subtract))
                        dve.tensor_tensor(t1[:, 1], t1[:, 1], t2[:, 0], ALU.add).then_inc(*up(pairs_ok, me))
                        step(dve.tensor_scalar(Q3[:, 0], Q3[:, 2], -1.0, None, ALU.mult))
                        off = 0
                        for lev in range(LEVELS):
                            n = NT >> lev
                            w = TT[:, :, off:off + n].rearrange("p r (j two) -> p r j two", two=2)
                            wider = TT[:, :, off + n:off + n + n // 2]
                            ta, tb = t2[:, :, 0:n // 2], t2[:, :, 256:256 + n // 2]
                            step(dve.tensor_tensor(ta, w[:, :, :, 0], twice(w[:, 0, :, 1]), ALU.mult))
                            step(dve.tensor_tensor(tb, w[:, :, :, 0], twice(w[:, 1, :, 1]), ALU.mult))
                            step(dve.tensor_tensor(wider[:, 0], ta[:, 0], tb[:, 1], ALU.subtract))
                            step(dve.tensor_tensor(wider[:, 1], ta[:, 1], tb[:, 0], ALU.add))
                            off += n
                        dve.sem_inc(*up(a_ok))
                        dve.wait_ge(*at(diag_mm, hg + 1))
                        dve.tensor_copy(diag[:, :, :, :].rearrange("p b h r -> p (b h r)"), bank[6][:, 0:B * HP * 2])\
                           .then_inc(*up(diag_ok, me))
                        step(dve.tensor_tensor(t1[:, :, :], q2, twice(TT[:, 0, 0:NT]), ALU.mult))
                        step(dve.tensor_tensor(t2[:, :, :], Q3[:, 0:2].rearrange(flat), twice(TT[:, 1, 0:NT]), ALU.mult))
                        step(dve.tensor_tensor(q2, t1[:, :, :], t2[:, :, :], ALU.add))
                        for bp in range(2):
                            two = slice(2 * bp, 2 * bp + 2)
                            dve.tensor_scalar(Q3[:, 0, two], Q3[:, 2, two], -1.0, None, ALU.mult).then_inc(*up(q_ready, me))
                        off = 0
                        for lev in range(LEVELS):
                            m = 1 << lev
                            nb = SEG // (2 * m)
                            for bp in range(2):
                                u = (hg * LEVELS + lev) * 2 + bp
                                for i in range(2):
                                    b = 2 * bp + i
                                    dve.wait_ge(*at(scored, 2 * u + i + 1))
                                    if lev == 0:
                                        dve.wait_ge(*at(score_init, B * hg + b + 1))
                                    dve.sem_inc(passed.handle, 1)
                                    dst = score[:, b].rearrange("p h r (n two m) -> p (h r) n two m", two=2, m=m)[:, :, :, 1]
                                    dve.copy_predicated(
                                        dst,
                                        masks[:, lev].rearrange("p (n m) -> p n m", m=m).unsqueeze(1)
                                        .to_broadcast([P, 2 * HP, nb, m]),
                                        bank[b][:, :].rearrange("p (g n m) -> p g n m", g=2 * HP, m=m))\
                                       .then_inc(*up(masked, me))
                                n = 2 * nb
                                half = "p r b (n two m) -> p r (b n) two m"
                                two = slice(2 * bp, 2 * bp + 2)
                                Tb = TT[:, :, off + bp * 2 * n:off + (bp + 1) * 2 * n]\
                                    .rearrange("p r (n two) -> p r n two", two=2)[:, :, :, 0]

                                def over(v):
                                    return v.unsqueeze(1).unsqueeze(3).to_broadcast([P, 2, n, m])

                                def tmp(t):
                                    return t[:, :, 0:P].rearrange("p r (n m) -> p r n m", m=m)

                                q_hi = Q3[:, 1:3, two].rearrange(half, two=2, m=m)[:, :, :, 1]
                                q_lo = Q3[:, 0:2, two].rearrange(half, two=2, m=m)[:, :, :, 1]
                                dve.tensor_tensor(tmp(t1), q_hi, over(Tb[:, 0]), ALU.mult).then_inc(*up(dve_step, me))
                                step(dve.tensor_tensor(tmp(t2), q_lo, over(Tb[:, 1]), ALU.mult))
                                step(dve.tensor_tensor(q_hi, tmp(t1), tmp(t2), ALU.add))
                                dve.tensor_scalar(q_lo[:, 0], q_hi[:, 1], -1.0, None, ALU.mult).then_inc(*up(q_ready, me))
                            off += NT >> lev
                        dve.wait_ge(*at(r_mm, hg + 1))
                        settle()
                        for b in range(B):
                            old = t1[:, 0, 64 * b:64 * b + 64]
                            step(dve.scalar_tensor_tensor(old, H3[:, hg, b, 1:3].rearrange("p r e -> p (r e)"),
                                                          TT[:, 0, off + b:off + b + 1],
                                                          bank[7][:, 64 * b:64 * b + 64], ALU.mult, ALU.add))
                            step(dve.scalar_tensor_tensor(t1[:, 1, 64 * b:64 * b + 64],
                                                          H3[:, hg, b, 0:2].rearrange("p r e -> p (r e)"),
                                                          TT[:, 1, off + b:off + b + 1], old, ALU.mult, ALU.add))
                        step(dve.tensor_copy(H3[:, hg, :, 1:3].rearrange("p b r e -> p b (r e)"),
                                             t1[:, 1, 0:256].rearrange("p (b j) -> p b j", b=B)))
                        dve.tensor_scalar(H3[:, hg, :, 0], H3[:, hg, :, 2], -1.0, None, ALU.mult)\
                           .then_inc(*up(state_ok, me))
                    residual(2, (2, 3), 1, 0, "b_out")

                    layer_norm(nxt + 2)
                    dve.wait_ge(*at(hT_ok, nxt + 3))
                    dve.tensor_tensor(sqh[:, :, :, :], hT[:, :, :, :], hT[:, :, :, :], ALU.mult).then_inc(*up(hsq_ok, me))
                    dve.wait_ge(*at(router, 2))
                    dve.tensor_copy(rs[:, 0], bank[7][:, 32:36]).then_inc(*up(rt_var, me))
                    sim = rt[:, 0]
                    step(dve.tensor_copy(sim, bank[7][:, 0:B * E1].rearrange("p (b e) -> p b e", b=B)))
                    step(dve.tensor_scalar(rt[:, 1], sim, -1.0, None, ALU.mult))
                    pick(rs[:, 2], rt[:, 2], rt[:, 1], None, const("up8"), rt[:, 3], rt[:, 4], rs[:, 3])
                    dve.wait_ge(*at(rt_root, 1))
                    step(dve.tensor_scalar(rs[:, 4], rs[:, 1], 1e-8, None, ALU.add))
                    step(dve.reciprocal(rs[:, 5], rs[:, 4]))
                    step(dve.tensor_tensor(rt[:, 5], sim, emb_rnorm[:, :].unsqueeze(1).to_broadcast([P, B, E1]), ALU.mult))
                    step(dve.tensor_tensor(rt[:, 5], rt[:, 5], wide(rs[:, 5], E1), ALU.mult))
                    step(dve.tensor_scalar(rt[:, 6], row("cache").unsqueeze(1).to_broadcast([P, B, E1]), 0.1, None,
                                           ALU.mult))
                    step(dve.tensor_tensor(rt[:, 5], rt[:, 5], rt[:, 6], ALU.add))

                    def flat2(v):
                        return v.rearrange("p b e -> p (b e)")

                    step(dve.scalar_tensor_tensor(flat2(rt[:, 5]), flat2(rt[:, 2]), -1e30, flat2(rt[:, 5]),
                                                  ALU.mult, ALU.add))
                    pick(rs[:, 6], rt[:, 7], rt[:, 5], sim, const("rev8"), rt[:, 3], rt[:, 4], rs[:, 3])
                    step(dve.scalar_tensor_tensor(flat2(rt[:, 8]), flat2(rt[:, 7]), -1e30, flat2(rt[:, 5]),
                                                  ALU.mult, ALU.add))
                    pick(rs[:, 7], rt[:, 9], rt[:, 8], sim, const("rev8"), rt[:, 3], rt[:, 4], rs[:, 3])
                    dve.tensor_tensor(rs[:, 10], rs[:, 7], rs[:, 6], ALU.subtract).then_inc(*up(rt_gap, me))
                    dve.wait_ge(*at(rt_exp, 1))
                    step(dve.tensor_scalar(rs[:, 12], rs[:, 11], 1.0, None, ALU.add))
                    step(dve.reciprocal(rs[:, 13], rs[:, 12]))
                    step(dve.tensor_tensor(rs[:, 14], rs[:, 11], rs[:, 13], ALU.mult))
                    step(dve.tensor_tensor(rt[:, 7], rt[:, 7], wide(rs[:, 13], E1), ALU.mult))
                    step(dve.tensor_tensor(rt[:, 9], rt[:, 9], wide(rs[:, 14], E1), ALU.mult))
                    dve.tensor_tensor(rt[:, 10], rt[:, 7], rt[:, 9], ALU.add).then_inc(*up(comb1_ok, me))
                    dve.wait_ge(*at(comb_tr, 2))
                    dve.tensor_copy(combT1[:, :, :].rearrange("p b t -> p (b t)"), bank[6][0:E1, :])\
                       .then_inc(*up(comb1_copied, me))
                    for j in range(2):
                        dve.wait_ge(*at(down_bias, j + 1))
                        dve.tensor_copy(acc[:, 2 * j:2 * j + 2].rearrange("p b d -> p (b d)"), bank[6 + j][:, :])\
                           .then_inc(*up(acc_ok, me))
                    for e in range(E1):
                        scan(SCAN_EXPERT)
                        settle()
                        for j in range(2):
                            dve.wait_ge(*at(down_mm, 2 * e + j + 1))
                            for i in range(2):
                                b = 2 * j + i
                                ins_ = dve.scalar_tensor_tensor(acc[:, b], bank[4 + 2 * (e % 2) + j][:, i * D:(i + 1) * D],
                                                                rt[:, 10, b, e:e + 1], acc[:, b], ALU.mult, ALU.add)
                            ins_.then_inc(*up(acc_ok, me))
                    settle()
                    step(dve.tensor_tensor(xn[:, :, :], acc[:, :, :], gates[:, 1, 1], ALU.mult))
                    dve.tensor_tensor(X[:, :, :], X[:, :, :], xn[:, :, :], ALU.add).then_inc(*up(x_final, me))
                scan(SEG)
                assert scanned[0] == SEG * nxt
                settle()
                top_up(dve, [dve_step, ln_var_ok, xn_ok, px_free, k_sq, conv_v, k_unit, q_unit, v_unit, o0_ok, o_sq,
                             o_norm_ok, logit_sub, comb_ok, comb_copied, hid0_ok, x_done, mag_ok, v3_ok, a_ok,
                             pairs_ok, diag_ok, q_ready, masked, state_ok, hsq_ok, rt_var, rt_gap, comb1_ok,
                             comb1_copied, acc_ok, x_final])
                dve.sem_inc(started.handle, 1)

            turns(dve, turn)

        @block.gpsimd
        def _(pool):
            me = "pool"
            pool.sem_inc(started.handle, 1)

            def turn(seg, rest, nxt):
                def at(s, k):
                    return s.handle, (seg + 1) * s.stride + k

                def settle():
                    s = last[me]
                    pool.wait_ge(s.handle, (seg + 1) * s.stride + s.count)

                def step(ins_):
                    ins_.then_inc(*up(pool_step, me))
                    settle()

                if rest:
                    pool.wait_ge(*at(ln_var_ok, nxt + 2))
                    pool.sem_inc(passed.handle, 1)
                    pool.memset(Kx[:, :, :, :, :].rearrange("p r h b t -> p (r h b t)"), 0.0).then_inc(*up(zeroed, me))
                    pool.memset(Hx[:, :, :, :, :].rearrange("p b r h j -> p (b r h j)"), 0.0).then_inc(*up(zeroed, me))
                    for hg in range(HG):
                        pool.wait_ge(*at(diag_ok, hg + 1))
                        if hg:
                            pool.wait_ge(*at(y_mm, 2 * hg))
                        for b in range(B):
                            pool.tensor_tensor(score[:, b].rearrange("p h r t -> p (h r) t"),
                                               ident.unsqueeze(1).to_broadcast([P, 2 * HP, SEG]),
                                               diag[:, b].rearrange("p h r -> p (h r)").unsqueeze(2)
                                               .to_broadcast([P, 2 * HP, SEG]), ALU.mult).then_inc(*up(score_init, me))
                        off = 0
                        for lev in range(LEVELS):
                            m = 1 << lev
                            n = SEG // m
                            for bp in range(2):
                                u = (hg * LEVELS + lev) * 2 + bp
                                pool.wait_ge(*at(kx_ready, u + 1))
                                if lev == 0:
                                    pool.wait_ge(*at(a_ok, hg + 1))
                                two = slice(2 * bp, 2 * bp + 2)
                                Tb = TT[:, :, off + bp * 2 * n:off + (bp + 1) * 2 * n]\
                                    .rearrange("p r (n two) -> p r n two", two=2)[:, :, :, 1]

                                def over(v):
                                    return v.unsqueeze(1).unsqueeze(3).to_broadcast([P, 2, n, m])

                                def tmp(t):
                                    return t[:, :, 0:P].rearrange("p r (n m) -> p r n m", m=m)

                                kk = K2[:, :, two].rearrange("p r b (n two m) -> p r (b n) two m", two=2, m=m)[:, :, :, 0]
                                settle()
                                pool.tensor_tensor(tmp(u1), kk, over(Tb[:, 0]), ALU.mult).then_inc(*up(pool_step, me))
                                step(pool.tensor_tensor(tmp(u2), kk, over(Tb[:, 1]), ALU.mult))
                                pool.tensor_tensor(kk[:, 0], tmp(u1)[:, 0], tmp(u2)[:, 1], ALU.subtract)\
                                    .then_inc(*up(pool_step, me))
                                pool.tensor_tensor(kk[:, 1], tmp(u1)[:, 1], tmp(u2)[:, 0], ALU.add)\
                                    .then_inc(*up(k_ready, me))
                            off += NT >> lev
                    settle()
                else:
                    pool.wait_ge(seg_open.handle, seg + 2)
                pool.sem_inc(passed.handle, 1)
                top_up(pool, [pool_step, zeroed, score_init, k_ready])
                pool.sem_inc(started.handle, 1)

            turns(pool, turn)

        @block.tensor
        def _(pe):
            NTAB = 16 * (len(TABLES) + 3 + HG * B)
            mm = pe.matmul
            pe.wait_ge(tables_in.handle, NTAB)
            pe.wait_ge(emb_sq.handle, 2)
            esq = arena[:, 4096:4096 + KC * E1].rearrange("p (k e) -> p k e", k=KC)
            for k in range(KC):
                i_ = mm(bank[1][:, 0:E1], const("ones"), esq[:, k], start=(k == 0), stop=(k == KC - 1))
            i_.then_inc(emb_sum.handle, 1)
            for blk in range(2):
                for w, src in enumerate((0, 1, 3, 4)):
                    for kc in range(KC):
                        at_ = ((blk * 4 + w) * KC + kc) * B
                        for k in range(KC):
                            i_ = mm(bank[0][:, at_:at_ + B], wmod[blk][:, k, src * D + kc * P:src * D + kc * P + P],
                                    silu_c[:, blk, k, :], start=(k == 0), stop=(k == KC - 1))
            i_.then_inc(mod_cols.handle, 1)
            pe.wait_ge(mod_cols.handle, 2)
            c_wide = arena[:, 0:2 * KC * B * P].rearrange("p (a k b j) -> p a k b j", a=2, k=KC, b=B)
            for i in range(8):
                blk, g = i // 4, (i // 2) % 2
                for j in range(2):
                    b = 2 * (i % 2) + j
                    for k in range(KC):
                        src = (2 + 3 * g) * D
                        i_ = mm(bank[i][:, j * D:(j + 1) * D], c_wide[:, blk, k, b], wmod[blk][:, k, src:src + D],
                                start=(k == 0), stop=(k == KC - 1))
                i_.then_inc(mod_rows.handle, 1)
            pe.sem_inc(started.handle, 1)


            def turn(seg, rest, nxt):
                def at(s, k):
                    return s.handle, (seg + 1) * s.stride + k

                def rhs(t, k):
                    return t[:, k].rearrange("p b t -> p (b t)")

                def layer_norm(n):
                    pe.wait_ge(*at(xn_ok, n + 1))
                    for k in range(KC):
                        for b in range(B):
                            i_ = pe.transpose(bank[k][:, b * SEG:(b + 1) * SEG], xn[:, b, k * P:(k + 1) * P], ident)
                    i_.then_inc(*up(ln_tr))
                    pe.wait_ge(*at(hT_ok, n + 1))

                def channels(dst, w, cols_, src, n=KC):
                    for k in range(n):
                        i_ = mm(dst, w[:, k, cols_], rhs(src, k), start=(k == 0), stop=(k == n - 1))
                    return i_

                def tokens(banks, src, w):
                    for j in range(2):
                        for i in range(2):
                            for k in range(KC):
                                i_ = mm(bank[banks[j]][:, i * D:(i + 1) * D], src[:, k, 2 * j + i, :], w[:, k, :],
                                        start=(k == 0), stop=(k == KC - 1))
                        i_.then_inc(*up(res))

                done = KC if rest else 0
                pe.wait_ge(seg_open.handle, seg + 2)
                if rest:
                    for k in range(KC):
                        pe.wait_ge(*at(o_sq, k + 1))
                        mm(bank[5 + k][:, :], const("ones16"), rhs(osq, k), start=True, stop=True).then_inc(*up(nrm))
                    pe.wait_ge(*at(o_norm_ok, KC))
                    tokens((2, 3), oT, w_o)

                if nxt:
                    layer_norm(0)
                    for n in range(6):
                        if n >= 2:
                            pe.wait_ge(*at(px_ok, n - 1))
                        channels(bank[2 + n % 2][:, :], w_qkv, slice(n * P, (n + 1) * P), hT).then_inc(*up(proj))
                    channels(bank[4][0:H0, :], w_beta, slice(0, H0), hT).then_inc(*up(proj))
                    for n in range(4):
                        pe.wait_ge(*at(k_sq, n + 1))
                        if n >= 2:
                            pe.wait_ge(*at(root, done + n - 1))
                        mm(bank[5 + n % 2][:, :], const("ones16"), rhs(sq, n % 2), start=True, stop=True)\
                            .then_inc(*up(nrm))
                if rest:
                    layer_norm(nxt)
                    for b in range(B):
                        for k in range(KC):
                            i_ = mm(bank[7][:, b * E0:(b + 1) * E0], hT[:, k, b, :], w_router[:, k, :],
                                    start=(k == 0), stop=(k == KC - 1))
                    i_.then_inc(*up(router))

                    def slot(n):
                        pe.wait_ge(*at(ring_in[n % SLOTS], 16 * (n // SLOTS + 1)))
                        return ring[:, n % SLOTS, :]

                    def spread(i):
                        mm(bank[3 * (i % 2) + 2][:, :], sel[:, i, :], combT[:, :, :].rearrange("e b t -> e (b t)"),
                           start=True, stop=True).then_inc(*up(up_mm))

                    def turn_weights(n, src, width):
                        for b in range(B):
                            i_ = pe.transpose(bank[6][0:width, b * SEG:(b + 1) * SEG], src[:, b, :], ident)
                        i_.then_inc(*up(comb_tr))

                    for i in range(TILES0):
                        if i % 2 == 0:
                            both = slot(UP0_AT + i // 2).rearrange("p (g k c) -> p g k c", g=2, k=KC)
                        if i == 2:
                            pe.wait_ge(*at(comb_ok, 1))
                            turn_weights(0, lg[:, 9], E0)
                            pe.wait_ge(*at(comb_copied, 1))
                            spread(0)
                            spread(1)
                        if i >= 2:
                            pe.wait_ge(*at(sg_ok, i - 1))
                            pe.wait_ge(*at(hid0_ok, i - 1))
                        c = slice((i % 2) * P, (i % 2 + 1) * P)
                        channels(bank[3 * (i % 2)][:, :], both[:, 0], c, hT).then_inc(*up(gate_mm))
                        i_ = channels(bank[3 * (i % 2) + 1][:, :], both[:, 1], c, hT)
                        if i >= ROUTED0:
                            i_.then_inc(*up(up_mm))
                        elif i >= 2:
                            spread(i)
                    pe.wait_ge(*at(hid0_ok, TILES0))
                    downs = [slot(DOWN0_AT + d).rearrange("p (t c) -> p t c", c=D) for d in range(len(DOWN0))]
                    for b in range(B):
                        for d, (first, end) in enumerate(DOWN0):
                            for i in range(first, end):
                                i_ = mm(bank[6 + b // 2][:, (b % 2) * D:(b % 2 + 1) * D], hid0[:, i, b, :],
                                        downs[d][:, i - first, :], start=(i == 0), stop=(i == TILES0 - 1))
                            if b == B - 1 and d + 1 < len(DOWN0):
                                i_.then_inc(*up(down0_used))
                        if b % 2:
                            i_.then_inc(*up(res))

                    layer_norm(nxt + 1)
                    for k in range(KC):
                        channels(bank[2 + k][:, :], w_in, slice(k * P, (k + 1) * P), hT).then_inc(*up(u_mm))
                    pe.wait_ge(*at(u_ok, KC))
                    w_v = slot(V_AT).rearrange("p (k c) -> p k c", k=KC)
                    for b in range(B):
                        for k in range(KC):
                            i_ = mm(bank[4 + b][:, :], uT[:, k, b, :], w_v[:, k, :], start=(k == 0), stop=(k == KC - 1))
                        i_.then_inc(*up(v_mm))
                    for hg in range(HG):
                        if hg:
                            pe.wait_ge(*at(kt_ok, B * hg))
                        for c in range(6):
                            n = hg * 6 + c
                            if c >= 4:
                                pe.wait_ge(*at(plane_ok, n - 3))
                            four = slot(QKA_AT + n // 4).rearrange("p (k c) -> p k c", k=KC)
                            channels(bank[n % 4][:, :], four, slice((n % 4) * P, (n % 4 + 1) * P), uT)\
                                .then_inc(*up(plane_mm))
                        pe.wait_ge(*at(v3_ok, B))
                        pe.wait_ge(*at(pairs_ok, hg + 1))
                        d6 = bank[6][:, 0:B * HP * 2].rearrange("p (b h r) -> p b h r", b=B, r=2)
                        for b in range(B):
                            for r in range(2):
                                i_ = mm(d6[:, b, :, r], t1[:, r, b * SEG:(b + 1) * SEG], const("head_of"),
                                        start=True, stop=True)
                        i_.then_inc(*up(diag_mm))
                        for lev in range(LEVELS):
                            m = 1 << lev
                            for bp in range(2):
                                u = (hg * LEVELS + lev) * 2 + bp
                                pe.wait_ge(*at(kx_ready, u + 1))
                                pe.wait_ge(*at(q_ready, hg * 16 + lev * 2 + bp + 1))
                                if lev:
                                    pe.wait_ge(*at(masked, 2 * (u - 1)))
                                for b in (2 * bp, 2 * bp + 1):
                                    for h in range(HP):
                                        for r in range(2):
                                            qv = Q3[:, 1 - r:3 - r, b].rearrange("p r (n two m) -> p r n two m",
                                                                                 two=2, m=m)[:, :, :, 1]
                                            i_ = mm(bank[b][:, h * P:(h + 1) * P], Kx[:, r, h, b, :], qv,
                                                    start=(r == 0), stop=(r == 1))
                                    i_.then_inc(*up(scored))
                        pe.wait_ge(*at(hx_ok, 2 * HP * (hg + 1)))
                        pe.wait_ge(*at(q_ready, hg * 16 + 16))
                        pe.wait_ge(*at(masked, 28 * (hg + 1)))
                        for j in range(2):
                            for b in range(B):
                                y = bank[4 + j][:, b * SEG:(b + 1) * SEG]
                                for r in range(2):
                                    mm(y, Hx[:, b, r, 2 * j:2 * j + 2].rearrange("p h j -> p (h j)"),
                                       Q3[:, 1 + r, b, :], start=(r == 0), stop=False, skip_group_check=True)
                                for i in range(2):
                                    h = 2 * j + i
                                    for r in range(2):
                                        i_ = mm(y[64 * i:64 * i + 64],
                                                V3[:, b, hg * HP + h, 1 - r:3 - r, :].rearrange("p r e -> p (r e)"),
                                                score[:, b, h, r, :], start=False, stop=(r == 1), skip_group_check=True)
                            i_.then_inc(*up(y_mm))
                        pe.wait_ge(*at(k_ready, 14 * (hg + 1)))
                        for b in range(B):
                            for r in range(2):
                                i_ = pe.transpose(bank[b][:, r * P:(r + 1) * P], K2[:, r, b, :], ident)
                            i_.then_inc(*up(kt_mm))
                        if hg:
                            pe.wait_ge(*at(state_ok, hg))
                        for b in range(B):
                            pe.wait_ge(*at(kt_ok, hg * B + b + 1))
                            for h in range(HP):
                                for r in range(2):
                                    i_ = mm(bank[7][32 * h:32 * h + 32, 64 * b:64 * b + 64], KT[:, b, r, 32 * h:32 * h + 32],
                                            V3[:, b, hg * HP + h, 1 - r:3 - r, :].rearrange("p r e -> p (r e)"),
                                            start=(r == 0), stop=(r == 1))
                        i_.then_inc(*up(r_mm))
                    pe.wait_ge(*at(y2_ok, 4))
                    w_y = slot(Y_AT).rearrange("p (k c) -> p k c", c=D)
                    for k in range(KC):
                        channels(bank[k][:, :], w_y, slice(k * P, (k + 1) * P), y2T, 4).then_inc(*up(y3_mm))
                    pe.wait_ge(*at(y3_ok, KC))
                    tokens((2, 3), uT, w_out)

                    layer_norm(nxt + 2)
                    for b in range(B):
                        for k in range(KC):
                            mm(bank[7][:, b * E1:(b + 1) * E1], hT[:, k, b, :], w_emb[:, k, :],
                               start=(k == 0), stop=(k == KC - 1))
                    pe.wait_ge(*at(hsq_ok, 1))
                    for b in range(B):
                        for k in range(KC):
                            i_ = mm(bank[7][:, 32 + b:33 + b], sqh[:, k, b, :], const("ones")[:, 0:1],
                                    start=(k == 0), stop=(k == KC - 1))
                    i_.then_inc(*up(router))

                    def hidden(e):
                        for t in range(HT1):
                            if t % 4 == 0:
                                w1 = slot(EXPERT_AT + EXPERT_LOADS.index((0, e, t // 4)))\
                                    .rearrange("p (k c) -> p k c", k=KC)
                            if e or t >= 4:
                                pe.wait_ge(*at(hid1_ok, e * HT1 + t - 3))
                            channels(bank[t % 4][:, :], w1, slice(t % 4 * P, (t % 4 + 1) * P), hT).then_inc(*up(h1_mm))

                    hidden(0)
                    pe.wait_ge(*at(comb1_ok, 1))
                    turn_weights(1, rt[:, 10], E1)
                    pe.wait_ge(*at(comb1_copied, 1))
                    for j in range(2):
                        for i in range(2):
                            i_ = mm(bank[6 + j][:, i * D:(i + 1) * D], combT1[:, 2 * j + i, :], b2[:, :],
                                    start=True, stop=True)
                        i_.then_inc(*up(down_bias))
                    for e in range(E1):
                        if e + 1 < E1:
                            hidden(e + 1)
                        w2 = [slot(EXPERT_AT + EXPERT_LOADS.index((1, e, half))).rearrange("p (t c) -> p t c", c=D)
                              for half in range(2)]
                        pe.wait_ge(*at(hid1_ok, HT1 * (e + 1)))
                        for j in range(2):
                            if e:
                                pe.wait_ge(*at(acc_ok, 2 * (e - 1) + j + 1))
                            for i in range(2):
                                for t in range(HT1):
                                    i_ = mm(bank[4 + 2 * (e % 2) + j][:, i * D:(i + 1) * D], hid1[:, e % 2, t, 2 * j + i, :],
                                            w2[t // 4][:, t % 4, :], start=(t == 0), stop=(t == HT1 - 1))
                            i_.then_inc(*up(down_mm))
                if rest:
                    pe.wait_ge(*at(down_mm, down_mm.count))
                else:
                    pe.wait_ge(*at(nrm, nrm.count))
                pe.sem_inc(passed.handle, 1)
                top_up(pe, [ln_tr, proj, nrm, res, router, comb_tr, gate_mm, up_mm, down0_used, u_mm, plane_mm, v_mm,
                            diag_mm, scored, y_mm, kt_mm, r_mm, y3_mm, h1_mm, down_mm, down_bias])
                pe.sem_inc(started.handle, 1)

            turns(pe, turn)


INPUTS = {"x": (B, L, D), "w_qkv": (P, KC, 3 * D), "w_beta": (P, KC, H0), "w_o": (P, KC, D),
          "w_router": (P, KC, E0), "w_in": (P, KC, D), "w_out": (P, KC, D), "w_emb": (P, KC, E1), "b2": (E1, D), "cols": (P, NCOLS),
          "consts": (P, NCONST), "rows": (NROWS,), "c_cols": (P, 2, KC, B), "wmod": (2, P, KC, 1536),
          "w_ring": (LOADS, P, SLOT)}


def constants():
    t = np.zeros((P, NCONST), np.float32)

    def put(name, v):
        a, n = CONSTS[name]
        t[:v.shape[0], a:a + n] = v

    p = np.arange(P)
    put("ident", np.eye(P))
    put("ones16", (p[:, None] // HD0 == p[None] // HD0) * 1.0)
    put("ones", np.ones((P, P)))
    put("head_of", (p[:, None] // HD1 == np.arange(HP)[None]) * 1.0)
    put("rev16", np.tile(16.0 - np.arange(16), (P, 1)))
    put("rev8", np.tile(8.0 - np.arange(8), (P, 1)))
    put("up8", np.tile(1.0 + np.arange(8), (P, 1)))
    masks = []
    for lev in range(LEVELS):
        m = 1 << lev
        j = np.arange(64)
        block = j // m
        masks.append((p[:, None] // (2 * m) == block[None]) & (p[:, None] % (2 * m) < m))
    put("masks", np.concatenate(masks, 1) * 1.0)
    sel = (np.arange(E0)[:, None, None] == 2 * np.arange(ROUTED0)[None, :, None] + p[None, None] // MID0) * 1.0
    put("sel", sel.reshape(E0, -1))
    return t


def kernel(**inputs):
    import concourse.bacc as bacc
    from concourse.bass_utils import run_bass_kernel_spmd

    a = {k: np.asarray(v) for k, v in inputs.items()}

    def chunks(w):
        return w.reshape(-1, P, w.shape[-1]).transpose(1, 0, 2)

    def column(v):
        return v.reshape(-1, P).T

    def planes(w):
        v = w.reshape(HG, P, 4, 2, *w.shape[1:])
        return np.stack([v[g, :, c, r] for g in range(HG) for c in (0, 1, 3) for r in range(2)])

    w_qkva, b_qkva = a["L1_attn_W_qkva"], a["L1_attn_b_qkva"]
    values = w_qkva.reshape(H1, HD1, 4, 2, D)[:, :, 2].transpose(0, 2, 1, 3).reshape(512, D)
    b_values = b_qkva.reshape(H1, HD1, 4, 2)[:, :, 2].transpose(0, 2, 1).reshape(512)
    w_y = a["L1_attn_W_y"].reshape(D, H1, HD1, 2).transpose(1, 3, 2, 0).reshape(512, D)
    conv = [a[f"L0_attn_w{z}_conv"].reshape(KC, P, TAPS).transpose(1, 0, 2).reshape(P, -1) for z in "kqv"]
    cols_ = [column(a[f"L0_attn_b{z}"]) for z in "kqv"] + [column(a[f"L0_attn_b{z}_conv"]) for z in "kqv"] + conv
    bbeta = np.zeros((P, 1), np.float32)
    bbeta[:H0, 0] = a["L0_attn_bbeta"]
    cols_ += [np.tile(a["L0_attn_norm_w"], P // HD0)[:, None], bbeta, column(a["L1_attn_b_in"]),
              planes(b_qkva).T, column(a["L1_attn_b_y"]), column(a["L1_ffn_b1"].reshape(-1))]
    h0 = np.stack([a["L1_attn_h0_re"], a["L1_attn_h0_im"]], 2).reshape(HG, P, 2, HD1).transpose(1, 0, 2, 3)

    def hidden_columns(shared, routed):
        both = [w.transpose(1, 0, 2).reshape(D, -1) for w in (routed, shared)]
        return np.concatenate(both, 1)

    gate = chunks(hidden_columns(a["L0_ffn_wg_s"], a["L0_ffn_wg_r"]))
    up_ = chunks(hidden_columns(a["L0_ffn_wu_s"], a["L0_ffn_wu_r"]))
    down = chunks(np.concatenate([a["L0_ffn_wd_r"].reshape(-1, D), a["L0_ffn_wd_s"].reshape(-1, D)]))
    loads = [np.concatenate([w[:, :, 256 * g:256 * (g + 1)].reshape(P, -1) for w in (gate, up_)], 1)
             for g in range(TILES0 // 2)]
    loads += [down[:, s:e].reshape(P, -1) for s, e in DOWN0] + [chunks(values.T).reshape(P, -1)]
    qka = chunks(planes(w_qkva).reshape(12 * P, D).T)
    loads += [qka[:, :, 512 * g:512 * (g + 1)].reshape(P, -1) for g in range(3)] + [chunks(w_y).reshape(P, -1)]
    for w, e, half in EXPERT_LOADS:
        if w:
            loads.append(chunks(a["L1_ffn_W2"][e])[:, 4 * half:4 * half + 4].reshape(P, -1))
        else:
            loads.append(chunks(a["L1_ffn_W1"][e])[:, :, 512 * half:512 * half + 512].reshape(P, -1))
    loads = [np.pad(w, ((0, 0), (0, SLOT - w.shape[1]))) for w in loads]
    arrays = {
        "x": a["L0_attn_x"],
        "w_qkv": chunks(np.concatenate([a[f"L0_attn_W{z}"].T for z in "kqv"], 1)),
        "w_beta": chunks(a["L0_attn_Wbeta"].T), "w_o": chunks(a["L0_attn_Wo"].T),
        "w_router": chunks(a["L0_ffn_router_w"]), "w_in": chunks(a["L1_attn_W_in"].T),
        "w_out": chunks(a["L1_attn_W_out"].T),
        "w_emb": chunks(a["L1_ffn_uzman_embeddings"].T), "b2": a["L1_ffn_b2"],
        "cols": np.concatenate(cols_, 1), "consts": constants(),
        "rows": np.concatenate([a["L0_attn_bo"], a["L1_attn_b_out"], b_values, a["L1_ffn_onbellek_durumu"]]),
        "c_cols": np.stack([a["L0_c"].T.reshape(KC, P, B), a["L1_c"].T.reshape(KC, P, B)]).transpose(2, 0, 1, 3),
        "wmod": np.stack([chunks(a["L0_wmod"]), chunks(a["L1_wmod"])]),
        "w_ring": np.stack(loads), "h0": h0,
    }
    arrays = {k: np.ascontiguousarray(v) for k, v in arrays.items()}
    for k, shape in INPUTS.items():
        assert arrays[k].shape == shape, (k, arrays[k].shape, shape)
    nc = bacc.Bacc("TRN2", target_bir_lowering=False, num_devices=1)
    ins = {k: nc.dram_tensor(f"in_{k}", v.shape, mybir.dt.from_np(v.dtype), kind="ExternalInput").ap()
           for k, v in arrays.items()}
    out = nc.dram_tensor("out_x", (B, L, D), F32, kind="ExternalOutput").ap()
    nc.disable_value_cache = True
    build(nc, ins, out)
    r = run_bass_kernel_spmd(nc, [{f"in_{k}": v for k, v in arrays.items()}], core_ids=[0])
    return r.results[0]["out_x"]
```

```python
from contextlib import ExitStack

import numpy as np

import concourse.bass as bass
from concourse import mybir

F32 = mybir.dt.float32
I32 = mybir.dt.int32
ALU = mybir.AluOpType
ACT = mybir.ActivationFunctionType
AX = mybir.AxisListType

P = 128
B, L, D = 4, 1024, 256
KC = D // P
SEG = 128
NSEG = L // SEG
NT = B * SEG
H0, HD0, TAPS = 16, 16, 4
PAST = TAPS - 1
EV = HD0 // 2
E0, MID0, SHARED0 = 16, 64, 256
TILES0 = (E0 * MID0 + SHARED0) // P
SHARED_TILES = SHARED0 // P
ROUTED0 = TILES0 - SHARED_TILES
DOWN0 = [(0, 4), (4, 8), (8, 10)]
H1, HD1 = 8, 32
HG = 2
HP = 4
LEVELS = 7
E1, MID1 = 8, 1024
HT1 = MID1 // P

SLOT = 1024
SLOTS = 5
UP0_AT, DOWN0_AT = 0, TILES0 // 2
V_AT = DOWN0_AT + len(DOWN0)
QKA_AT = V_AT + 1
Y_AT = QKA_AT + 3
EXPERT_AT = Y_AT + 1


def expert_order():
    order = [(0, 0)]
    for e in range(E1):
        order += [(0, e + 1)] * (e + 1 < E1) + [(1, e)]
    return order


EXPERT_LOADS = [(w, e, half) for w, e in expert_order() for half in range(2)]
LOADS = EXPERT_AT + len(EXPERT_LOADS)
assert LOADS % SLOTS == 0
SCAN_TILE, SCAN_EXPERT = 1, 14
STRIDE = 4096

def scan_order():
    order = [(-1, "k*S"), (-1, "k.S"), (-1, "open delta")]
    for t in range(SEG):
        for name in ("k*S", "q*S", "delta", "k.S", "k*delta", "open delta", "S", "q.S"):
            if t == 0 and name == "delta" or t == SEG - 1 and name in ("k*S", "k.S", "open delta"):
                continue
            order.append((t, name))
    return order


SCAN_ORDER = scan_order()
SCAN_PARTS = 8

COLS = {}


def column_layout():
    at = 0
    for name, n in (("bqkv", 6), ("bqkv_conv", 6), ("w_conv", 24), ("norm_w", 1), ("bbeta", 1),
                    ("b_in", 2), ("b_qka", 12), ("b_y", 2), ("b1", E1 * HT1)):
        COLS[name] = (at, n)
        at += n
    return at


NCOLS = column_layout()
CONSTS = {}


def const_layout():
    at = 0
    for name, n in (("ident", P), ("ones16", P), ("ones", P), ("head_of", HP), ("rev16", 16), ("rev8", 8),
                    ("up8", 8), ("masks", LEVELS * 64), ("sel", ROUTED0 * P)):
        CONSTS[name] = (at, n)
        at += n
    return at


NCONST = const_layout()
ROWS = {"bo": (0, D), "b_out": (D, D), "b_v": (2 * D, 512), "cache": (2 * D + 512, E1)}
NROWS = 2 * D + 512 + E1


class Signal:

    def __init__(self, handle, stride):
        self.handle, self.stride, self.count = handle, stride, 0


def build(nc, ins, out):
    with ExitStack() as ctx:
        def sb(name, shape, dt=F32):
            return ctx.enter_context(nc.sbuf_tensor(name, shape, dt))

        w_qkv = sb("w_qkv", [P, KC, 3 * D])
        w_beta = sb("w_beta", [P, KC, H0])
        w_o = sb("w_o", [P, KC, D])
        w_router = sb("w_router", [P, KC, E0])
        w_in = sb("w_in", [P, KC, D])
        w_out = sb("w_out", [P, KC, D])
        w_emb = sb("w_emb", [P, KC, E1])
        b2 = sb("b2", [E1, D])
        cols = sb("cols", [P, NCOLS])
        consts = sb("consts", [P, NCONST])
        rows = sb("rows", [P, NROWS])
        ring = sb("ring", [P, SLOTS, SLOT])
        c_cols = sb("c_cols", [P, 2, KC, B])
        silu_c = sb("silu_c", [P, 2, KC, B])
        shift_scale = sb("shift_scale", [P, 2, 4, KC, B])
        gates = sb("gates", [P, 2, 2, B, D])
        emb_rnorm = sb("emb_rnorm", [P, E1])

        def col(name, i=0):
            return cols[:, COLS[name][0] + i:COLS[name][0] + i + 1]

        def const(name):
            a, n = CONSTS[name]
            return consts[:, a:a + n]

        def row(name):
            a, n = ROWS[name]
            return rows[:, a:a + n]

        ident = const("ident")
        masks = const("masks").bitcast(I32).rearrange("p (l j) -> p l j", l=LEVELS)
        sel = const("sel")[0:E0].rearrange("p (c j) -> p c j", c=ROUTED0)

        X = sb("X", [P, B, D])
        xn = sb("xn", [P, B, D])
        hT = sb("hT", [P, KC, B, SEG])
        ln_stats = sb("ln_stats", [P, B, 6])
        ln_mv = sb("ln_mv", [P, B, 2])
        ln_var = sb("ln_var", [P, B])
        ln_std = sb("ln_std", [P, B])
        ln_rstd = sb("ln_rstd", [P, B])
        past = sb("past", [P, 6, B, PAST])
        S0 = sb("S0", [P, EV, HD0])
        H3 = sb("H3", [P, HG, B, 3, HD1])
        KQ = sb("KQ", [P, 2, HD0, SEG])
        V0 = sb("V0", [P, EV, SEG])
        beta_scan = sb("beta_scan", [P, SEG])
        nbeta = sb("nbeta", [P, SEG])
        nbeta_kk = sb("nbeta_kk", [P, SEG])
        q_S = sb("q_S", [P, SEG, EV])
        kS = sb("kS", [P, 2, EV])
        delta = sb("delta", [P, SEG, EV])
        prod = sb("prod", [P, 2, EV, HD0])
        outer = sb("outer", [P, EV, HD0])
        arena = sb("arena", [P, 24096])

        def carve(offset, shape):
            n = int(np.prod(shape[1:]))
            flat = arena[0:shape[0], offset:offset + n]
            assert offset + n <= 24096, (offset, n)
            names = "abcdef"[:len(shape) - 1]
            view = flat if len(shape) == 2 else flat.rearrange(
                f"p ({' '.join(names)}) -> p {' '.join(names)}",
                **{k: v for k, v in zip(names, shape[1:])})
            return view, offset + n

        o = 0
        PX, o = carve(o, [P, KC, B, PAST + SEG])
        kqv, o = carve(o, [P, 3, KC, B, SEG])
        sq, o = carve(o, [P, KC, B, SEG])
        rn, o = carve(o, [P, KC, B, SEG])
        tmp_dot, o = carve(o, [P, HD0, SEG])
        qk_dot, o = carve(o, [P, SEG])
        O0, o = carve(o, [P, EV, SEG])
        betaT, o = carve(o, [H0, B, SEG])
        oT, o = carve(o, [P, KC, B, SEG])
        osq, o = carve(o, [P, KC, B, SEG])
        orn, o = carve(o, [P, KC, B, SEG])
        X_next, o = carve(o, [P, B, D])
        tmp_kk, o = carve(o, [P, HD0, SEG - 1])
        o = 0
        hid0, o = carve(o, [P, TILES0, B, SEG])
        sg0, o = carve(o, [P, 2, B, SEG])
        combT, o = carve(o, [E0, B, SEG])
        lg, o = carve(o, [P, 12, B, E0])
        sm, o = carve(o, [P, 16, B])
        o = 0
        V3, o = carve(o, [P, B, H1, 3, HD1])
        y2T, o = carve(o, [P, 4, B, SEG])
        uT, o = carve(o, [P, KC, B, SEG])
        Q3, o = carve(o, [P, 3, B, SEG])
        K2, o = carve(o, [P, 2, B, SEG])
        TT, o = carve(o, [P, 2, 1024])
        t1, o = carve(o, [P, 2, NT])
        t2, o = carve(o, [P, 2, NT])
        u1, o = carve(o, [P, 2, NT // 2])
        u2, o = carve(o, [P, 2, NT // 2])
        Kx, o = carve(o, [P, 2, HP, B, SEG])
        score, o = carve(o, [P, B, HP, 2, SEG])
        pair_re = score[:, 0].rearrange("p h r t -> p (h r t)").rearrange("p (c t) -> p c t", c=2)
        pair_im = score[:, 1].rearrange("p h r t -> p (h r t)").rearrange("p (c t) -> p c t", c=2)
        Hx, o = carve(o, [P, B, 2, HP, 2 * HD1])
        diag, o = carve(o, [P, B, HP, 2])
        KT = t2.rearrange("p r (b c) -> p (r b) c", c=2 * P).rearrange("p b (r c) -> p b r c", r=2)
        o = 0
        hid1, o = carve(o, [P, 2, HT1, B, SEG])
        acc, o = carve(o, [P, B, D])
        combT1, o = carve(o, [E1, B, SEG])
        sqh, o = carve(o, [P, KC, B, SEG])
        rt, o = carve(o, [P, 16, B, E1])
        rs, o = carve(o, [P, 24, B])

        bank = [ctx.enter_context(nc.psum_tensor(f"bank{i}", [P, 512], F32)) for i in range(8)]

        signals = []

        def signal(name, stride=STRIDE):
            s = Signal(ctx.enter_context(nc.semaphore(name)), stride)
            signals.append(s)
            return s

        tables_in = signal("tables_in")
        silu_done = signal("silu_done")
        mod_cols = signal("mod_cols")
        mod_rows = signal("mod_rows")
        mod_rows_taken = signal("mod_rows_taken")
        emb_sq = signal("emb_sq")
        emb_sum = signal("emb_sum")
        emb_root = signal("emb_root")
        started = signal("started")
        seg_open = signal("seg_open")
        passed = signal("passed")
        x_in = signal("x_in", 16)
        x_next_in = signal("x_next_in", 32)
        x_out = signal("x_out", 16)
        ring_in = [signal(f"ring_in{i}", 16 * (LOADS // SLOTS)) for i in range(SLOTS)]
        kq_out = signal("kq_out", 16 * 4)
        k_scan = signal("k_scan", 16 * 8)
        q_scan = signal("q_scan", 16 * 8)
        v_scan = signal("v_scan", 16 * 8)
        beta_in = signal("beta_in", 16 * 8)
        o_out = signal("o_out", 16 * 8)
        o_in = signal("o_in", 16)
        scan_step = signal("scan_step")
        dve_step = signal("dve_step")
        ln_var_ok = signal("ln_var_ok")
        xn_ok = signal("xn_ok")
        px_free = signal("px_free")
        k_sq = signal("k_sq")
        conv_v = signal("conv_v")
        k_unit = signal("k_unit")
        q_unit = signal("q_unit")
        v_unit = signal("v_unit")
        o0_ok = signal("o0_ok")
        o_sq = signal("o_sq")
        o_norm_ok = signal("o_norm_ok")
        logit_sub = signal("logit_sub")
        comb_ok = signal("comb_ok")
        comb_copied = signal("comb_copied")
        hid0_ok = signal("hid0_ok")
        res_taken = signal("res_taken")
        x_done = signal("x_done")
        mag_ok = signal("mag_ok")
        k_neg = signal("k_neg")
        v3_ok = signal("v3_ok")
        a_ok = signal("a_ok")
        q_ready = signal("q_ready")
        masked = signal("masked")
        state_ok = signal("state_ok")
        hsq_ok = signal("hsq_ok")
        rt_var = signal("rt_var")
        rt_gap = signal("rt_gap")
        comb1_ok = signal("comb1_ok")
        comb1_copied = signal("comb1_copied")
        acc_ok = signal("acc_ok")
        x_final = signal("x_final")
        ln_tr = signal("ln_tr")
        proj = signal("proj")
        nrm = signal("nrm")
        res = signal("res")
        router = signal("router")
        comb_tr = signal("comb_tr")
        gate_mm = signal("gate_mm")
        up_mm = signal("up_mm")
        down0_used = signal("down0_used")
        u_mm = signal("u_mm")
        plane_mm = signal("plane_mm")
        v_mm = signal("v_mm")
        diag_mm = signal("diag_mm")
        scored = signal("scored")
        y_mm = signal("y_mm")
        kt_mm = signal("kt_mm")
        r_mm = signal("r_mm")
        y3_mm = signal("y3_mm")
        h1_mm = signal("h1_mm")
        down_mm = signal("down_mm")
        down_bias = signal("down_bias")
        act_step = signal("act_step")
        ln_root = signal("ln_root")
        hT_ok = signal("hT_ok")
        px_ok = signal("px_ok")
        beta_ok = signal("beta_ok")
        root = signal("root")
        v_silu = signal("v_silu")
        exp_ok = signal("exp_ok")
        sg_ok = signal("sg_ok")
        u_ok = signal("u_ok")
        plane_ok = signal("plane_ok")
        mag_root = signal("mag_root")
        hx_ok = signal("hx_ok")
        kx_ready = signal("kx_ready")
        diag_ok = signal("diag_ok")
        y2_ok = signal("y2_ok")
        kt_ok = signal("kt_ok")
        y3_ok = signal("y3_ok")
        rt_root = signal("rt_root")
        rt_exp = signal("rt_exp")
        hid1_ok = signal("hid1_ok")
        pool_step = signal("pool_step")
        zeroed = signal("zeroed")
        pairs_ok = signal("pairs_ok")
        score_init = signal("score_init")
        k_ready = signal("k_ready")

        last = {}

        def up(s, who=None):
            s.count += 1
            if who is not None:
                last[who] = s
            return s.handle, 1

        def up16(s):
            s.count += 16
            return s.handle, 16

        def top_up(eng, mine):
            for s in mine:
                assert s.count <= s.stride
                if s.count < s.stride:
                    eng.sem_inc(s.handle, s.stride - s.count)
                s.count = 0

        def turns(eng, turn):
            turn(-1, False, True)
            with eng.Fori(0, NSEG - 1) as seg:
                turn(seg, True, True)
            turn(NSEG - 1, True, False)

        kqv_d = nc.dram_tensor("kqv_d", (3, D, B, SEG), F32, kind="Internal").ap()
        beta_d = nc.dram_tensor("beta_d", (H0, B, SEG), F32, kind="Internal").ap()
        o_d = nc.dram_tensor("o_d", (KC, H0 // KC, 2, EV, B, SEG), F32, kind="Internal").ap()

        x_seg = ins["x"].rearrange("b (s p) d -> s p b d", p=SEG)
        out_seg = out.rearrange("b (s p) d -> s p b d", p=SEG)
        block = ctx.enter_context(nc.Block())

        TABLES = [(w_qkv, "w_qkv"), (w_beta, "w_beta"), (w_o, "w_o"), (w_router, "w_router"), (w_in, "w_in"),
                  (w_out, "w_out"), (w_emb, "w_emb"), (b2, "b2"),
                  (cols, "cols"), (consts, "consts"), (c_cols, "c_cols")]
        wmod = [arena[:, 12288 + i * KC * 1536:12288 + (i + 1) * KC * 1536].rearrange("p (k n) -> p k n", k=KC)
                for i in range(2)]

        @block.sync
        def _(sp):
            for t, name in TABLES:
                sp.dma_start(t[:], ins[name]).then_inc(tables_in.handle, 16)
            sp.dma_start(rows[:, :], ins["rows"].partition_broadcast(P)).then_inc(tables_in.handle, 16)
            for i in range(2):
                sp.dma_start(wmod[i], ins["wmod"][i]).then_inc(tables_in.handle, 16)
            for g in range(HG):
                for b in range(B):
                    sp.dma_start(H3[:, g, b, 1:3], ins["h0"][:, g]).then_inc(tables_in.handle, 16)

            def turn(seg, rest, nxt):
                def at(s, k):
                    return s.handle, (seg + 1) * s.stride + k

                sp.wait_ge(started.handle, (seg + 1) * 4 + 4)
                sp.sem_inc(seg_open.handle, 1)
                def load_next():
                    src = x_seg[bass.ds(seg + 2, 1)] if rest else x_seg[1:2]
                    sp.dma_start(X_next, src.rearrange("a p b d -> (a p) b d")).then_inc(*up16(x_next_in))

                if not rest:
                    sp.dma_start(X_next, x_seg[0:1].rearrange("a p b d -> (a p) b d")).then_inc(*up16(x_next_in))
                    sp.wait_ge(*at(xn_ok, 1))
                    load_next()

                def load(n):
                    if n >= SLOTS:
                        was = n - SLOTS
                        if was < DOWN0_AT:
                            free = at(up_mm, 2 * was + 2)
                        elif was < V_AT:
                            d = was - DOWN0_AT
                            free = at(down0_used, d + 1) if d + 1 < len(DOWN0) else at(res, 4)
                        elif was < QKA_AT:
                            free = at(v_mm, B)
                        elif was < Y_AT:
                            free = at(plane_mm, 4 * (was - QKA_AT + 1))
                        elif was < EXPERT_AT:
                            free = at(y3_mm, KC)
                        else:
                            w, e, half = EXPERT_LOADS[was - EXPERT_AT]
                            free = at(down_mm, 2 * e + 2) if w else at(h1_mm, HT1 * e + 4 * half + 4)
                        sp.wait_ge(*free)
                    sp.dma_start(ring[:, n % SLOTS, :], ins["w_ring"][n]).then_inc(*up16(ring_in[n % SLOTS]))

                if rest:
                    here = x_seg[bass.ds(seg, 1)] if nxt else x_seg[NSEG - 1:NSEG]
                    sp.wait_ge(x_out.handle, (seg + 1) * x_out.stride)
                    sp.dma_start(X[:, :, :], here.rearrange("a p b d -> (a p) b d")).then_inc(*up16(x_in))
                    for n in range(SLOTS):
                        load(n)
                    sp.wait_ge(*at(o0_ok, 1))
                    for half in range(2):
                        for b in range(B):
                            p0 = half * 64 + b * H0
                            dst = o_d.rearrange("k h g e b t -> g b (k h) e t")[half, b]
                            sp.dma_start(dst, O0[p0:p0 + H0]).then_inc(*up16(o_out))
                    sp.wait_ge(*at(o_out, o_out.stride))
                    sp.dma_start(oT, o_d.rearrange("k h g e b t -> (h g e) k b t")).then_inc(*up16(o_in))
                if nxt:
                    sp.wait_ge(*at(beta_ok, 1))
                    sp.dma_start(beta_d, betaT[:, :, :]).then_inc(*up16(kq_out))
                    sp.wait_ge(*at(kq_out, 16))
                    for half in range(2):
                        for b in range(B):
                            p0 = half * 64 + b * H0
                            sp.dma_start(beta_scan[p0:p0 + H0, :], beta_d.rearrange("h b t -> b h t")[b])\
                                .then_inc(*up16(beta_in))
                    for z, (ready, sem) in enumerate(((k_unit, k_scan), (q_unit, q_scan), (v_unit, v_scan))):
                        sp.wait_ge(*at(ready, KC))
                        sp.dma_start(kqv_d[z].rearrange("(k p) b t -> p k b t", p=P), kqv[:, z]).then_inc(*up16(kq_out))
                        sp.wait_ge(*at(kq_out, kq_out.count))
                        for half in range(2):
                            for b in range(B):
                                p0 = half * 64 + b * H0
                                if z < 2:
                                    src = kqv_d[z].rearrange("(h d) b t -> b h d t", h=H0)[b]
                                    sp.dma_start(KQ[p0:p0 + H0, z], src).then_inc(*up16(sem))
                                else:
                                    src = kqv_d[z].rearrange("(h g e) b t -> g b h e t", h=H0, g=2)[half, b]
                                    sp.dma_start(V0[p0:p0 + H0], src).then_inc(*up16(sem))
                if rest:
                    for n in range(SLOTS, LOADS):
                        load(n)
                        if nxt and n == EXPERT_AT + SLOTS:
                            load_next()
                    sp.wait_ge(*at(x_final, 1))
                    there = out_seg[bass.ds(seg, 1)] if nxt else out_seg[NSEG - 1:NSEG]
                    sp.dma_start(there.rearrange("a p b d -> (a p) b d"), X[:, :, :]).then_inc(*up16(x_out))
                    if not nxt:
                        sp.wait_ge(*at(x_out, 16))
                sp.sem_inc(passed.handle, 1)
                top_up(sp, [x_in, x_next_in, x_out, kq_out, k_scan, q_scan, v_scan, beta_in, o_out, o_in, *ring_in])

            turns(sp, turn)

        @block.scalar
        def _(act):
            me = "act"

            NTAB = 16 * (len(TABLES) + 3 + HG * B)
            act.wait_ge(tables_in.handle, NTAB)
            act.activation(silu_c[:, :, :, :].rearrange("p a k b -> p (a k b)"),
                           c_cols[:, :, :, :].rearrange("p a k b -> p (a k b)"), ACT.Silu).then_inc(silu_done.handle, 1)
            act.wait_ge(emb_sum.handle, 1)
            act.activation(emb_rnorm[:, :], bank[1][:, 0:E1], ACT.Sqrt).then_inc(emb_root.handle, 1)
            act.wait_ge(emb_root.handle, 1)
            act.sem_inc(started.handle, 1)

            def turn(seg, rest, nxt):
                def at(s, k):
                    return s.handle, (seg + 1) * s.stride + k

                def settle():
                    s = last[me]
                    act.wait_ge(s.handle, (seg + 1) * s.stride + s.count)

                act.wait_ge(seg_open.handle, seg + 2)

                def norm_root(n):
                    act.wait_ge(*at(ln_var_ok, n + 1))
                    act.activation(ln_std[:, :], ln_var[:, :], ACT.Sqrt).then_inc(*up(ln_root, me))

                def norm_modulate(n, blk, which):
                    act.wait_ge(*at(ln_tr, n + 1))
                    for k in range(KC):
                        for b in range(B):
                            ins_ = act.activation(hT[:, k, b, :], bank[k][:, b * SEG:(b + 1) * SEG], ACT.Identity,
                                                  bias=shift_scale[:, blk, which, k, b:b + 1],
                                                  scale=shift_scale[:, blk, which + 1, k, b:b + 1])
                    ins_.then_inc(*up(hT_ok, me))

                def layer_norm(n, blk, which):
                    norm_root(n)
                    norm_modulate(n, blk, which)

                done = 4 if nxt else 0
                if nxt:
                    if not rest:
                        layer_norm(0, 0, 0)
                    for z in range(3):
                        for k in range(KC):
                            n = z * KC + k
                            act.wait_ge(*at(proj, n + 1))
                            if z:
                                act.wait_ge(*at(px_free, (z - 1) * KC + k + 1))
                            act.activation(PX[:, k, :, PAST:], bank[2 + n % 2][:, :].rearrange("p (b t) -> p b t", b=B),
                                           ACT.Identity, bias=col("bqkv", n)).then_inc(*up(px_ok, me))
                    act.wait_ge(*at(proj, 7))
                    act.activation(betaT[:, :, :].rearrange("p b t -> p (b t)"), bank[4][0:H0, :], ACT.Sigmoid,
                                   bias=col("bbeta")[0:H0]).then_inc(*up(beta_ok, me))
                    for n in range(4):
                        act.wait_ge(*at(nrm, n + 1))
                        if n >= 2:
                            act.wait_ge(*at(v_unit, n - 1))
                        act.activation(rn[:, n % 2].rearrange("p b t -> p (b t)"), bank[5 + n % 2][:, :], ACT.Sqrt)\
                            .then_inc(*up(root, me))
                        if n == 1:
                            for k in range(KC):
                                act.wait_ge(*at(conv_v, k + 1))
                                act.activation(kqv[:, 2, k], kqv[:, 2, k], ACT.Silu).then_inc(*up(v_silu, me))
                if rest:
                    for k in range(KC):
                        act.wait_ge(*at(o_sq, KC + k + 1))
                        act.activation(orn[:, k], osq[:, k], ACT.Sqrt).then_inc(*up(root, me))

                    layer_norm(0, 0, 2)
                    act.wait_ge(*at(logit_sub, 1))
                    act.activation(lg[:, 1], lg[:, 0], ACT.Exp).then_inc(*up(exp_ok, me))
                    for i in range(TILES0):
                        act.wait_ge(*at(gate_mm, i + 1))
                        if i >= 2:
                            act.wait_ge(*at(hid0_ok, i - 1))
                        act.activation(sg0[:, i % 2].rearrange("p b t -> p (b t)"), bank[3 * (i % 2)][:, :], ACT.Silu)\
                            .then_inc(*up(sg_ok, me))

                    layer_norm(1, 1, 0)
                    for k in range(KC):
                        act.wait_ge(*at(u_mm, k + 1))
                        act.activation(uT[:, k].rearrange("p b t -> p (b t)"), bank[2 + k][:, :], ACT.Silu,
                                       bias=col("b_in", k)).then_inc(*up(u_ok, me))
                    for hg in range(HG):
                        for c in range(6):
                            n = hg * 6 + c
                            act.wait_ge(*at(plane_mm, n + 1))
                            dst = TT[:, c, 0:NT] if c < 2 \
                                else (Q3[:, 1], Q3[:, 2], K2[:, 0], K2[:, 1])[c - 2].rearrange("p b t -> p (b t)")
                            if hg and c == 0:
                                act.wait_ge(*at(y_mm, 2 * hg))
                            if hg and c == 4:
                                act.wait_ge(*at(kt_mm, B * hg))
                            act.activation(dst, bank[n % 4][:, :], ACT.Identity, bias=col("b_qka", n))\
                                .then_inc(*up(plane_ok, me))
                            if c == 3:
                                act.wait_ge(*at(mag_ok, hg + 1))
                                act.activation(t2[:, 0], t1[:, 0], ACT.Sqrt).then_inc(*up(mag_root, me))
                        settle()
                        act.wait_ge(*at(zeroed, 2))
                        for lev in range(LEVELS):
                            m = 1 << lev
                            for bp in range(2):
                                u = (hg * LEVELS + lev) * 2 + bp
                                if lev:
                                    act.wait_ge(*at(k_ready, u - 1))
                                if u >= 2:
                                    act.wait_ge(*at(scored, 2 * (u - 1)))
                                for r in range(2):
                                    for h in range(HP):
                                        src = K2[32 * h:32 * h + 32, r, 2 * bp:2 * bp + 2]
                                        dst = Kx[32 * h:32 * h + 32, r, h, 2 * bp:2 * bp + 2]
                                        if lev:
                                            half = "p b (n two m) -> p (b n) two m"
                                            src = src.rearrange(half, two=2, m=m // 2)[:, :, 0]
                                            dst = dst.rearrange(half, two=2, m=m // 2)[:, :, 0]
                                        ins_ = act.activation(dst, src, ACT.Copy)
                                ins_.then_inc(*up(kx_ready, me))
                            if lev == 0:
                                act.wait_ge(*at(diag_mm, hg + 1))
                                act.activation(diag[:, :, :, :].rearrange("p b h r -> p (b h r)"),
                                               bank[6][:, 0:B * HP * 2], ACT.Copy).then_inc(*up(diag_ok, me))
                                for h in range(HP):
                                    for r in range(2):
                                        act.activation(Hx[32 * h:32 * h + 32, :, r, h],
                                                       H3[32 * h:32 * h + 32, hg, :, 1 - r:3 - r]
                                                       .rearrange("p b r e -> p b (r e)"), ACT.Copy)\
                                           .then_inc(*up(hx_ok, me))
                        for j in range(2):
                            act.wait_ge(*at(y_mm, 2 * hg + j + 1))
                            act.activation(y2T[:, 2 * hg + j].rearrange("p b t -> p (b t)"), bank[4 + j][:, :], ACT.Copy)\
                                .then_inc(*up(y2_ok, me))
                        for b in range(B):
                            act.wait_ge(*at(kt_mm, hg * B + b + 1))
                            act.activation(KT[:, b].rearrange("p r c -> p (r c)"), bank[b][:, 0:2 * P], ACT.Copy)\
                                .then_inc(*up(kt_ok, me))
                    for k in range(KC):
                        act.wait_ge(*at(y3_mm, k + 1))
                        act.activation(uT[:, k].rearrange("p b t -> p (b t)"), bank[k][:, :], ACT.Silu,
                                       bias=col("b_y", k)).then_inc(*up(y3_ok, me))

                    layer_norm(2, 1, 2)
                    act.wait_ge(*at(rt_var, 1))
                    act.activation(rs[:, 1], rs[:, 0], ACT.Sqrt).then_inc(*up(rt_root, me))
                    act.wait_ge(*at(rt_gap, 1))
                    act.activation(rs[:, 11], rs[:, 10], ACT.Exp).then_inc(*up(rt_exp, me))
                    for e in range(E1):
                        if nxt and e == E1 - 2:
                            norm_root(3)
                        for t in range(HT1):
                            n = e * HT1 + t
                            act.wait_ge(*at(h1_mm, n + 1))
                            if e >= 2:
                                act.wait_ge(*at(down_mm, 2 * (e - 1)))
                            act.activation(hid1[:, e % 2, t].rearrange("p b t -> p (b t)"), bank[n % 4][:, :], ACT.Gelu,
                                           bias=col("b1", n)).then_inc(*up(hid1_ok, me))
                if nxt:
                    if rest:
                        norm_modulate(3, 0, 0)
                    else:
                        layer_norm(1, 0, 0)
                settle()
                top_up(act, [ln_root, hT_ok, px_ok, beta_ok, root, v_silu, exp_ok, sg_ok, u_ok, plane_ok, mag_root,
                             hx_ok, diag_ok, kx_ready, y2_ok, kt_ok, y3_ok, rt_root, rt_exp, hid1_ok])
                act.sem_inc(started.handle, 1)

            turns(act, turn)

        @block.vector
        def _(dve):
            me = "dve"

            NTAB = 16 * (len(TABLES) + 3 + HG * B)
            steps = [0]

            def once(ins_):
                steps[0] += 1
                ins_.then_inc(mod_rows_taken.handle, 1)
                dve.wait_ge(mod_rows_taken.handle, steps[0])

            once(dve.memset(past[:, :, :, :], 0.0))
            once(dve.memset(S0[:, :, :], 0.0))
            dve.wait_ge(tables_in.handle, NTAB)
            once(dve.tensor_scalar(H3[:, :, :, 0].rearrange("p g b e -> p (g b) e"),
                                   H3[:, :, :, 2].rearrange("p g b e -> p (g b) e"), -1.0, None, ALU.mult))
            esq = arena[:, 4096:4096 + KC * E1].rearrange("p (k e) -> p k e", k=KC)
            dve.tensor_tensor(esq, w_emb[:, :, :], w_emb[:, :, :], ALU.mult).then_inc(emb_sq.handle, 1)
            dve.wait_ge(silu_done.handle, 1)
            c_wide = arena[:, 0:2 * KC * B * P].rearrange("p (a j) -> p a j", j=P)
            once(dve.memset(c_wide, 1.0))
            dve.tensor_tensor(c_wide, c_wide, silu_c[:, :, :, :].rearrange("p a k b -> p (a k b)").unsqueeze(2)
                              .to_broadcast([P, 2 * KC * B, P]), ALU.mult).then_inc(emb_sq.handle, 1)
            dve.wait_ge(mod_cols.handle, 1)
            once(dve.tensor_copy(shift_scale[:, :, :, :, :].rearrange("p a w k b -> p (a w k b)"), bank[0][:, 0:64]))
            for blk in range(2):
                for w in (1, 3):
                    v = shift_scale[:, blk, w].rearrange("p k b -> p (k b)")
                    once(dve.tensor_scalar(v, v, 1.0, None, ALU.add))
            dve.wait_ge(emb_root.handle, 1)
            once(dve.tensor_scalar(emb_rnorm[:, :], emb_rnorm[:, :], 1e-8, None, ALU.add))
            once(dve.reciprocal(emb_rnorm[:, :], emb_rnorm[:, :]))
            dve.sem_inc(mod_cols.handle, 1)
            half_t = arena[:, 8192:8192 + 512]
            for i in range(8):
                g = gates[:, i // 4, (i // 2) % 2, 2 * (i % 2):2 * (i % 2) + 2].rearrange("p b d -> p (b d)")
                dve.wait_ge(mod_rows.handle, i + 1)
                once(dve.tensor_scalar(half_t, bank[i][:, :], 0.0, 2.0, ALU.is_ge, ALU.mult))
                once(dve.tensor_scalar(g, bank[i][:, :], -1.0, 0.25, ALU.mult, ALU.max))
                once(dve.tensor_tensor(g, g, bank[i][:, :], ALU.max))
                once(dve.scalar_tensor_tensor(g, half_t, -1.0, g, ALU.add, ALU.mult))
            dve.sem_inc(started.handle, 1)


            def turn(seg, rest, nxt):
                def at(s, k):
                    return s.handle, (seg + 1) * s.stride + k

                def settle():
                    s = last[me]
                    dve.wait_ge(s.handle, (seg + 1) * s.stride + s.count)

                scanned = [0]
                scan_open = [False]

                def step(ins_):
                    ins_.then_inc(*up(dve_step, me))
                    if scan_open[0] and scanned[0] < len(SCAN_ORDER):
                        scan_instruction()
                    settle()

                def norm_sums(n, rows_=X):
                    if rows_ is not X:
                        dve.wait_ge(*at(x_next_in, 16 if n in (0, 3) else 32))
                    if me in last:
                        settle()
                    for b in range(B):
                        ins_ = dve.bn_stats(ln_stats[:, b, :], rows_[:, b, :])
                    step(ins_)
                    dve.sem_inc(passed.handle, 1)
                    for b in range(B):
                        ins_ = dve.bn_aggr(ln_mv[:, b, :], ln_stats[:, b, :])
                    step(ins_)
                    dve.tensor_scalar(ln_var[:, :], ln_mv[:, :, 1], 1e-5, None, ALU.add).then_inc(*up(ln_var_ok, me))

                def norm_rows(n, rows_=X):
                    dve.wait_ge(*at(ln_root, n + 1))
                    step(dve.reciprocal(ln_rstd[:, :], ln_std[:, :]))
                    for b in range(B):
                        ins_ = dve.tensor_scalar(xn[:, b, :], rows_[:, b, :], ln_mv[:, b, 0:1], ln_rstd[:, b:b + 1],
                                                 ALU.subtract, ALU.mult)
                    ins_.then_inc(*up(xn_ok, me))

                def layer_norm(n, rows_=X):
                    norm_sums(n, rows_)
                    norm_rows(n, rows_)

                def residual(n, banks, blk, which, bias):
                    for j in range(2):
                        two = slice(2 * j, 2 * j + 2)
                        dve.wait_ge(*at(res, 2 * n + j + 1))
                        y = bank[banks[j]][:, :].rearrange("p (b d) -> p b d", b=2)
                        g = gates[:, blk, which, two]
                        if bias is None:
                            step(dve.tensor_tensor(xn[:, two], y, g, ALU.mult))
                        else:
                            step(dve.tensor_tensor(xn[:, two], y, row(bias).unsqueeze(1).to_broadcast([P, 2, D]),
                                                   ALU.add))
                            step(dve.tensor_tensor(xn[:, two], xn[:, two], g, ALU.mult))
                        dve.tensor_tensor(X[:, two], X[:, two], xn[:, two], ALU.add).then_inc(*up(x_done, me))

                dve.wait_ge(seg_open.handle, seg + 2)

                done = 4 if nxt else 0

                def scan_instruction():
                    t, name = SCAN_ORDER[scanned[0]]

                    def after(position, producer):
                        dve.wait_ge(*at(scan_step, SCAN_ORDER.index((position, producer)) + 1))

                    def wide_k(position, z=0):
                        return KQ[:, z, :, position].unsqueeze(1).to_broadcast([P, EV, HD0])

                    if name == "k*S":
                        if t > 0:
                            after(t - 1, "S")
                        ins_ = dve.tensor_tensor(prod[:, 0], S0[:, :, :], wide_k(t + 1), ALU.mult)
                    elif name == "q*S":
                        if t > 0:
                            after(t - 1, "q.S")
                        ins_ = dve.tensor_tensor(prod[:, 1], S0[:, :, :], wide_k(t, 1), ALU.mult)
                    elif name == "k.S":
                        after(t, "k*S")
                        ins_ = dve.tensor_reduce(kS[:, t % 2], prod[:, 0], AX.X, ALU.add)
                    elif name == "q.S":
                        after(t, "q*S")
                        ins_ = dve.tensor_reduce(q_S[:, t], prod[:, 1], AX.X, ALU.add)
                    elif name == "open delta":
                        after(t, "k.S")
                        ins_ = dve.scalar_tensor_tensor(delta[:, t + 1], kS[:, t % 2], nbeta[:, t + 1:t + 2],
                                                        V0[:, :, t + 1], ALU.mult, ALU.add)
                    elif name == "delta":
                        after(t - 1, "open delta")
                        ins_ = dve.scalar_tensor_tensor(delta[:, t], delta[:, t - 1], nbeta_kk[:, t:t + 1],
                                                        delta[:, t], ALU.mult, ALU.add)
                    elif name == "k*delta":
                        after(t, "delta") if t else after(-1, "open delta")
                        ins_ = dve.tensor_tensor(outer[:, :, :], delta[:, t].unsqueeze(2).to_broadcast([P, EV, HD0]),
                                                 wide_k(t), ALU.mult)
                    else:
                        after(t, "k*delta")
                        ins_ = dve.tensor_tensor(S0[:, :, :], S0[:, :, :], outer[:, :, :], ALU.add)
                    ins_.then_inc(*up(scan_step))
                    scanned[0] += 1

                def scan(n):
                    if nxt:
                        for _ in range(min(n * SCAN_PARTS, len(SCAN_ORDER) - scanned[0])):
                            scan_instruction()

                def open_scan():
                    dve.wait_ge(*at(beta_in, beta_in.stride))
                    dve.wait_ge(*at(v_scan, v_scan.stride))
                    step(dve.tensor_tensor(V0[:, :, :], V0[:, :, :], beta_scan[:, :].unsqueeze(1)
                                           .to_broadcast([P, EV, SEG]), ALU.mult))
                    step(dve.tensor_scalar(nbeta[:, :], beta_scan[:, :], -1.0, None, ALU.mult))
                    dve.wait_ge(*at(k_scan, k_scan.stride))
                    step(dve.tensor_tensor(tmp_kk, KQ[:, 0, :, 1:SEG], KQ[:, 0, :, 0:SEG - 1], ALU.mult))
                    step(dve.tensor_reduce(nbeta_kk[:, 1:SEG], tmp_kk.rearrange("p d t -> p t d"), AX.X, ALU.add))
                    step(dve.tensor_tensor(nbeta_kk[:, 1:SEG], nbeta_kk[:, 1:SEG], nbeta[:, 1:SEG], ALU.mult))
                    dve.wait_ge(*at(q_scan, q_scan.stride))
                    scan_open[0] = True

                if nxt:
                    if not rest:
                        layer_norm(0, X_next)

                if rest:
                    step(dve.tensor_tensor(tmp_dot[:, :, :], KQ[:, 0], KQ[:, 1], ALU.mult))
                    step(dve.tensor_reduce(qk_dot[:, :], tmp_dot[:, :, :].rearrange("p d t -> p t d"), AX.X, ALU.add))
                    step(dve.tensor_tensor(delta[:, :, :], delta[:, :, :], qk_dot[:, :].unsqueeze(2)
                                           .to_broadcast([P, SEG, EV]), ALU.mult))
                    dve.tensor_tensor(O0[:, :, :].rearrange("p e t -> p t e"), q_S[:, :, :], delta[:, :, :], ALU.add)\
                       .then_inc(*up(o0_ok, me))

                if nxt:
                    for z in range(3):
                        for k in range(KC):
                            ins_ = dve.tensor_copy(PX[:, k, :, 0:PAST], past[:, z * KC + k])
                        step(ins_)
                        for i in range(TAPS):
                            for k in range(KC):
                                n = z * KC + k
                                y = kqv[:, z, k]
                                if i == 0:
                                    dve.wait_ge(*at(px_ok, n + 1))
                                    ins_ = dve.tensor_scalar(y, PX[:, k, :, 0:SEG], col("w_conv", 4 * n),
                                                             col("bqkv_conv", n), ALU.mult, ALU.add)
                                else:
                                    dve.wait_ge(*at(dve_step, dve_step.count - 1))
                                    ins_ = dve.scalar_tensor_tensor(y, PX[:, k, :, i:i + SEG], col("w_conv", 4 * n + i),
                                                                    y, ALU.mult, ALU.add)
                                ins_.then_inc(*up(dve_step, me))
                        settle()
                        for k in range(KC):
                            n = z * KC + k
                            dve.tensor_copy(past[:, n], PX[:, k, :, SEG:]).then_inc(*up(px_free, me))
                            if z < 2:
                                if z:
                                    dve.wait_ge(*at(nrm, k + 1))
                                dve.tensor_tensor(sq[:, k], kqv[:, z, k], kqv[:, z, k], ALU.mult)\
                                   .then_inc(*up(k_sq, me))
                            else:
                                dve.sem_inc(*up(conv_v))
                    for z in range(2):
                        for k in range(KC):
                            n = z * KC + k
                            dve.wait_ge(*at(root, n + 1))
                            step(dve.tensor_scalar(rn[:, k], rn[:, k], 1e-6, None, ALU.add))
                            step(dve.reciprocal(rn[:, k], rn[:, k]))
                            dve.tensor_tensor(kqv[:, z, k], kqv[:, z, k], rn[:, k], ALU.mult)\
                               .then_inc(*up((k_unit, q_unit)[z], me))
                            if z == 0:
                                dve.wait_ge(*at(v_silu, k + 1))
                                dve.tensor_tensor(kqv[:, 2, k], kqv[:, 2, k], rn[:, k], ALU.mult)\
                                   .then_inc(*up(v_unit, me))
                if rest:
                    dve.wait_ge(*at(o_in, 16))
                    for k in range(KC):
                        dve.tensor_tensor(osq[:, k], oT[:, k], oT[:, k], ALU.mult).then_inc(*up(o_sq, me))
                    for k in range(KC):
                        dve.wait_ge(*at(nrm, done + 1 + k))
                        dve.tensor_scalar(osq[:, k].rearrange("p b t -> p (b t)"), bank[5 + k][:, :], 1.0 / HD0, 1e-6,
                                          ALU.mult, ALU.add).then_inc(*up(o_sq, me))
                    for k in range(KC):
                        dve.wait_ge(*at(root, done + 1 + k))
                        step(dve.reciprocal(orn[:, k], orn[:, k]))
                        dve.scalar_tensor_tensor(oT[:, k], oT[:, k], col("norm_w"), orn[:, k], ALU.mult, ALU.mult)\
                           .then_inc(*up(o_norm_ok, me))
                    dve.wait_ge(*at(x_in, 16))
                    residual(0, (2, 3), 0, 0, "bo")

                    layer_norm(0)

                    def wide(v, n):
                        return v.unsqueeze(2).to_broadcast([P, B, n])

                    def pick(best, hot, scores, tie, rev, s1, s2, m):
                        n = rev.shape[-1]
                        step(dve.tensor_reduce(best, scores, AX.X, ALU.max))
                        step(dve.tensor_tensor(s1, scores, wide(best, n), ALU.is_equal))
                        if tie is not None:
                            step(dve.tensor_scalar(s1, s1, 1e30, -1e30, ALU.mult, ALU.add))
                            step(dve.tensor_tensor(s1, s1, tie, ALU.add))
                            step(dve.tensor_reduce(m, s1, AX.X, ALU.max))
                            step(dve.tensor_tensor(s1, s1, wide(m, n), ALU.is_equal))
                        step(dve.tensor_tensor(s2, s1, rev.unsqueeze(1).to_broadcast([P, B, n]), ALU.mult))
                        step(dve.tensor_reduce(m, s2, AX.X, ALU.max))
                        step(dve.tensor_tensor(hot, s2, wide(m, n), ALU.is_equal))

                    def hidden_tile(i):
                        h = hid0[:, i].rearrange("p b t -> p (b t)")
                        dve.wait_ge(*at(sg_ok, i + 1))
                        dve.wait_ge(*at(up_mm, i + 1))
                        ins_ = dve.tensor_tensor(h, sg0[:, i % 2].rearrange("p b t -> p (b t)"),
                                                 bank[3 * (i % 2) + 1][:, :], ALU.mult)
                        if i >= SHARED_TILES:
                            step(ins_)
                            ins_ = dve.tensor_tensor(h, h, bank[3 * (i % 2) + 2][:, :], ALU.mult)
                        ins_.then_inc(*up(hid0_ok, me))

                    dve.wait_ge(*at(router, 1))
                    logits = bank[7][:, 0:B * E0].rearrange("p (b e) -> p b e", b=B)
                    step(dve.tensor_reduce(sm[:, 0], logits, AX.X, ALU.max))
                    dve.tensor_tensor(lg[:, 0], logits, wide(sm[:, 0], E0), ALU.subtract).then_inc(*up(logit_sub, me))
                    dve.wait_ge(*at(exp_ok, 1))
                    step(dve.tensor_reduce(sm[:, 1], lg[:, 1], AX.X, ALU.add))
                    step(dve.reciprocal(sm[:, 2], sm[:, 1]))
                    step(dve.tensor_tensor(lg[:, 2], lg[:, 1], wide(sm[:, 2], E0), ALU.mult))
                    pick(sm[:, 3], lg[:, 3], lg[:, 2], None, const("rev16"), lg[:, 4], lg[:, 5], sm[:, 4])
                    hidden_tile(0)
                    step(dve.scalar_tensor_tensor(lg[:, 6].rearrange("p b e -> p (b e)"),
                                                  lg[:, 3].rearrange("p b e -> p (b e)"), -4.0,
                                                  lg[:, 2].rearrange("p b e -> p (b e)"), ALU.mult, ALU.add))
                    pick(sm[:, 5], lg[:, 7], lg[:, 6], None, const("rev16"), lg[:, 4], lg[:, 5], sm[:, 4])
                    hidden_tile(1)
                    step(dve.tensor_tensor(sm[:, 6], sm[:, 3], sm[:, 5], ALU.add))
                    step(dve.tensor_scalar(sm[:, 6], sm[:, 6], 1e-9, None, ALU.add))
                    step(dve.reciprocal(sm[:, 7], sm[:, 6]))
                    step(dve.tensor_tensor(lg[:, 8], lg[:, 3], lg[:, 7], ALU.add))
                    step(dve.tensor_tensor(lg[:, 8], lg[:, 8], lg[:, 2], ALU.mult))
                    dve.tensor_tensor(lg[:, 9], lg[:, 8], wide(sm[:, 7], E0), ALU.mult).then_inc(*up(comb_ok, me))
                    dve.wait_ge(*at(comb_tr, 1))
                    dve.tensor_copy(combT[:, :, :].rearrange("p b t -> p (b t)"), bank[6][0:E0, :])\
                       .then_inc(*up(comb_copied, me))
                    if nxt:
                        open_scan()
                    for i in range(SHARED_TILES, TILES0):
                        hidden_tile(i)
                        scan(SCAN_TILE)
                    residual(1, (6, 7), 0, 1, None)

                    layer_norm(1)

                    def values():
                        for b in range(B):
                            dve.wait_ge(*at(v_mm, b + 1))
                            step(dve.tensor_tensor(V3[:, b, :, 1:3, :].rearrange("p h r e -> p h (r e)"),
                                                   bank[4 + b][:, :].rearrange("p (h j) -> p h j", h=H1),
                                                   row("b_v").rearrange("p (h j) -> p h j", h=H1), ALU.add))
                            dve.tensor_scalar(V3[:, b, :, 0, :], V3[:, b, :, 2, :], -1.0, None, ALU.mult)\
                               .then_inc(*up(v3_ok, me))

                    flat = "p r b t -> p r (b t)"
                    for hg in range(HG):
                        q2 = Q3[:, 1:3].rearrange(flat)
                        k2 = K2[:, :].rearrange(flat)
                        a2 = TT[:, :, 0:NT]

                        def twice(v):
                            return v.unsqueeze(1).to_broadcast([P, 2, v.shape[-1]])

                        scan_open[0] = False
                        dve.wait_ge(*at(plane_ok, 6 * hg + 2))
                        step(dve.tensor_tensor(t1[:, :, :], a2, a2, ALU.mult))
                        dve.tensor_tensor(t1[:, 0], t1[:, 0], t1[:, 1], ALU.add).then_inc(*up(mag_ok, me))
                        settle()
                        step(dve.tensor_scalar(t1[:, 1], t1[:, 0], 1.0, None, ALU.add))
                        step(dve.reciprocal(t1[:, 1], t1[:, 1]))
                        if hg == 0:
                            values()
                        dve.wait_ge(*at(mag_root, hg + 1))
                        step(dve.tensor_tensor(t1[:, 0], t2[:, 0], t1[:, 1], ALU.mult))
                        dve.tensor_tensor(a2, a2, twice(t1[:, 0]), ALU.mult).then_inc(*up(a_ok, me))
                        settle()
                        dve.wait_ge(*at(plane_ok, 6 * hg + 4))
                        step(dve.tensor_tensor(t1[:, :, :], q2, twice(TT[:, 0, 0:NT]), ALU.mult))
                        step(dve.tensor_scalar(Q3[:, 0], Q3[:, 2], -1.0, None, ALU.mult))
                        step(dve.tensor_tensor(t2[:, :, :], Q3[:, 0:2].rearrange(flat), twice(TT[:, 1, 0:NT]), ALU.mult))
                        dve.wait_ge(*at(pairs_ok, hg + 1))
                        step(dve.tensor_tensor(q2, t1[:, :, :], t2[:, :, :], ALU.add))
                        for bp in range(2):
                            two = slice(2 * bp, 2 * bp + 2)
                            dve.tensor_scalar(Q3[:, 0, two], Q3[:, 2, two], -1.0, None, ALU.mult).then_inc(*up(q_ready, me))
                        scan_open[0] = nxt
                        off = 0
                        for lev in range(LEVELS):
                            m = 1 << lev
                            nb = SEG // (2 * m)
                            n = NT >> lev
                            w = TT[:, :, off:off + n].rearrange("p r (j two) -> p r j two", two=2)
                            wider = TT[:, :, off + n:off + n + n // 2]
                            ta, tb = t2[:, :, 0:n // 2], t2[:, :, 256:256 + n // 2]
                            dve.tensor_tensor(ta, w[:, :, :, 0], twice(w[:, 0, :, 1]), ALU.mult)
                            step(dve.tensor_tensor(tb, w[:, :, :, 0], twice(w[:, 1, :, 1]), ALU.mult))
                            dve.tensor_tensor(wider[:, 0], ta[:, 0], tb[:, 1], ALU.subtract)
                            dve.tensor_tensor(wider[:, 1], ta[:, 1], tb[:, 0], ALU.add).then_inc(*up(a_ok, me))
                            settle()
                            for bp in range(2):
                                u = (hg * LEVELS + lev) * 2 + bp
                                for i in range(2):
                                    b = 2 * bp + i
                                    dve.wait_ge(*at(scored, 2 * u + i + 1))
                                    if lev == 0:
                                        dve.wait_ge(*at(score_init, B * hg + b + 1))
                                    dve.sem_inc(passed.handle, 1)
                                    dst = score[:, b].rearrange("p h r (n two m) -> p (h r) n two m", two=2, m=m)[:, :, :, 1]
                                    dve.copy_predicated(
                                        dst,
                                        masks[:, lev].rearrange("p (n m) -> p n m", m=m).unsqueeze(1)
                                        .to_broadcast([P, 2 * HP, nb, m]),
                                        bank[b][:, :].rearrange("p (g n m) -> p g n m", g=2 * HP, m=m))\
                                       .then_inc(*up(masked, me))
                                n = 2 * nb
                                half = "p r b (n two m) -> p r (b n) two m"
                                two = slice(2 * bp, 2 * bp + 2)
                                Tb = TT[:, :, off + bp * 2 * n:off + (bp + 1) * 2 * n]\
                                    .rearrange("p r (n two) -> p r n two", two=2)[:, :, :, 0]

                                def over(v):
                                    return v.unsqueeze(1).unsqueeze(3).to_broadcast([P, 2, n, m])

                                def tmp(t):
                                    return t[:, :, 0:P].rearrange("p r (n m) -> p r n m", m=m)

                                q_hi = Q3[:, 1:3, two].rearrange(half, two=2, m=m)[:, :, :, 1]
                                q_lo = Q3[:, 0:2, two].rearrange(half, two=2, m=m)[:, :, :, 1]
                                dve.tensor_tensor(tmp(t1), q_hi, over(Tb[:, 0]), ALU.mult).then_inc(*up(dve_step, me))
                                step(dve.tensor_tensor(tmp(t2), q_lo, over(Tb[:, 1]), ALU.mult))
                                step(dve.tensor_tensor(q_hi, tmp(t1), tmp(t2), ALU.add))
                                dve.tensor_scalar(q_lo[:, 0], q_hi[:, 1], -1.0, None, ALU.mult).then_inc(*up(q_ready, me))
                            off += NT >> lev
                        dve.wait_ge(*at(r_mm, hg + 1))
                        settle()
                        for b in range(B):
                            old = t1[:, 0, 64 * b:64 * b + 64]
                            step(dve.scalar_tensor_tensor(old, H3[:, hg, b, 1:3].rearrange("p r e -> p (r e)"),
                                                          TT[:, 0, off + b:off + b + 1],
                                                          bank[7][:, 64 * b:64 * b + 64], ALU.mult, ALU.add))
                            step(dve.scalar_tensor_tensor(t1[:, 1, 64 * b:64 * b + 64],
                                                          H3[:, hg, b, 0:2].rearrange("p r e -> p (r e)"),
                                                          TT[:, 1, off + b:off + b + 1], old, ALU.mult, ALU.add))
                        step(dve.tensor_copy(H3[:, hg, :, 1:3].rearrange("p b r e -> p b (r e)"),
                                             t1[:, 1, 0:256].rearrange("p (b j) -> p b j", b=B)))
                        dve.tensor_scalar(H3[:, hg, :, 0], H3[:, hg, :, 2], -1.0, None, ALU.mult)\
                           .then_inc(*up(state_ok, me))
                    residual(2, (2, 3), 1, 0, "b_out")

                    layer_norm(2)
                    dve.wait_ge(*at(hT_ok, 3))
                    dve.tensor_tensor(sqh[:, :, :, :], hT[:, :, :, :], hT[:, :, :, :], ALU.mult).then_inc(*up(hsq_ok, me))
                    dve.wait_ge(*at(router, 2))
                    dve.tensor_copy(rs[:, 0], bank[7][:, 32:36]).then_inc(*up(rt_var, me))
                    sim = rt[:, 0]
                    step(dve.tensor_copy(sim, bank[7][:, 0:B * E1].rearrange("p (b e) -> p b e", b=B)))
                    step(dve.tensor_scalar(rt[:, 1], sim, -1.0, None, ALU.mult))
                    pick(rs[:, 2], rt[:, 2], rt[:, 1], None, const("up8"), rt[:, 3], rt[:, 4], rs[:, 3])
                    dve.wait_ge(*at(rt_root, 1))
                    step(dve.tensor_scalar(rs[:, 4], rs[:, 1], 1e-8, None, ALU.add))
                    step(dve.reciprocal(rs[:, 5], rs[:, 4]))
                    step(dve.tensor_tensor(rt[:, 5], sim, emb_rnorm[:, :].unsqueeze(1).to_broadcast([P, B, E1]), ALU.mult))
                    step(dve.tensor_tensor(rt[:, 5], rt[:, 5], wide(rs[:, 5], E1), ALU.mult))
                    step(dve.tensor_scalar(rt[:, 6], row("cache").unsqueeze(1).to_broadcast([P, B, E1]), 0.1, None,
                                           ALU.mult))
                    step(dve.tensor_tensor(rt[:, 5], rt[:, 5], rt[:, 6], ALU.add))

                    def flat2(v):
                        return v.rearrange("p b e -> p (b e)")

                    step(dve.scalar_tensor_tensor(flat2(rt[:, 5]), flat2(rt[:, 2]), -1e30, flat2(rt[:, 5]),
                                                  ALU.mult, ALU.add))
                    pick(rs[:, 6], rt[:, 7], rt[:, 5], sim, const("rev8"), rt[:, 3], rt[:, 4], rs[:, 3])
                    step(dve.scalar_tensor_tensor(flat2(rt[:, 8]), flat2(rt[:, 7]), -1e30, flat2(rt[:, 5]),
                                                  ALU.mult, ALU.add))
                    pick(rs[:, 7], rt[:, 9], rt[:, 8], sim, const("rev8"), rt[:, 3], rt[:, 4], rs[:, 3])
                    dve.tensor_tensor(rs[:, 10], rs[:, 7], rs[:, 6], ALU.subtract).then_inc(*up(rt_gap, me))
                    dve.wait_ge(*at(rt_exp, 1))
                    step(dve.tensor_scalar(rs[:, 12], rs[:, 11], 1.0, None, ALU.add))
                    step(dve.reciprocal(rs[:, 13], rs[:, 12]))
                    step(dve.tensor_tensor(rs[:, 14], rs[:, 11], rs[:, 13], ALU.mult))
                    step(dve.tensor_tensor(rt[:, 7], rt[:, 7], wide(rs[:, 13], E1), ALU.mult))
                    step(dve.tensor_tensor(rt[:, 9], rt[:, 9], wide(rs[:, 14], E1), ALU.mult))
                    dve.tensor_tensor(rt[:, 10], rt[:, 7], rt[:, 9], ALU.add).then_inc(*up(comb1_ok, me))
                    dve.wait_ge(*at(comb_tr, 2))
                    dve.tensor_copy(combT1[:, :, :].rearrange("p b t -> p (b t)"), bank[6][0:E1, :])\
                       .then_inc(*up(comb1_copied, me))
                    for j in range(2):
                        dve.wait_ge(*at(down_bias, j + 1))
                        dve.tensor_copy(acc[:, 2 * j:2 * j + 2].rearrange("p b d -> p (b d)"), bank[6 + j][:, :])\
                           .then_inc(*up(acc_ok, me))
                    for e in range(E1):
                        if nxt and e == E1 - 4:
                            norm_sums(3, X_next)
                        if nxt and e == E1 - 3:
                            norm_rows(3, X_next)
                        scan(SCAN_EXPERT)
                        settle()
                        for j in range(2):
                            dve.wait_ge(*at(down_mm, 2 * e + j + 1))
                            for i in range(2):
                                b = 2 * j + i
                                ins_ = dve.scalar_tensor_tensor(acc[:, b], bank[4 + 2 * (e % 2) + j][:, i * D:(i + 1) * D],
                                                                rt[:, 10, b, e:e + 1], acc[:, b], ALU.mult, ALU.add)
                            ins_.then_inc(*up(acc_ok, me))
                    settle()
                    step(dve.tensor_tensor(xn[:, :, :], acc[:, :, :], gates[:, 1, 1], ALU.mult))
                    dve.tensor_tensor(X[:, :, :], X[:, :, :], xn[:, :, :], ALU.add).then_inc(*up(x_final, me))
                if nxt and not rest:
                    layer_norm(1, X_next)
                    open_scan()
                scan(SEG)
                assert scanned[0] == len(SCAN_ORDER) * nxt
                settle()
                if nxt:
                    dve.wait_ge(*at(scan_step, scan_step.count))
                top_up(dve, [scan_step, dve_step, ln_var_ok, xn_ok, px_free, k_sq, conv_v, k_unit, q_unit, v_unit, o0_ok, o_sq,
                             o_norm_ok, logit_sub, comb_ok, comb_copied, hid0_ok, x_done, mag_ok, v3_ok, a_ok,
                             q_ready, masked, state_ok, hsq_ok, rt_var, rt_gap, comb1_ok,
                             comb1_copied, acc_ok, x_final])
                dve.sem_inc(started.handle, 1)

            turns(dve, turn)

        @block.gpsimd
        def _(pool):
            me = "pool"
            pool.sem_inc(started.handle, 1)

            def turn(seg, rest, nxt):
                def at(s, k):
                    return s.handle, (seg + 1) * s.stride + k

                def settle():
                    s = last[me]
                    pool.wait_ge(s.handle, (seg + 1) * s.stride + s.count)

                def step(ins_):
                    ins_.then_inc(*up(pool_step, me))
                    settle()

                if rest:
                    pool.wait_ge(*at(ln_var_ok, 2))
                    pool.sem_inc(passed.handle, 1)
                    pool.memset(Kx[:, :, :, :, :].rearrange("p r h b t -> p (r h b t)"), 0.0).then_inc(*up(zeroed, me))
                    pool.memset(Hx[:, :, :, :, :].rearrange("p b r h j -> p (b r h j)"), 0.0).then_inc(*up(zeroed, me))
                    for hg in range(HG):
                        if hg:
                            pool.wait_ge(*at(y_mm, 2 * hg))
                        pool.wait_ge(*at(plane_ok, 6 * hg + 6))
                        pool.sem_inc(passed.handle, 1)
                        q2 = Q3[:, 1:3].rearrange("p r b t -> p r (b t)")

                        def k_part(r):
                            return K2[:, r].rearrange("p b t -> p (b t)").unsqueeze(1).to_broadcast([P, 2, NT])

                        settle()
                        pool.tensor_tensor(pair_re, q2, k_part(0), ALU.mult).then_inc(*up(pool_step, me))
                        step(pool.tensor_tensor(pair_im, q2, k_part(1), ALU.mult))
                        pool.tensor_tensor(pair_re[:, 0], pair_re[:, 0], pair_im[:, 1], ALU.subtract)\
                            .then_inc(*up(pool_step, me))
                        pool.tensor_tensor(pair_re[:, 1], pair_re[:, 1], pair_im[:, 0], ALU.add)\
                            .then_inc(*up(pairs_ok, me))
                        off = 0
                        for lev in range(LEVELS):
                            m = 1 << lev
                            n = SEG // m
                            for bp in range(2):
                                u = (hg * LEVELS + lev) * 2 + bp
                                if lev == 0:
                                    pool.wait_ge(*at(diag_ok, hg + 1))
                                    for b in (2 * bp, 2 * bp + 1):
                                        pool.tensor_tensor(score[:, b].rearrange("p h r t -> p (h r) t"),
                                                           ident.unsqueeze(1).to_broadcast([P, 2 * HP, SEG]),
                                                           diag[:, b].rearrange("p h r -> p (h r)").unsqueeze(2)
                                                           .to_broadcast([P, 2 * HP, SEG]), ALU.mult)\
                                            .then_inc(*up(score_init, me))
                                pool.wait_ge(*at(kx_ready, u + 1))
                                pool.wait_ge(*at(a_ok, hg * (LEVELS + 1) + lev + 1))
                                two = slice(2 * bp, 2 * bp + 2)
                                Tb = TT[:, :, off + bp * 2 * n:off + (bp + 1) * 2 * n]\
                                    .rearrange("p r (n two) -> p r n two", two=2)[:, :, :, 1]

                                def over(v):
                                    return v.unsqueeze(1).unsqueeze(3).to_broadcast([P, 2, n, m])

                                def tmp(t):
                                    return t[:, :, 0:P].rearrange("p r (n m) -> p r n m", m=m)

                                kk = K2[:, :, two].rearrange("p r b (n two m) -> p r (b n) two m", two=2, m=m)[:, :, :, 0]
                                settle()
                                pool.tensor_tensor(tmp(u1), kk, over(Tb[:, 0]), ALU.mult).then_inc(*up(pool_step, me))
                                step(pool.tensor_tensor(tmp(u2), kk, over(Tb[:, 1]), ALU.mult))
                                pool.tensor_tensor(kk[:, 0], tmp(u1)[:, 0], tmp(u2)[:, 1], ALU.subtract)\
                                    .then_inc(*up(pool_step, me))
                                pool.tensor_tensor(kk[:, 1], tmp(u1)[:, 1], tmp(u2)[:, 0], ALU.add)\
                                    .then_inc(*up(k_ready, me))
                            off += NT >> lev
                    settle()
                else:
                    pool.wait_ge(seg_open.handle, seg + 2)
                pool.sem_inc(passed.handle, 1)
                top_up(pool, [pool_step, zeroed, pairs_ok, score_init, k_ready])
                pool.sem_inc(started.handle, 1)

            turns(pool, turn)

        @block.tensor
        def _(pe):
            NTAB = 16 * (len(TABLES) + 3 + HG * B)
            mm = pe.matmul
            pe.wait_ge(tables_in.handle, NTAB)
            pe.wait_ge(emb_sq.handle, 2)
            esq = arena[:, 4096:4096 + KC * E1].rearrange("p (k e) -> p k e", k=KC)
            for k in range(KC):
                i_ = mm(bank[1][:, 0:E1], const("ones"), esq[:, k], start=(k == 0), stop=(k == KC - 1))
            i_.then_inc(emb_sum.handle, 1)
            for blk in range(2):
                for w, src in enumerate((0, 1, 3, 4)):
                    for kc in range(KC):
                        at_ = ((blk * 4 + w) * KC + kc) * B
                        for k in range(KC):
                            i_ = mm(bank[0][:, at_:at_ + B], wmod[blk][:, k, src * D + kc * P:src * D + kc * P + P],
                                    silu_c[:, blk, k, :], start=(k == 0), stop=(k == KC - 1))
            i_.then_inc(mod_cols.handle, 1)
            pe.wait_ge(mod_cols.handle, 2)
            c_wide = arena[:, 0:2 * KC * B * P].rearrange("p (a k b j) -> p a k b j", a=2, k=KC, b=B)
            for i in range(8):
                blk, g = i // 4, (i // 2) % 2
                for j in range(2):
                    b = 2 * (i % 2) + j
                    for k in range(KC):
                        src = (2 + 3 * g) * D
                        i_ = mm(bank[i][:, j * D:(j + 1) * D], c_wide[:, blk, k, b], wmod[blk][:, k, src:src + D],
                                start=(k == 0), stop=(k == KC - 1))
                i_.then_inc(mod_rows.handle, 1)
            pe.sem_inc(started.handle, 1)


            def turn(seg, rest, nxt):
                def at(s, k):
                    return s.handle, (seg + 1) * s.stride + k

                def rhs(t, k):
                    return t[:, k].rearrange("p b t -> p (b t)")

                def turn_rows(n):
                    pe.wait_ge(*at(xn_ok, n + 1))
                    for k in range(KC):
                        for b in range(B):
                            i_ = pe.transpose(bank[k][:, b * SEG:(b + 1) * SEG], xn[:, b, k * P:(k + 1) * P], ident)
                    i_.then_inc(*up(ln_tr))

                def layer_norm(n):
                    turn_rows(n)
                    pe.wait_ge(*at(hT_ok, n + 1))

                def channels(dst, w, cols_, src, n=KC):
                    for k in range(n):
                        i_ = mm(dst, w[:, k, cols_], rhs(src, k), start=(k == 0), stop=(k == n - 1))
                    return i_

                def tokens(banks, src, w):
                    for j in range(2):
                        for i in range(2):
                            for k in range(KC):
                                i_ = mm(bank[banks[j]][:, i * D:(i + 1) * D], src[:, k, 2 * j + i, :], w[:, k, :],
                                        start=(k == 0), stop=(k == KC - 1))
                        i_.then_inc(*up(res))

                done = 4 if nxt else 0
                pe.wait_ge(seg_open.handle, seg + 2)
                if nxt:
                    if not rest:
                        layer_norm(0)
                    for n in range(6):
                        if n >= 2:
                            pe.wait_ge(*at(px_ok, n - 1))
                        channels(bank[2 + n % 2][:, :], w_qkv, slice(n * P, (n + 1) * P), hT).then_inc(*up(proj))
                    channels(bank[4][0:H0, :], w_beta, slice(0, H0), hT).then_inc(*up(proj))
                    for n in range(4):
                        pe.wait_ge(*at(k_sq, n + 1))
                        if n >= 2:
                            pe.wait_ge(*at(root, n - 1))
                        mm(bank[5 + n % 2][:, :], const("ones16"), rhs(sq, n % 2), start=True, stop=True)\
                            .then_inc(*up(nrm))
                if rest:
                    for k in range(KC):
                        pe.wait_ge(*at(o_sq, k + 1))
                        if nxt:
                            pe.wait_ge(*at(root, 3 + k))
                        mm(bank[5 + k][:, :], const("ones16"), rhs(osq, k), start=True, stop=True).then_inc(*up(nrm))
                    pe.wait_ge(*at(o_norm_ok, KC))
                    tokens((2, 3), oT, w_o)

                    layer_norm(0)
                    for b in range(B):
                        for k in range(KC):
                            i_ = mm(bank[7][:, b * E0:(b + 1) * E0], hT[:, k, b, :], w_router[:, k, :],
                                    start=(k == 0), stop=(k == KC - 1))
                    i_.then_inc(*up(router))

                    def slot(n):
                        pe.wait_ge(*at(ring_in[n % SLOTS], 16 * (n // SLOTS + 1)))
                        return ring[:, n % SLOTS, :]

                    def spread(i):
                        mm(bank[3 * (i % 2) + 2][:, :], sel[:, i - SHARED_TILES, :], combT[:, :, :].rearrange("e b t -> e (b t)"),
                           start=True, stop=True).then_inc(*up(up_mm))

                    def turn_weights(n, src, width):
                        for b in range(B):
                            i_ = pe.transpose(bank[6][0:width, b * SEG:(b + 1) * SEG], src[:, b, :], ident)
                        i_.then_inc(*up(comb_tr))

                    for i in range(TILES0):
                        if i % 2 == 0:
                            both = slot(UP0_AT + i // 2).rearrange("p (g k c) -> p g k c", g=2, k=KC)
                        if i == SHARED_TILES + 2:
                            pe.wait_ge(*at(comb_ok, 1))
                            turn_weights(0, lg[:, 9], E0)
                            pe.wait_ge(*at(comb_copied, 1))
                            spread(i - 2)
                            spread(i - 1)
                        if i >= 2:
                            pe.wait_ge(*at(sg_ok, i - 1))
                            pe.wait_ge(*at(hid0_ok, i - 1))
                        c = slice((i % 2) * P, (i % 2 + 1) * P)
                        channels(bank[3 * (i % 2)][:, :], both[:, 0], c, hT).then_inc(*up(gate_mm))
                        i_ = channels(bank[3 * (i % 2) + 1][:, :], both[:, 1], c, hT)
                        if i < SHARED_TILES:
                            i_.then_inc(*up(up_mm))
                        elif i >= SHARED_TILES + 2:
                            spread(i)
                    pe.wait_ge(*at(hid0_ok, TILES0))
                    downs = [slot(DOWN0_AT + d).rearrange("p (t c) -> p t c", c=D) for d in range(len(DOWN0))]
                    for b in range(B):
                        for d, (first, end) in enumerate(DOWN0):
                            for i in range(first, end):
                                i_ = mm(bank[6 + b // 2][:, (b % 2) * D:(b % 2 + 1) * D], hid0[:, i, b, :],
                                        downs[d][:, i - first, :], start=(i == 0), stop=(i == TILES0 - 1))
                            if b == B - 1 and d + 1 < len(DOWN0):
                                i_.then_inc(*up(down0_used))
                        if b % 2:
                            i_.then_inc(*up(res))

                    layer_norm(1)
                    for k in range(KC):
                        channels(bank[2 + k][:, :], w_in, slice(k * P, (k + 1) * P), hT).then_inc(*up(u_mm))
                    pe.wait_ge(*at(u_ok, KC))
                    for hg in range(HG):
                        if hg:
                            pe.wait_ge(*at(kt_ok, B * hg))
                        for c in range(6):
                            n = hg * 6 + c
                            if c >= 4:
                                pe.wait_ge(*at(plane_ok, n - 3))
                            four = slot(QKA_AT + n // 4).rearrange("p (k c) -> p k c", k=KC)
                            channels(bank[n % 4][:, :], four, slice((n % 4) * P, (n % 4 + 1) * P), uT)\
                                .then_inc(*up(plane_mm))
                        if hg == 0:
                            w_v = slot(V_AT).rearrange("p (k c) -> p k c", k=KC)
                            for b in range(B):
                                for k in range(KC):
                                    i_ = mm(bank[4 + b][:, :], uT[:, k, b, :], w_v[:, k, :], start=(k == 0), stop=(k == KC - 1))
                                i_.then_inc(*up(v_mm))
                            pe.wait_ge(*at(v3_ok, B))
                        pe.wait_ge(*at(pairs_ok, hg + 1))
                        d6 = bank[6][:, 0:B * HP * 2].rearrange("p (b h r) -> p b h r", b=B, r=2)
                        for b in range(B):
                            for r in range(2):
                                i_ = mm(d6[:, b, :, r], pair_re[:, r, b * SEG:(b + 1) * SEG], const("head_of"),
                                        start=True, stop=True)
                        i_.then_inc(*up(diag_mm))
                        for lev in range(LEVELS):
                            m = 1 << lev
                            for bp in range(2):
                                u = (hg * LEVELS + lev) * 2 + bp
                                pe.wait_ge(*at(kx_ready, u + 1))
                                pe.wait_ge(*at(q_ready, hg * 16 + lev * 2 + bp + 1))
                                if lev:
                                    pe.wait_ge(*at(masked, 2 * (u - 1)))
                                for b in (2 * bp, 2 * bp + 1):
                                    for h in range(HP):
                                        for r in range(2):
                                            qv = Q3[:, 1 - r:3 - r, b].rearrange("p r (n two m) -> p r n two m",
                                                                                 two=2, m=m)[:, :, :, 1]
                                            i_ = mm(bank[b][:, h * P:(h + 1) * P], Kx[:, r, h, b, :], qv,
                                                    start=(r == 0), stop=(r == 1))
                                    i_.then_inc(*up(scored))
                        pe.wait_ge(*at(hx_ok, 2 * HP * (hg + 1)))
                        pe.wait_ge(*at(q_ready, hg * 16 + 16))
                        pe.wait_ge(*at(masked, 28 * (hg + 1)))
                        for j in range(2):
                            for b in range(B):
                                y = bank[4 + j][:, b * SEG:(b + 1) * SEG]
                                for r in range(2):
                                    mm(y, Hx[:, b, r, 2 * j:2 * j + 2].rearrange("p h j -> p (h j)"),
                                       Q3[:, 1 + r, b, :], start=(r == 0), stop=False, skip_group_check=True)
                                for i in range(2):
                                    h = 2 * j + i
                                    for r in range(2):
                                        i_ = mm(y[64 * i:64 * i + 64],
                                                V3[:, b, hg * HP + h, 1 - r:3 - r, :].rearrange("p r e -> p (r e)"),
                                                score[:, b, h, r, :], start=False, stop=(r == 1), skip_group_check=True)
                            i_.then_inc(*up(y_mm))
                        pe.wait_ge(*at(k_ready, 14 * (hg + 1)))
                        for b in range(B):
                            for r in range(2):
                                i_ = pe.transpose(bank[b][:, r * P:(r + 1) * P], K2[:, r, b, :], ident)
                            i_.then_inc(*up(kt_mm))
                        if hg:
                            pe.wait_ge(*at(state_ok, hg))
                        for b in range(B):
                            pe.wait_ge(*at(kt_ok, hg * B + b + 1))
                            for h in range(HP):
                                for r in range(2):
                                    i_ = mm(bank[7][32 * h:32 * h + 32, 64 * b:64 * b + 64], KT[:, b, r, 32 * h:32 * h + 32],
                                            V3[:, b, hg * HP + h, 1 - r:3 - r, :].rearrange("p r e -> p (r e)"),
                                            start=(r == 0), stop=(r == 1))
                        i_.then_inc(*up(r_mm))
                    pe.wait_ge(*at(y2_ok, 4))
                    w_y = slot(Y_AT).rearrange("p (k c) -> p k c", c=D)
                    for k in range(KC):
                        channels(bank[k][:, :], w_y, slice(k * P, (k + 1) * P), y2T, 4).then_inc(*up(y3_mm))
                    pe.wait_ge(*at(y3_ok, KC))
                    tokens((2, 3), uT, w_out)

                    layer_norm(2)
                    for b in range(B):
                        for k in range(KC):
                            mm(bank[7][:, b * E1:(b + 1) * E1], hT[:, k, b, :], w_emb[:, k, :],
                               start=(k == 0), stop=(k == KC - 1))
                    pe.wait_ge(*at(hsq_ok, 1))
                    for b in range(B):
                        for k in range(KC):
                            i_ = mm(bank[7][:, 32 + b:33 + b], sqh[:, k, b, :], const("ones")[:, 0:1],
                                    start=(k == 0), stop=(k == KC - 1))
                    i_.then_inc(*up(router))

                    def hidden(e):
                        for t in range(HT1):
                            if t % 4 == 0:
                                w1 = slot(EXPERT_AT + EXPERT_LOADS.index((0, e, t // 4)))\
                                    .rearrange("p (k c) -> p k c", k=KC)
                            if e or t >= 4:
                                pe.wait_ge(*at(hid1_ok, e * HT1 + t - 3))
                            channels(bank[t % 4][:, :], w1, slice(t % 4 * P, (t % 4 + 1) * P), hT).then_inc(*up(h1_mm))

                    hidden(0)
                    pe.wait_ge(*at(comb1_ok, 1))
                    turn_weights(1, rt[:, 10], E1)
                    pe.wait_ge(*at(comb1_copied, 1))
                    for j in range(2):
                        for i in range(2):
                            i_ = mm(bank[6 + j][:, i * D:(i + 1) * D], combT1[:, 2 * j + i, :], b2[:, :],
                                    start=True, stop=True)
                        i_.then_inc(*up(down_bias))
                    for e in range(E1):
                        if e + 1 < E1:
                            hidden(e + 1)
                        w2 = [slot(EXPERT_AT + EXPERT_LOADS.index((1, e, half))).rearrange("p (t c) -> p t c", c=D)
                              for half in range(2)]
                        pe.wait_ge(*at(hid1_ok, HT1 * (e + 1)))
                        if nxt and e == E1 - 1:
                            turn_rows(3)
                        for j in range(2):
                            if e:
                                pe.wait_ge(*at(acc_ok, 2 * (e - 1) + j + 1))
                            for i in range(2):
                                for t in range(HT1):
                                    i_ = mm(bank[4 + 2 * (e % 2) + j][:, i * D:(i + 1) * D], hid1[:, e % 2, t, 2 * j + i, :],
                                            w2[t // 4][:, t % 4, :], start=(t == 0), stop=(t == HT1 - 1))
                            i_.then_inc(*up(down_mm))
                if nxt and not rest:
                    turn_rows(1)
                if rest:
                    pe.wait_ge(*at(down_mm, down_mm.count))
                else:
                    pe.wait_ge(*at(ln_tr, ln_tr.count))
                pe.sem_inc(passed.handle, 1)
                top_up(pe, [ln_tr, proj, nrm, res, router, comb_tr, gate_mm, up_mm, down0_used, u_mm, plane_mm, v_mm,
                            diag_mm, scored, y_mm, kt_mm, r_mm, y3_mm, h1_mm, down_mm, down_bias])
                pe.sem_inc(started.handle, 1)

            turns(pe, turn)


INPUTS = {"x": (B, L + SEG, D), "w_qkv": (P, KC, 3 * D), "w_beta": (P, KC, H0), "w_o": (P, KC, D),
          "w_router": (P, KC, E0), "w_in": (P, KC, D), "w_out": (P, KC, D), "w_emb": (P, KC, E1), "b2": (E1, D), "cols": (P, NCOLS),
          "consts": (P, NCONST), "rows": (NROWS,), "c_cols": (P, 2, KC, B), "wmod": (2, P, KC, 1536),
          "w_ring": (LOADS, P, SLOT)}


def constants():
    t = np.zeros((P, NCONST), np.float32)

    def put(name, v):
        a, n = CONSTS[name]
        t[:v.shape[0], a:a + n] = v

    p = np.arange(P)
    put("ident", np.eye(P))
    put("ones16", (p[:, None] // HD0 == p[None] // HD0) * 1.0)
    put("ones", np.ones((P, P)))
    put("head_of", (p[:, None] // HD1 == np.arange(HP)[None]) * 1.0)
    put("rev16", np.tile(16.0 - np.arange(16), (P, 1)))
    put("rev8", np.tile(8.0 - np.arange(8), (P, 1)))
    put("up8", np.tile(1.0 + np.arange(8), (P, 1)))
    masks = []
    for lev in range(LEVELS):
        m = 1 << lev
        j = np.arange(64)
        block = j // m
        masks.append((p[:, None] // (2 * m) == block[None]) & (p[:, None] % (2 * m) < m))
    put("masks", np.concatenate(masks, 1) * 1.0)
    sel = (np.arange(E0)[:, None, None] == 2 * np.arange(ROUTED0)[None, :, None] + p[None, None] // MID0) * 1.0
    put("sel", sel.reshape(E0, -1))
    return t


def kernel(**inputs):
    import concourse.bacc as bacc
    from concourse.bass_utils import run_bass_kernel_spmd

    a = {k: np.asarray(v) for k, v in inputs.items()}

    def chunks(w):
        return w.reshape(-1, P, w.shape[-1]).transpose(1, 0, 2)

    def column(v):
        return v.reshape(-1, P).T

    def planes(w):
        v = w.reshape(HG, P, 4, 2, *w.shape[1:])
        return np.stack([v[g, :, c, r] for g in range(HG) for c in (3, 0, 1) for r in range(2)])

    w_qkva, b_qkva = a["L1_attn_W_qkva"], a["L1_attn_b_qkva"]
    values = w_qkva.reshape(H1, HD1, 4, 2, D)[:, :, 2].transpose(0, 2, 1, 3).reshape(512, D)
    b_values = b_qkva.reshape(H1, HD1, 4, 2)[:, :, 2].transpose(0, 2, 1).reshape(512)
    w_y = a["L1_attn_W_y"].reshape(D, H1, HD1, 2).transpose(1, 3, 2, 0).reshape(512, D)
    conv = [a[f"L0_attn_w{z}_conv"].reshape(KC, P, TAPS).transpose(1, 0, 2).reshape(P, -1) for z in "kqv"]
    cols_ = [column(a[f"L0_attn_b{z}"]) for z in "kqv"] + [column(a[f"L0_attn_b{z}_conv"]) for z in "kqv"] + conv
    bbeta = np.zeros((P, 1), np.float32)
    bbeta[:H0, 0] = a["L0_attn_bbeta"]
    cols_ += [np.tile(a["L0_attn_norm_w"], P // HD0)[:, None], bbeta, column(a["L1_attn_b_in"]),
              planes(b_qkva).T, column(a["L1_attn_b_y"]), column(a["L1_ffn_b1"].reshape(-1))]
    h0 = np.stack([a["L1_attn_h0_re"], a["L1_attn_h0_im"]], 2).reshape(HG, P, 2, HD1).transpose(1, 0, 2, 3)

    def hidden_columns(shared, routed):
        both = [w.transpose(1, 0, 2).reshape(D, -1) for w in (shared, routed)]
        return np.concatenate(both, 1)

    gate = chunks(hidden_columns(a["L0_ffn_wg_s"], a["L0_ffn_wg_r"]))
    up_ = chunks(hidden_columns(a["L0_ffn_wu_s"], a["L0_ffn_wu_r"]))
    down = chunks(np.concatenate([a["L0_ffn_wd_s"].reshape(-1, D), a["L0_ffn_wd_r"].reshape(-1, D)]))
    loads = [np.concatenate([w[:, :, 256 * g:256 * (g + 1)].reshape(P, -1) for w in (gate, up_)], 1)
             for g in range(TILES0 // 2)]
    loads += [down[:, s:e].reshape(P, -1) for s, e in DOWN0] + [chunks(values.T).reshape(P, -1)]
    qka = chunks(planes(w_qkva).reshape(12 * P, D).T)
    loads += [qka[:, :, 512 * g:512 * (g + 1)].reshape(P, -1) for g in range(3)] + [chunks(w_y).reshape(P, -1)]
    for w, e, half in EXPERT_LOADS:
        if w:
            loads.append(chunks(a["L1_ffn_W2"][e])[:, 4 * half:4 * half + 4].reshape(P, -1))
        else:
            loads.append(chunks(a["L1_ffn_W1"][e])[:, :, 512 * half:512 * half + 512].reshape(P, -1))
    loads = [np.pad(w, ((0, 0), (0, SLOT - w.shape[1]))) for w in loads]
    arrays = {
        "x": np.concatenate([a["L0_attn_x"], np.zeros((B, SEG, D), np.float32)], 1),
        "w_qkv": chunks(np.concatenate([a[f"L0_attn_W{z}"].T for z in "kqv"], 1)),
        "w_beta": chunks(a["L0_attn_Wbeta"].T), "w_o": chunks(a["L0_attn_Wo"].T),
        "w_router": chunks(a["L0_ffn_router_w"]), "w_in": chunks(a["L1_attn_W_in"].T),
        "w_out": chunks(a["L1_attn_W_out"].T),
        "w_emb": chunks(a["L1_ffn_uzman_embeddings"].T), "b2": a["L1_ffn_b2"],
        "cols": np.concatenate(cols_, 1), "consts": constants(),
        "rows": np.concatenate([a["L0_attn_bo"], a["L1_attn_b_out"], b_values, a["L1_ffn_onbellek_durumu"]]),
        "c_cols": np.stack([a["L0_c"].T.reshape(KC, P, B), a["L1_c"].T.reshape(KC, P, B)]).transpose(2, 0, 1, 3),
        "wmod": np.stack([chunks(a["L0_wmod"]), chunks(a["L1_wmod"])]),
        "w_ring": np.stack(loads), "h0": h0,
    }
    arrays = {k: np.ascontiguousarray(v) for k, v in arrays.items()}
    for k, shape in INPUTS.items():
        assert arrays[k].shape == shape, (k, arrays[k].shape, shape)
    nc = bacc.Bacc("TRN2", target_bir_lowering=False, num_devices=1)
    ins = {k: nc.dram_tensor(f"in_{k}", v.shape, mybir.dt.from_np(v.dtype), kind="ExternalInput").ap()
           for k, v in arrays.items()}
    out = nc.dram_tensor("out_x", (B, L, D), F32, kind="ExternalOutput").ap()
    nc.disable_value_cache = True
    build(nc, ins, out)
    r = run_bass_kernel_spmd(nc, [{f"in_{k}": v for k, v in arrays.items()}], core_ids=[0])
    return r.results[0]["out_x"]
```
